# Optimizing a Trainium2 kernel written in Bass

```python
import numpy as np
import jax
import jax.numpy as jnp

def _softmax(x, axis=-1):
    return jax.nn.softmax(x, axis=axis)

def _gelu(x):
    return jax.nn.gelu(x, approximate=True)

def _silu(x):
    return jax.nn.silu(x)

def _sigmoid(x):
    return jax.nn.sigmoid(x)

def _layernorm(x, axis=-1, eps=1e-05):
    m = jnp.mean(x, axis=axis, keepdims=True)
    v = jnp.var(x, axis=axis, keepdims=True)
    return (x - m) / jnp.sqrt(v + eps)

def _scatter_add(tgt, idx, src, axis=0):
    return tgt.at[idx].add(src)

def _segment_sum(src, seg, n):
    return jax.ops.segment_sum(src, seg, n)
kernel_name = 'mk_seq_preln_d2_jaxref_r8_ccc7cd'

def setup_inputs(seed: int=0):
    np.random.seed(seed)
    _w = jnp.asarray

    def _L0_attn_setup():
        import jax, jax.numpy as jnp
        import numpy as np
        N_HEAD = 32
        HEAD_ID = 0
        MASKED_BIAS = -10000.0
        key = jax.random.key(seed)
        k1, k2, k3 = jax.random.split(key, 3)
        B, S, E = (1, 256, 256)
        hidden_states = jax.random.normal(k1, (B, S, E), dtype=jnp.float32)
        W_attn = jax.random.normal(k2, (E, 3 * E), dtype=jnp.float32) * (1.0 / np.sqrt(E))
        b_attn = jnp.zeros((3 * E,), dtype=jnp.float32)
        W_proj = jax.random.normal(k3, (E, E), dtype=jnp.float32) * (1.0 / np.sqrt(E))
        b_proj = jnp.zeros((E,), dtype=jnp.float32)
        return {'hidden_states': hidden_states, 'W_attn': W_attn, 'b_attn': b_attn, 'W_proj': W_proj, 'b_proj': b_proj}
    _L0_attn_in = _L0_attn_setup()

    def _L0_ffn_setup():
        import jax, jax.numpy as jnp
        import numpy as np
        from jax import lax
        E = 8
        K = 2
        D = 256
        H = 176
        NS = 2
        B, T = (2, 256)
        EPS = 1e-20
        HS = H * NS

        def _silu(v):
            return v * jax.nn.sigmoid(v)
        key = jax.random.key(seed)
        ks = jax.random.split(key, 8)
        s = 0.02
        return {'x': jax.random.normal(ks[0], (B, T, D), jnp.float32), 'router_w': jax.random.normal(ks[1], (E, D), jnp.float32) * 0.006, 'wg': jax.random.normal(ks[2], (E, D, H), jnp.float32) * s, 'wu': jax.random.normal(ks[3], (E, D, H), jnp.float32) * s, 'wd': jax.random.normal(ks[4], (E, H, D), jnp.float32) * s, 'sg': jax.random.normal(ks[5], (D, HS), jnp.float32) * s, 'su': jax.random.normal(ks[6], (D, HS), jnp.float32) * s, 'sd': jax.random.normal(ks[7], (HS, D), jnp.float32) * s}
    _L0_ffn_in = _L0_ffn_setup()

    def _L1_attn_setup():
        import jax, jax.numpy as jnp
        import numpy as np
        B, T, C = (4, 128, 256)
        N = 64
        H = C // N
        D_DECAY, D_AAA, D_MV, D_GATE = (64, 64, 32, 128)

        def rwkv7_op(r, w, k, v, a, b):
            Bq, Tq, Cq = r.shape
            decay = jnp.exp(-jnp.exp(w))

            def resh(t):
                return t.reshape(Bq, Tq, H, N).transpose(1, 0, 2, 3)
            rs, ws, ks, vs, as_, bs = map(resh, (r, decay, k, v, a, b))
            S0 = jnp.zeros((Bq, H, N, N), r.dtype)

            def step(S, inp):
                rt, wt, kt, vt, at, bt = inp
                sa = jnp.einsum('bhij,bhj->bhi', S, at)
                S = S * wt[:, :, None, :] + sa[:, :, :, None] * bt[:, :, None, :] + vt[:, :, :, None] * kt[:, :, None, :]
                yt = jnp.einsum('bhij,bhj->bhi', S, rt)
                return (S, yt)
            _, y = jax.lax.scan(step, S0, (rs, ws, ks, vs, as_, bs))
            return y.transpose(1, 0, 2, 3).reshape(Bq, Tq, Cq)

        def _reference_tuple_inner(x, x_r, x_w, x_k, x_v, x_a, x_g, w0, w1, w2, a0, a1, a2, v0, v1, v2, g1, g2, k_k, k_a, r_k, W_r, W_k, W_v, W_o, gn_scale, gn_offset):
            Bq, Tq, Cq = x.shape
            xx = jnp.pad(x, ((0, 0), (1, 0), (0, 0)))[:, :-1, :] - x
            xr = x + xx * x_r
            xw = x + xx * x_w
            xk = x + xx * x_k
            xv = x + xx * x_v
            xa = x + xx * x_a
            xg = x + xx * x_g
            r = xr @ W_r
            w = -jax.nn.softplus(-(w0 + jnp.tanh(xw @ w1) @ w2)) - 0.5
            k = xk @ W_k
            v = xv @ W_v
            v_first = v
            a = jax.nn.sigmoid(a0 + xa @ a1 @ a2)
            g = jax.nn.sigmoid(xg @ g1) @ g2
            kk = (k * k_k).reshape(Bq, Tq, H, N)
            nrm = jnp.sqrt(jnp.sum(kk * kk, axis=-1, keepdims=True))
            kk = (kk / jnp.maximum(nrm, 1e-12)).reshape(Bq, Tq, Cq)
            k2 = k * (1.0 + (a - 1.0) * k_a)
            o = rwkv7_op(r, w, k2, v, -kk, kk * a)
            o = (o.reshape(Bq, Tq, H, N) * gn_scale + gn_offset).reshape(Bq, Tq, Cq)
            r4 = r.reshape(Bq, Tq, H, N)
            k4 = k2.reshape(Bq, Tq, H, N)
            v4 = v.reshape(Bq, Tq, H, N)
            rwkv = jnp.sum(r4 * k4 * r_k, axis=-1, keepdims=True) * v4
            o = o + rwkv.reshape(Bq, Tq, Cq)
            out = o * g @ W_o
            return (out, v_first)
        key = jax.random.key(seed)
        ks = jax.random.split(key, 32)

        def rn(k, shape, s=0.02):
            return jax.random.normal(k, shape, jnp.float32) * s
        inp = {'x': jax.random.normal(ks[0], (B, T, C), jnp.float32), 'x_r': rn(ks[1], (1, 1, C), 0.5), 'x_w': rn(ks[2], (1, 1, C), 0.5), 'x_k': rn(ks[3], (1, 1, C), 0.5), 'x_v': rn(ks[4], (1, 1, C), 0.5), 'x_a': rn(ks[5], (1, 1, C), 0.5), 'x_g': rn(ks[6], (1, 1, C), 0.5), 'w0': rn(ks[7], (1, 1, C), 0.3), 'w1': rn(ks[8], (C, D_DECAY)), 'w2': rn(ks[9], (D_DECAY, C)), 'a0': rn(ks[10], (1, 1, C), 0.3), 'a1': rn(ks[11], (C, D_AAA)), 'a2': rn(ks[12], (D_AAA, C)), 'v0': rn(ks[13], (1, 1, C), 0.3), 'v1': rn(ks[14], (C, D_MV)), 'v2': rn(ks[15], (D_MV, C)), 'g1': rn(ks[16], (C, D_GATE)), 'g2': rn(ks[17], (D_GATE, C)), 'k_k': rn(ks[18], (1, 1, C), 0.5), 'k_a': rn(ks[19], (1, 1, C), 0.5), 'r_k': rn(ks[20], (H, N), 0.5), 'W_r': rn(ks[21], (C, C)), 'W_k': rn(ks[22], (C, C)), 'W_v': rn(ks[23], (C, C)), 'W_o': rn(ks[24], (C, C)), 'gn_scale': jnp.ones((H, N), jnp.float32) + rn(ks[25], (H, N), 0.1), 'gn_offset': rn(ks[26], (H, N), 0.1)}
        return inp
    _L1_attn_in = _L1_attn_setup()

    def _L1_ffn_setup():
        import jax, jax.numpy as jnp
        import numpy as np
        H = 256
        key = jax.random.key(seed)
        ks = jax.random.split(key, 10)
        s = 1.0 / np.sqrt(H)
        x = jax.random.normal(ks[0], (4, 256, H), dtype=jnp.float32)
        Wg = jax.random.uniform(ks[1], (2, H), jnp.float32, -s, s)
        W0a = jax.random.uniform(ks[2], (2 * H, H), jnp.float32, -s, s)
        b0a = jax.random.uniform(ks[3], (2 * H,), jnp.float32, -s, s)
        W0b = jax.random.uniform(ks[4], (H, 2 * H), jnp.float32, -s, s)
        b0b = jax.random.uniform(ks[5], (H,), jnp.float32, -s, s)
        W1a = jax.random.uniform(ks[6], (2 * H, H), jnp.float32, -s, s)
        b1a = jax.random.uniform(ks[7], (2 * H,), jnp.float32, -s, s)
        W1b = jax.random.uniform(ks[8], (H, 2 * H), jnp.float32, -s, s)
        b1b = jax.random.uniform(ks[9], (H,), jnp.float32, -s, s)
        return {'x': x, 'Wg': Wg, 'W0a': W0a, 'b0a': b0a, 'W0b': W0b, 'b0b': b0b, 'W1a': W1a, 'b1a': b1a, 'W1b': W1b, 'b1b': b1b}
    _L1_ffn_in = _L1_ffn_setup()
    _d = {'L0_attn_hidden_states': _L0_attn_in['hidden_states'], 'L0_attn_W_attn': _L0_attn_in['W_attn'], 'L0_attn_b_attn': _L0_attn_in['b_attn'], 'L0_attn_W_proj': _L0_attn_in['W_proj'], 'L0_attn_b_proj': _L0_attn_in['b_proj'], 'L0_ffn_router_w': _L0_ffn_in['router_w'], 'L0_ffn_wg': _L0_ffn_in['wg'], 'L0_ffn_wu': _L0_ffn_in['wu'], 'L0_ffn_wd': _L0_ffn_in['wd'], 'L0_ffn_sg': _L0_ffn_in['sg'], 'L0_ffn_su': _L0_ffn_in['su'], 'L0_ffn_sd': _L0_ffn_in['sd'], 'L1_attn_x_r': _L1_attn_in['x_r'], 'L1_attn_x_w': _L1_attn_in['x_w'], 'L1_attn_x_k': _L1_attn_in['x_k'], 'L1_attn_x_v': _L1_attn_in['x_v'], 'L1_attn_x_a': _L1_attn_in['x_a'], 'L1_attn_x_g': _L1_attn_in['x_g'], 'L1_attn_w0': _L1_attn_in['w0'], 'L1_attn_w1': _L1_attn_in['w1'], 'L1_attn_w2': _L1_attn_in['w2'], 'L1_attn_a0': _L1_attn_in['a0'], 'L1_attn_a1': _L1_attn_in['a1'], 'L1_attn_a2': _L1_attn_in['a2'], 'L1_attn_v0': _L1_attn_in['v0'], 'L1_attn_v1': _L1_attn_in['v1'], 'L1_attn_v2': _L1_attn_in['v2'], 'L1_attn_g1': _L1_attn_in['g1'], 'L1_attn_g2': _L1_attn_in['g2'], 'L1_attn_k_k': _L1_attn_in['k_k'], 'L1_attn_k_a': _L1_attn_in['k_a'], 'L1_attn_r_k': _L1_attn_in['r_k'], 'L1_attn_W_r': _L1_attn_in['W_r'], 'L1_attn_W_k': _L1_attn_in['W_k'], 'L1_attn_W_v': _L1_attn_in['W_v'], 'L1_attn_W_o': _L1_attn_in['W_o'], 'L1_attn_gn_scale': _L1_attn_in['gn_scale'], 'L1_attn_gn_offset': _L1_attn_in['gn_offset'], 'L1_ffn_Wg': _L1_ffn_in['Wg'], 'L1_ffn_W0a': _L1_ffn_in['W0a'], 'L1_ffn_b0a': _L1_ffn_in['b0a'], 'L1_ffn_W0b': _L1_ffn_in['W0b'], 'L1_ffn_b0b': _L1_ffn_in['b0b'], 'L1_ffn_W1a': _L1_ffn_in['W1a'], 'L1_ffn_b1a': _L1_ffn_in['b1a'], 'L1_ffn_W1b': _L1_ffn_in['W1b'], 'L1_ffn_b1b': _L1_ffn_in['b1b']}
    _x0 = _d['L0_attn_hidden_states']
    _d['L0_attn_hidden_states'] = jax.random.normal(jax.random.fold_in(jax.random.key(seed), 1), (2, 1024, 256), dtype=_x0.dtype)
    del _x0
    return _d

def reference(L0_attn_hidden_states, L0_attn_W_attn, L0_attn_b_attn, L0_attn_W_proj, L0_attn_b_proj, L0_ffn_router_w, L0_ffn_wg, L0_ffn_wu, L0_ffn_wd, L0_ffn_sg, L0_ffn_su, L0_ffn_sd, L1_attn_x_r, L1_attn_x_w, L1_attn_x_k, L1_attn_x_v, L1_attn_x_a, L1_attn_x_g, L1_attn_w0, L1_attn_w1, L1_attn_w2, L1_attn_a0, L1_attn_a1, L1_attn_a2, L1_attn_v0, L1_attn_v1, L1_attn_v2, L1_attn_g1, L1_attn_g2, L1_attn_k_k, L1_attn_k_a, L1_attn_r_k, L1_attn_W_r, L1_attn_W_k, L1_attn_W_v, L1_attn_W_o, L1_attn_gn_scale, L1_attn_gn_offset, L1_ffn_Wg, L1_ffn_W0a, L1_ffn_b0a, L1_ffn_W0b, L1_ffn_b0b, L1_ffn_W1a, L1_ffn_b1a, L1_ffn_W1b, L1_ffn_b1b):

    def _L0_attn_ref(hidden_states, W_attn, b_attn, W_proj, b_proj):
        import jax, jax.numpy as jnp
        import numpy as np
        N_HEAD = 32
        HEAD_ID = 0
        MASKED_BIAS = -10000.0
        B, S, E = hidden_states.shape
        H = N_HEAD
        D = E // H
        m = 2.0 ** (-(8.0 / H) * (HEAD_ID + 1))
        qkv = hidden_states @ W_attn + b_attn
        q, k, v = jnp.split(qkv, 3, axis=-1)
        q = q.reshape(B, S, H, D).transpose(0, 2, 1, 3)
        k = k.reshape(B, S, H, D).transpose(0, 2, 1, 3)
        v = v.reshape(B, S, H, D).transpose(0, 2, 1, 3)
        scores = jnp.einsum('bhqd,bhkd->bhqk', q, k) / jnp.sqrt(jnp.float32(D))
        rows = jnp.arange(S)[:, None]
        cols = jnp.arange(S)[None, :]
        causal = cols <= rows
        scores = jnp.where(causal, scores, jnp.float32(MASKED_BIAS))
        alibi = jnp.where(causal, (cols - rows).astype(scores.dtype), 0.0)
        scores = scores + alibi * m
        probs = jax.nn.softmax(scores, axis=-1)
        attn = jnp.einsum('bhqk,bhkd->bhqd', probs, v)
        attn = attn.transpose(0, 2, 1, 3).reshape(B, S, E)
        out = attn @ W_proj + b_proj
        return out

    def _L0_ffn_ref(x, router_w, wg, wu, wd, sg, su, sd):
        import jax, jax.numpy as jnp
        import numpy as np
        from jax import lax
        E = 8
        K = 2
        D = 256
        H = 176
        NS = 2
        B, T = (2, 256)
        EPS = 1e-20
        HS = H * NS

        def _silu(v):
            return v * jax.nn.sigmoid(v)
        b, t, d = x.shape
        xf = x.reshape(b * t, d)
        n = xf.shape[0]
        gates = jax.nn.softmax(xf @ router_w.T, axis=-1)
        topv, topi = lax.top_k(gates, K)
        masked = jnp.zeros_like(gates).at[jnp.arange(n)[:, None], topi].set(topv)
        masked = masked / (masked.sum(axis=-1, keepdims=True) + EPS)

        def step(acc, p):
            wg_e, wu_e, wd_e, g_e = p
            y = _silu(xf @ wg_e) * (xf @ wu_e) @ wd_e
            return (acc + y * g_e[:, None], None)
        routed, _ = lax.scan(step, jnp.zeros_like(xf), (wg, wu, wd, masked.T))
        shared = _silu(xf @ sg) * (xf @ su) @ sd
        return (routed + shared).reshape(b, t, d)

    def _L1_attn_ref(x, x_r, x_w, x_k, x_v, x_a, x_g, w0, w1, w2, a0, a1, a2, v0, v1, v2, g1, g2, k_k, k_a, r_k, W_r, W_k, W_v, W_o, gn_scale, gn_offset):
        import jax, jax.numpy as jnp
        import numpy as np
        B, T, C = (4, 128, 256)
        N = 64
        H = C // N
        D_DECAY, D_AAA, D_MV, D_GATE = (64, 64, 32, 128)

        def rwkv7_op(r, w, k, v, a, b):
            Bq, Tq, Cq = r.shape
            decay = jnp.exp(-jnp.exp(w))

            def resh(t):
                return t.reshape(Bq, Tq, H, N).transpose(1, 0, 2, 3)
            rs, ws, ks, vs, as_, bs = map(resh, (r, decay, k, v, a, b))
            S0 = jnp.zeros((Bq, H, N, N), r.dtype)

            def step(S, inp):
                rt, wt, kt, vt, at, bt = inp
                sa = jnp.einsum('bhij,bhj->bhi', S, at)
                S = S * wt[:, :, None, :] + sa[:, :, :, None] * bt[:, :, None, :] + vt[:, :, :, None] * kt[:, :, None, :]
                yt = jnp.einsum('bhij,bhj->bhi', S, rt)
                return (S, yt)
            _, y = jax.lax.scan(step, S0, (rs, ws, ks, vs, as_, bs))
            return y.transpose(1, 0, 2, 3).reshape(Bq, Tq, Cq)

        def _reference_tuple_inner(x, x_r, x_w, x_k, x_v, x_a, x_g, w0, w1, w2, a0, a1, a2, v0, v1, v2, g1, g2, k_k, k_a, r_k, W_r, W_k, W_v, W_o, gn_scale, gn_offset):
            Bq, Tq, Cq = x.shape
            xx = jnp.pad(x, ((0, 0), (1, 0), (0, 0)))[:, :-1, :] - x
            xr = x + xx * x_r
            xw = x + xx * x_w
            xk = x + xx * x_k
            xv = x + xx * x_v
            xa = x + xx * x_a
            xg = x + xx * x_g
            r = xr @ W_r
            w = -jax.nn.softplus(-(w0 + jnp.tanh(xw @ w1) @ w2)) - 0.5
            k = xk @ W_k
            v = xv @ W_v
            v_first = v
            a = jax.nn.sigmoid(a0 + xa @ a1 @ a2)
            g = jax.nn.sigmoid(xg @ g1) @ g2
            kk = (k * k_k).reshape(Bq, Tq, H, N)
            nrm = jnp.sqrt(jnp.sum(kk * kk, axis=-1, keepdims=True))
            kk = (kk / jnp.maximum(nrm, 1e-12)).reshape(Bq, Tq, Cq)
            k2 = k * (1.0 + (a - 1.0) * k_a)
            o = rwkv7_op(r, w, k2, v, -kk, kk * a)
            o = (o.reshape(Bq, Tq, H, N) * gn_scale + gn_offset).reshape(Bq, Tq, Cq)
            r4 = r.reshape(Bq, Tq, H, N)
            k4 = k2.reshape(Bq, Tq, H, N)
            v4 = v.reshape(Bq, Tq, H, N)
            rwkv = jnp.sum(r4 * k4 * r_k, axis=-1, keepdims=True) * v4
            o = o + rwkv.reshape(Bq, Tq, Cq)
            out = o * g @ W_o
            return (out, v_first)
        return _reference_tuple_inner(x, x_r, x_w, x_k, x_v, x_a, x_g, w0, w1, w2, a0, a1, a2, v0, v1, v2, g1, g2, k_k, k_a, r_k, W_r, W_k, W_v, W_o, gn_scale, gn_offset)[0]

    def _L1_ffn_ref(x, Wg, W0a, b0a, W0b, b0b, W1a, b1a, W1b, b1b):
        import jax, jax.numpy as jnp
        import numpy as np
        H = 256
        scores = jax.nn.softmax(jnp.einsum('bsh,eh->bse', x, Wg), axis=-1)
        top_expert = jnp.argmax(scores, axis=-1)
        h0 = jax.nn.gelu(jnp.einsum('bsh,fh->bsf', x, W0a) + b0a, approximate=False)
        out0 = jnp.einsum('bsf,hf->bsh', h0, W0b) + b0b
        h1 = jax.nn.relu(jnp.einsum('bsh,fh->bsf', x, W1a) + b1a)
        out1 = jnp.einsum('bsf,hf->bsh', h1, W1b) + b1b
        mask0 = (top_expert == 0).astype(x.dtype)[..., None]
        return out0 * mask0 + out1 * (1.0 - mask0)
    x = L0_attn_hidden_states
    x = x + _L0_attn_ref(_layernorm(x, axis=-1), L0_attn_W_attn, L0_attn_b_attn, L0_attn_W_proj, L0_attn_b_proj)
    x = x + _L0_ffn_ref(_layernorm(x, axis=-1), L0_ffn_router_w, L0_ffn_wg, L0_ffn_wu, L0_ffn_wd, L0_ffn_sg, L0_ffn_su, L0_ffn_sd)
    x = x + _L1_attn_ref(_layernorm(x, axis=-1), L1_attn_x_r, L1_attn_x_w, L1_attn_x_k, L1_attn_x_v, L1_attn_x_a, L1_attn_x_g, L1_attn_w0, L1_attn_w1, L1_attn_w2, L1_attn_a0, L1_attn_a1, L1_attn_a2, L1_attn_v0, L1_attn_v1, L1_attn_v2, L1_attn_g1, L1_attn_g2, L1_attn_k_k, L1_attn_k_a, L1_attn_r_k, L1_attn_W_r, L1_attn_W_k, L1_attn_W_v, L1_attn_W_o, L1_attn_gn_scale, L1_attn_gn_offset)
    x = x + _L1_ffn_ref(_layernorm(x, axis=-1), L1_ffn_Wg, L1_ffn_W0a, L1_ffn_b0a, L1_ffn_W0b, L1_ffn_b0b, L1_ffn_W1a, L1_ffn_b1a, L1_ffn_W1b, L1_ffn_b1b)
    return x

_drawn_inputs = setup_inputs


def setup_inputs(seed=0):
    import zlib

    import numpy as np

    out = dict(_drawn_inputs(seed))
    spreads = {'L0_attn_b_attn': (0.0, 0.1), 'L0_attn_b_proj': (0.0, 0.1)}
    factors = {'L0_ffn_router_w': 3.98,
     'L0_ffn_wg': 3.182,
     'L0_ffn_wu': 3.313,
     'L0_ffn_wd': 3.351,
     'L1_attn_x_w': 8.0,
     'L1_attn_x_a': 8.0,
     'L1_attn_x_g': 8.0,
     'L1_attn_w0': 8.0,
     'L1_attn_w1': 8.0,
     'L1_attn_w2': 8.0,
     'L1_attn_a0': 8.0,
     'L1_attn_a1': 8.0,
     'L1_attn_a2': 8.0,
     'L1_attn_g1': 4.976,
     'L1_attn_k_k': 8.0,
     'L1_attn_k_a': 3.486,
     'L1_attn_r_k': 3.384,
     'L1_attn_gn_scale': 5.265,
     'L1_attn_gn_offset': 8.0,
     'L1_ffn_b0a': 5.643,
     'L1_ffn_b0b': 2.69,
     'L1_ffn_b1a': 4.919,
     'L1_ffn_b1b': 2.729}
    for name, (base, spread) in spreads.items():
        noise = np.random.default_rng([zlib.crc32(name.encode()), seed]).standard_normal(out[name].shape)
        drawn = base * np.exp(spread * noise) if base else spread * noise
        out[name] = jnp.asarray(drawn.astype(out[name].dtype))
    for name, factor in factors.items():
        out[name] = (out[name] * factor).astype(out[name].dtype)
    return out
```

```python
from contextlib import ExitStack

import numpy as np

import concourse.bass as bass
from concourse import mybir

ALU = mybir.AluOpType
ACT = mybir.ActivationFunctionType
AX = mybir.AxisListType
F32 = mybir.dt.float32
BF16 = mybir.dt.bfloat16
U32 = mybir.dt.uint32
ds = bass.ds

P = 128
B, S, E = 2, 1024, 256
TILES = B * S // P
TPB = S // P
EH = E // P
HEADS, HD = 32, 8
GROUP = 4
UNITS = B * HEADS // GROUP
GPB = HEADS // GROUP
SLOPE = 2.0 ** (-8.0 / HEADS)
NEG = -1e30
EPS = 1e-5
QC = 512
NQC = S // QC


class Chain:

    def __init__(self, eng, sem):
        self.eng, self.sem, self.done, self.round = eng, sem, 0, None

    def loop(self, i, each):
        self.round, self.each, self.start = i, each, self.done

    def end(self, rounds):
        assert self.done - self.start == self.each, self.done - self.start
        self.round, self.done = None, self.start + self.each * rounds

    def mark(self, ins):
        ins.then_inc(self.sem, 1)
        self.done += 1
        return self.done

    def wait(self, mark=None):
        mark = self.done if mark is None else mark
        self.eng.wait_ge(self.sem, mark if self.round is None else self.round * self.each + mark)

    def link(self, ins):
        self.mark(ins)
        self.wait()


def layernorm_stats(nc, tag, x, mean, rstd, eps):
    with ExitStack() as ctx:
        sb = lambda n, s, d=F32: ctx.enter_context(nc.sbuf_tensor(tag + n, s, d))
        sem = lambda n: ctx.enter_context(nc.semaphore(tag + n))
        stats = sb("stats", [P, TILES, 6])
        half, diff, var, std = (sb(n, [P, TILES]) for n in ("half", "diff", "var", "std"))
        chain_s, var_ready, std_ready = sem("chain"), sem("var_ready"), sem("std_ready")
        with nc.Block() as block:
            @block.vector
            def _(dve):
                c = Chain(dve, chain_s)
                with dve.Fori(0, TILES) as i:
                    c.loop(i, 1)
                    c.mark(dve.bn_stats(stats[:, ds(i, 1), :], x[:, ds(i, 1), :]))
                c.end(TILES)
                c.wait()
                c.link(dve.tensor_tensor(half[:, :], stats[:, :, 1], stats[:, :, 4], ALU.add))
                c.link(dve.tensor_tensor(diff[:, :], stats[:, :, 1], stats[:, :, 4], ALU.subtract))
                c.link(dve.tensor_tensor(var[:, :], stats[:, :, 2], stats[:, :, 5], ALU.add))
                c.link(dve.tensor_scalar(mean[:, :], half[:, :], 0.5, None, ALU.mult))
                c.link(dve.scalar_tensor_tensor(diff[:, :], diff[:, :], 0.25, diff[:, :], ALU.mult, ALU.mult))
                dve.scalar_tensor_tensor(var[:, :], var[:, :], 1.0 / E, diff[:, :], ALU.mult,
                                         ALU.add).then_inc(var_ready, 1)
                dve.wait_ge(std_ready, 1)
                dve.reciprocal(rstd[:, :], std[:, :])

            @block.scalar
            def _(act):
                act.wait_ge(var_ready, 1)
                act.activation(std[:, :], var[:, :], ACT.Sqrt, bias=eps[:, 0:1]).then_inc(std_ready, 1)


def qkv_phase(nc, x, mean, rstd, ident, w, bias, qparts, kparts, v):
    with ExitStack() as ctx:
        sb = lambda n, s, d=F32: ctx.enter_context(nc.sbuf_tensor("qkv_" + n, s, d))
        ps = lambda n, s, d=F32: ctx.enter_context(nc.psum_tensor("qkv_" + n, s, d))
        sem = lambda n: ctx.enter_context(nc.semaphore("qkv_" + n))
        xn = [sb(f"xn{b}", [P, E]) for b in range(B)]
        xt = [sb(f"xt{b}", [P, EH, P]) for b in range(B)]
        qk = [sb(f"qk{b}", [P, 2 * E]) for b in range(B)]
        rest = [sb(f"rest{b}", [P, 2 * E]) for b in range(B)]
        pt = [ps(f"pt{b}", [P, 512]) for b in range(B)]
        pq = [ps(f"pq{b}", [P, 1024]) for b in range(B)]
        names = "xn_ready xt_psum xt_ready proj_ready qk_ready high_ready rest_ready mid_ready proj_used"
        s = {n: sem(n) for n in names.split()}
        scale = HD ** -0.5

        def parts_at(t, buf, part, b):
            return buf[:, part, b * GPB:(b + 1) * GPB, ds(t, 1), :].rearrange("p g t c -> p (g t) c")

        with nc.Block() as block:
            @block.vector
            def _(dve):
                def normalise(t, b):
                    dve.tensor_scalar(xn[b][:, :], x[:, ds(t + b * TPB, 1), :].rearrange("p a e -> p (a e)"),
                                      mean[:, ds(t + b * TPB, 1)], rstd[:, ds(t + b * TPB, 1)],
                                      ALU.subtract, ALU.mult).then_inc(s["xn_ready"], 1)

                def low(t, b):
                    dve.wait_ge(s["mid_ready"], t * B + b + 1)
                    for n, buf in enumerate((qparts, kparts)):
                        dve.tensor_tensor(parts_at(t, buf, 2, b),
                                          rest[b][:, n * E:(n + 1) * E].rearrange("p (g c) -> p g c", g=GPB),
                                          parts_at(t, buf, 1, b), ALU.subtract)

                with dve.Fori(0, TPB) as t:
                    for b in range(B):
                        normalise(t, b)
                    for b in range(B):
                        dve.wait_ge(s["proj_ready"], t * B + b + 1)
                        dve.scalar_tensor_tensor(qk[b][:, 0:E], pq[b][:, 0:E], scale, bias[:, 0:E],
                                                 ALU.mult, ALU.add).then_inc(s["qk_ready"], 1)
                        dve.tensor_tensor(qk[b][:, E:2 * E], pq[b][:, E:2 * E], bias[:, E:2 * E],
                                          ALU.add).then_inc(s["qk_ready"], 1)
                        dve.tensor_tensor(parts_at(t, v, 0, b),
                                          pq[b][:, 2 * E:3 * E].rearrange("p (g c) -> p g c", g=GPB),
                                          bias[:, 2 * E:3 * E].rearrange("p (g c) -> p g c", g=GPB),
                                          ALU.add).then_inc(s["proj_used"], 1)
                    for b in range(B):
                        dve.wait_ge(s["high_ready"], (t * B + b) * 2 + 2)
                        for n, buf in enumerate((qparts, kparts)):
                            dve.tensor_tensor(rest[b][:, n * E:(n + 1) * E].rearrange("p (g c) -> p g c", g=GPB),
                                              qk[b][:, n * E:(n + 1) * E].rearrange("p (g c) -> p g c", g=GPB),
                                              parts_at(t, buf, 0, b), ALU.subtract).then_inc(s["rest_ready"], 1)
                    for b in range(B):
                        low(t, b)

            @block.scalar
            def _(act):
                def high(t, b):
                    act.wait_ge(s["qk_ready"], (t * B + b) * 2 + 2)
                    for n, buf in enumerate((qparts, kparts)):
                        act.copy(parts_at(t, buf, 0, b),
                                 qk[b][:, n * E:(n + 1) * E].rearrange("p (g c) -> p g c", g=GPB)
                                 ).then_inc(s["high_ready"], 1)

                with act.Fori(0, TPB) as t:
                    for b in range(B):
                        act.wait_ge(s["xt_psum"], t * B + b + 1)
                        act.copy(xt[b][:, :, :], pt[b][:, 0:E].rearrange("p (h c) -> p h c", h=EH)
                                 ).then_inc(s["xt_ready"], 1)
                    for b in range(B):
                        high(t, b)

            @block.gpsimd
            def _(pool):
                with pool.Fori(0, TPB) as t:
                    for b in range(B):
                        pool.wait_ge(s["rest_ready"], (t * B + b) * 2 + 2)
                        for n, buf in enumerate((qparts, kparts)):
                            last = pool.tensor_copy(parts_at(t, buf, 1, b),
                                                    rest[b][:, n * E:(n + 1) * E].rearrange("p (g c) -> p g c", g=GPB))
                        last.then_inc(s["mid_ready"], 1)

            @block.tensor
            def _(pe):
                with pe.Fori(0, TPB) as t:
                    for b in range(B):
                        pe.wait_ge(s["xn_ready"], t * B + b + 1)
                        for h in range(EH):
                            mm = pe.transpose(pt[b][:, h * P:(h + 1) * P], xn[b][:, h * P:(h + 1) * P], ident[:, :])
                        mm.then_inc(s["xt_psum"], 1)
                    for b in range(B):
                        pe.wait_ge(s["xt_ready"], t * B + b + 1)
                        for lo, hi in ((0, 512), (512, 768)):
                            for h in range(EH):
                                mm = pe.matmul(pq[b][:, lo:hi], xt[b][:, h, :], w[:, h, lo:hi],
                                               start=h == 0, stop=h == EH - 1)
                        mm.then_inc(s["proj_ready"], 1)


ROWS = 64
PRODUCTS = 6
SHIFT_ROW = PRODUCTS * HD
ALIBI_ROW = SHIFT_ROW + 3
CROWS = 5
KEY_ORDER = [(0, 1, 3, 2), (0, 7, 1, 6, 2, 5, 3, 4)]
STEPS = [(c, kt) for c in range(NQC) for kt in KEY_ORDER[c]]
LAST0 = len(KEY_ORDER[0]) - 1
FILLS = [([(3, 0, 4)], 40, 1, 4), ([(4, 0, 4)], 16, 1, 4), ([(5, 0, 4)], 48, 1, 4), ([(6, 0, 4)], 27, 1, 4),
         ([(7, 0, 4)], 56, 1, 4), ([(7, 4, 4)], 60, 1, 4), ([(0, 0, 1), (2, 0, 3)], 7, 1, 4),
         ([(4, 4, 1), (6, 4, 3)], 23, 1, 4), ([(1, 0, 2), (5, 4, 2)], 32, 20, 2)]
SLOTS = 72
PAIR_FILLS = 2 * len(FILLS)
FILLS_PER_STEP = [3, 4, 2, 3, 4, 2, 5, 3, 5, 5, 0, 0]


def slot_events(kind):
    extra = {0: ["turn 0", "prev", "turn 1"], 1: ["turn 2"], 2: ["turn 3"], 3: ["out_prev"],
             6: ["out_now"], 8: ["shift 0"]}
    ev, fill = [], 0

    def fills(count):
        nonlocal fill
        for _ in range(count):
            ev.append(("fill", fill // PAIR_FILLS, fill % PAIR_FILLS))
            fill += 1
            if fill % PAIR_FILLS == 0:
                ev.append(("max", fill // PAIR_FILLS - 1))

    for k in range(len(STEPS)):
        step = []
        if "s" in kind:
            step.append(("scores", k, 0))
        for name in extra.get(k, []):
            what, _, arg = name.partition(" ")
            if what in ("turn", "shift") and "m" in kind:
                step.append((what, int(arg)))
            if what == "prev" and "p" in kind:
                step += [("pv", len(STEPS) - 1, 1), ("take", 1, 1)]
            if what == "out_prev" and "p" in kind:
                step.append(("out", 1, 1))
            if what == "out_now" and "s" in kind:
                step.append(("out", 0, 0))
        if "s" in kind:
            step.append(("scores", k, 1))
            if k >= 1:
                step.append(("pv", k - 1, 0))
            if k == LAST0 + 1:
                step.append(("take", 0, 0))
        left = FILLS_PER_STEP[k] if "m" in kind else 0
        after = [n for n, e in enumerate(step) if e[0] in ("scores", "turn", "pv", "out")
                 and not any(x == ("turn", 1) for x in step[n + 1:])]
        for n, e in enumerate(step):
            ev.append(e)
            if n in after:
                now = -(-left // (len(after) - after.index(n)))
                fills(now)
                left -= now
        fills(left)
    if "m" in kind:
        ev.append(("shift", 1))
    return ev


SHARED = ("turn", "shift", "out")


def shared_uses(kind):
    return sum(e[0] in SHARED for e in slot_events(kind))


def shared_place(events, n, u):
    before = sum(e[0] in SHARED for e in events[:n])
    first, second, full = shared_uses("m"), shared_uses("sm"), shared_uses("psm")
    if isinstance(u, int) and u <= 0:
        return before + (first if u == 0 else 0)
    if isinstance(u, int) and u == UNITS:
        return first + second + (UNITS - 2) * full + shared_uses("ps") + before
    return (u - 1) * full + (first + second + before)


def attention_phase(nc, ident, ident16, causal16, anticausal16, abias, shift0, key_alibi, qparts, kparts, v, attn):
    with ExitStack() as ctx:
        sb = lambda n, s, d=F32: ctx.enter_context(nc.sbuf_tensor("at_" + n, s, d))
        ps = lambda n, s, d=F32: ctx.enter_context(nc.psum_tensor("at_" + n, s, d))
        sem = lambda n: ctx.enter_context(nc.semaphore("at_" + n))
        qstack, kstack = (sb(n, [P, TPB, GROUP, ROWS], BF16) for n in ("qstack", "kstack"))
        qt = [sb(f"qt{i}", [P, 2, S], BF16) for i in range(2)]
        kt_ = [sb(f"kt{i}", [P, 2, S], BF16) for i in range(2)]
        vs = [sb(f"vs{i}", [P, TPB, GROUP, 32]) for i in range(2)]
        probs = [sb(f"probs{i}", [P, GROUP, QC]) for i in range(2)]
        block_max = sb("block_max", [P, GROUP, SLOTS])
        row_max = sb("row_max", [P, GROUP, TPB])
        shift = sb("shift", [P, 2, 2, TPB])
        rest = sb("rest", [P, 2, 2, TPB])
        shift16 = sb("shift16", [P, 2, 2, CROWS, TPB], BF16)
        rows16 = [sb(f"rows16{i}", [2 * CROWS * TPB, P], BF16) for i in range(2)]
        ot = sb("ot", [P, QC])
        rden = sb("rden", [P, QC // P, GROUP])
        p_score = [ps(f"p_score{i}", [P, 2, QC]) for i in range(2)]
        p_fill = [ps(f"p_fill{i}", [P, QC]) for i in range(2)]
        p_out = ps("p_out", [P, QC])
        p_shared = ps("p_shared", [P, QC])
        shared16 = p_shared[:, :].bitcast(BF16)
        s = {n: sem(n) for n in ("preset stack_ready v_ready shared_full shared_used fill_ready fill_used "
                                 "max_ready shift_ready rows0 rows1 scores_ready exp_done pv_done "
                                 "out_taken pool_chain dve_chain").split()}
        rows_loaded = [s["rows0"], s["rows1"]]
        NS = len(STEPS)
        DIAG = [k for k, (c, kt) in enumerate(STEPS) if kt * P >= c * QC]

        def left(k):
            c, kt = STEPS[k]
            return max(0, kt * P - c * QC)

        def slots(slot):
            def program(eng):
                slot(eng, -1, 1, "m")
                slot(eng, 0, 0, "sm")
                with eng.Fori(0, UNITS // 2 - 2) as r:
                    slot(eng, r * 2 + 1, 1, "psm")
                    slot(eng, r * 2 + 2, 0, "psm")
                slot(eng, UNITS - 3, 1, "psm")
                slot(eng, UNITS - 2, 0, "psm")
                slot(eng, UNITS - 1, 1, "ps")
                slot(eng, UNITS, 0, "p")
            return program

        def early(u, k=0):
            return isinstance(u, int) and u == 0 and k < 2

        def tensor_slot(pe, u, par, kind):
            ev, nxt = slot_events(kind), 1 - par
            for n, e in enumerate(ev):
                if e[0] in SHARED:
                    before = shared_place(ev, n, u)
                    if not (isinstance(before, int) and before == 0):
                        pe.wait_ge(s["shared_used"], before)
                if e[0] == "turn":
                    if e[1] == 0:
                        pe.wait_ge(s["stack_ready"], u + 2)
                    stack, pair = (qstack, kstack)[e[1] % 2], e[1] // 2
                    for t in range(TPB):
                        mm = pe.transpose(shared16[:, t * P:(t + 1) * P],
                                          stack[:, t, 2 * pair:2 * pair + 2, :].rearrange("p h r -> p (h r)"),
                                          ident16[:, :])
                    mm.then_inc(s["shared_full"], 1)
                elif e[0] == "fill":
                    pair, f = e[1:]
                    at, h = f // 2, f % 2
                    if pair * PAIR_FILLS + f >= 2:
                        pe.wait_ge(s["fill_used"], (u + 1) * 2 * PAIR_FILLS + pair * PAIR_FILLS + f - 1)
                    if f == 0:
                        pe.wait_ge(s["shared_used"], shared_place(ev, ev.index(("turn", 2 * pair + 1)), u) + 1)
                    bank, col = p_fill[f % 2], 0
                    for t, b0, nb in FILLS[at][0]:
                        diag = b0 + nb == t + 1
                        mm = pe.matmul(bank[:, col:col + nb * P], qt[nxt][h * ROWS:(h + 1) * ROWS, pair, t * P:(t + 1) * P],
                                       kt_[nxt][h * ROWS:(h + 1) * ROWS, pair, b0 * P:(b0 + nb) * P],
                                       start=col == 0, stop=not diag, skip_group_check=True)
                        col += nb * P
                        if diag:
                            mm = pe.matmul(bank[:, col - P:col], ident16[:, :], causal16[:, :],
                                           start=False, stop=True, skip_group_check=True)
                    mm.then_inc(s["fill_ready"], 1)
                elif e[0] == "shift":
                    pe.wait_ge(s["shift_ready"], (u + 1) * 2 + e[1] + 1)
                    pe.transpose(shared16[0:2 * CROWS * TPB, 0:P],
                                 shift16[:, e[1], :, :, :].rearrange("p h r t -> p (h r t)"),
                                 ident16[:, :]).then_inc(s["shared_full"], 1)
                elif e[0] == "scores":
                    k, pair = e[1:]
                    c, kt = STEPS[k]
                    if k == 0:
                        pe.wait_ge(rows_loaded[pair], (u + 1) * 32)
                    if k or not early(u):
                        pe.wait_ge(s["exp_done"], u * 2 * NS + 2 * (k - 1) + pair + 1)
                    for h in range(2):
                        mm = pe.matmul(p_score[pair][:, h, left(k):QC],
                                       kt_[par][h * ROWS:(h + 1) * ROWS, pair, kt * P:(kt + 1) * P],
                                       qt[par][h * ROWS:(h + 1) * ROWS, pair, c * QC + left(k):(c + 1) * QC],
                                       start=True, stop=k not in DIAG, skip_group_check=True)
                        if k in DIAG:
                            mm = pe.matmul(p_score[pair][:, h, left(k):left(k) + P], ident16[:, :], anticausal16[:, :],
                                           start=False, stop=True, skip_group_check=True)
                    mm.then_inc(s["scores_ready"], 1)
                elif e[0] == "pv":
                    k, unit = e[1], u - e[2]
                    c, kt = STEPS[k]
                    if k == 0:
                        pe.wait_ge(s["v_ready"], u + 1)
                    if kt == KEY_ORDER[c][0] and (c or not early(u)):
                        pe.wait_ge(s["out_taken"], unit * NQC + c)
                    pe.wait_ge(s["exp_done"], unit * 2 * NS + 2 * k + 2)
                    for h in range(GROUP):
                        mm = pe.matmul(p_out[32 * h:32 * h + 32, left(k):QC], vs[nxt if e[2] else par][:, kt, h, :],
                                       probs[k % 2][:, h, left(k):QC], start=kt == KEY_ORDER[c][0],
                                       stop=kt == KEY_ORDER[c][-1], skip_group_check=True)
                    mm.then_inc(s["pv_done"], 1)
                elif e[0] == "out":
                    pe.wait_ge(s["out_taken"], (u - e[2]) * NQC + e[1] + 1)
                    for t in range(QC // P):
                        mm = pe.transpose(p_shared[:, t * P:(t + 1) * P], ot[:, t * P:(t + 1) * P], ident[:, :])
                    mm.then_inc(s["shared_full"], 1)

        def scalar_slot(act, u, par, kind):
            ev, nxt = slot_events(kind), 1 - par
            for n, e in enumerate(ev):
                if e[0] == "turn" and e[1] % 2 == 0:
                    act.wait_ge(s["shared_full"], shared_place(ev, n, u) + 1)
                    act.copy(qt[nxt][:, e[1] // 2, :], shared16[:, 0:S]).then_inc(s["shared_used"], 1)
                elif e[0] == "shift":
                    act.wait_ge(s["shared_full"], shared_place(ev, n, u) + 1)
                    act.copy(rows16[e[1]][:, :], shared16[0:2 * CROWS * TPB, 0:P]).then_inc(s["shared_used"], 1)
                elif e[0] == "scores":
                    k, pair = e[1:]
                    c, kt = STEPS[k]
                    act.wait_ge(s["scores_ready"], u * 2 * NS + 2 * k + pair + 1)
                    if not early(u, k):
                        act.wait_ge(s["pv_done"], u * NS + (k - 1))
                    act.activation(probs[k % 2][:, 2 * pair:2 * pair + 2, left(k):QC],
                                   p_score[pair][:, :, left(k):QC], ACT.Exp,
                                   bias=abias[:, c * TPB + kt:c * TPB + kt + 1]).then_inc(s["exp_done"], 1)
                elif e[0] == "take":
                    act.wait_ge(s["pv_done"], (u - e[2]) * NS + (NS if e[1] else LAST0 + 1))
                    act.copy(ot[:, :], p_out[:, :]).then_inc(s["out_taken"], 1)

        def vector_slot(dve, u, par, kind):
            ev, nxt = slot_events(kind), 1 - par
            for n, e in enumerate(ev):
                if e[0] == "turn" and e[1] % 2:
                    dve.wait_ge(s["shared_full"], shared_place(ev, n, u) + 1)
                    dve.tensor_copy(kt_[nxt][:, e[1] // 2, :], shared16[:, 0:S]).then_inc(s["shared_used"], 1)
                elif e[0] == "fill":
                    pair, f = e[1:]
                    (_, first, step, count), h = FILLS[f // 2], 2 * pair + f % 2
                    dve.wait_ge(s["fill_ready"], (u + 1) * 2 * PAIR_FILLS + pair * PAIR_FILLS + f + 1)
                    if step == 1:
                        dst, src = block_max[:, h, first:first + count], p_fill[f % 2][:, :].rearrange("p (a c) -> p a c", c=P)
                    else:
                        dst = block_max[:, h, first:first + 2 * step].rearrange("p (a c) -> p a c", c=step)[:, :, 0:count]
                        src = p_fill[f % 2][:, :].rearrange("p (a b c) -> p a b c", a=2, c=P)
                    dve.tensor_reduce(dst, src, AX.X, ALU.max).then_inc(s["fill_used"], 1)
                elif e[0] == "max":
                    pair = e[1]
                    dve.wait_ge(s["fill_used"], (u + 1) * 2 * PAIR_FILLS + (pair + 1) * PAIR_FILLS)
                    dve.tensor_reduce(row_max[:, 2 * pair:2 * pair + 2, :].rearrange("p h (j e) -> p h e j", e=2),
                                      block_max[:, 2 * pair:2 * pair + 2, 0:64].rearrange(
                                          "p h (e j c) -> p h e j c", e=2, j=TPB // 2),
                                      AX.X, ALU.max).then_inc(s["max_ready"], 1)
                elif e[0] == "out":
                    dve.wait_ge(s["shared_full"], shared_place(ev, n, u) + 1)
                    view = p_shared[:, :].rearrange("p (t h r) -> p t h r", t=QC // P, h=GROUP)
                    dve.reciprocal(rden[:, :, :], view[:, :, :, HD]).then_inc(s["dve_chain"], 1)
                    unit = u - e[2]
                    dve.wait_ge(s["dve_chain"], unit * NQC + e[1] + 1)
                    dve.tensor_tensor(
                        attn[:, ds(unit, 1), 4 * e[1]:4 * e[1] + 4, :].rearrange("p u t (h r) -> p (u t) h r", r=HD),
                        view[:, :, :, 0:HD], rden[:, :, :].unsqueeze(3).to_broadcast([P, QC // P, GROUP, HD]),
                        ALU.mult).then_inc(s["shared_used"], 1)

        def build_stack(pool, u):
            for stack, parts, places in ((qstack, qparts, ((0, 0, 3, 1), (1, 3, 6, 2), (2, 4, 5, 1))),
                                         (kstack, kparts, ((0, 2, 5, 1), (1, 1, 6, 4), (2, 0, 1, 1)))):
                view = stack[:, :, :, 0:PRODUCTS * HD].rearrange("p t g (r c) -> p (t g) r c", c=HD)
                for part, lo, hi, step in places:
                    dst = view[:, :, lo:hi:step, :]
                    src = parts[:, part, ds(u, 1), :, :].rearrange("p u t (g c) -> p (u t g) c", c=HD)
                    last = pool.tensor_copy(dst, src.unsqueeze(2).to_broadcast(list(dst.shape)))
            last.then_inc(s["stack_ready"], 1)

        def pool_slot(pool, u, par, kind):
            ev, nxt = slot_events(kind), 1 - par
            maxima = "m" in kind
            if maxima:
                if "p" in kind:
                    pool.wait_ge(s["pv_done"], u * NS)
                pool.tensor_copy(vs[nxt][:, :, :, 0:HD],
                                 v[:, 0, ds(u + 1, 1), :, :].rearrange("p u t (g c) -> p (u t) g c", c=HD)
                                 ).then_inc(s["v_ready"], 1)
            more = maxima and not (isinstance(u, int) and u == UNITS - 2)
            for n, e in enumerate(ev):
                if e == ("turn", 3):
                    if more:
                        pool.wait_ge(s["shared_full"], shared_place(ev, ev.index(("turn", 3)), u) + 1)
                        build_stack(pool, u + 2)
                if e[0] == "max":
                    pair = e[1]
                    pool.wait_ge(s["max_ready"], (u + 1) * 2 + pair + 1)
                    base = [(u + 1) * 8 + 4 * pair]

                    def link(ins):
                        ins.then_inc(s["pool_chain"], 1)
                        base[0] = base[0] + 1
                        pool.wait_ge(s["pool_chain"], base[0])
                    cut = shift16[:, pair, :, :, :]
                    own, top = shift0[:, :].unsqueeze(1).to_broadcast([P, 2, TPB]), row_max[:, 2 * pair:2 * pair + 2, :]
                    link(pool.tensor_tensor(shift[:, pair, :, :], own, top, ALU.subtract))
                    link(pool.tensor_tensor(cut[:, :, 0, :], own, top, ALU.subtract))
                    link(pool.tensor_tensor(rest[:, pair, :, :], shift[:, pair, :, :], cut[:, :, 0, :], ALU.subtract))
                    link(pool.tensor_tensor(cut[:, :, 1, :], shift[:, pair, :, :], cut[:, :, 0, :], ALU.subtract))
                    pool.tensor_tensor(cut[:, :, 2, :], rest[:, pair, :, :], cut[:, :, 1, :], ALU.subtract
                                       ).then_inc(s["shift_ready"], 1)

        def sync_slot(sp, u, par, kind):
            ev, nxt = slot_events(kind), 1 - par
            for n, e in enumerate(ev):
                if e[0] == "shift":
                    sp.wait_ge(s["shared_used"], shared_place(ev, n, u) + 1)
                    for h in range(2):
                        at = h * ROWS + SHIFT_ROW
                        sp.dma_start(qt[nxt][at:at + CROWS, e[1], :],
                                     rows16[e[1]][h * CROWS * TPB:(h + 1) * CROWS * TPB, :]
                                     ).then_inc(rows_loaded[e[1]], 16)

        with nc.Block() as block:
            @block.vector
            def _(dve):
                dve.memset(block_max[:, :, :], NEG)
                for i in range(2):
                    dve.memset(vs[i][:, :, :, HD + 1:32], 0.0)
                    dve.memset(vs[i][:, :, :, HD:HD + 1], 1.0)

            @block.gpsimd
            def _(pool):
                done = 0
                for ins in (lambda: pool.memset(qstack[:, :, :, SHIFT_ROW:ROWS], 0.0),
                            lambda: pool.memset(qstack[:, :, :, ALIBI_ROW:ALIBI_ROW + 2], 1.0),
                            lambda: pool.memset(kstack[:, :, :, SHIFT_ROW:ROWS], 0.0),
                            lambda: pool.memset(kstack[:, :, :, SHIFT_ROW:SHIFT_ROW + 3], 1.0),
                            lambda: pool.memset(shift16[:, :, :, :, :], 0.0),
                            lambda: pool.tensor_copy(kstack[:, :, :, ALIBI_ROW:ALIBI_ROW + 2],
                                                     key_alibi[:, :, :].unsqueeze(2).to_broadcast([P, TPB, GROUP, 2]))):
                    ins().then_inc(s["preset"], 1)
                    done += 1
                    pool.wait_ge(s["preset"], done)
        with nc.Block() as block:
            @block.tensor
            def _(pe):
                slots(tensor_slot)(pe)

            @block.scalar
            def _(act):
                slots(scalar_slot)(act)

            @block.vector
            def _(dve):
                slots(vector_slot)(dve)

            @block.gpsimd
            def _(pool):
                build_stack(pool, 0)
                slots(pool_slot)(pool)

            @block.sync
            def _(sp):
                slots(sync_slot)(sp)


def project_attention(nc, attn, x, bias, ident, w):
    with ExitStack() as ctx:
        sb = lambda n, s, d=F32: ctx.enter_context(nc.sbuf_tensor("pa_" + n, s, d))
        ps = lambda n, s, d=F32: ctx.enter_context(nc.psum_tensor("pa_" + n, s, d))
        sem = lambda n: ctx.enter_context(nc.semaphore("pa_" + n))
        tile = [sb(f"tile{b}", [P, E]) for b in range(B)]
        turned = [sb(f"turned{b}", [P, EH, P]) for b in range(B)]
        p_turn = [ps(f"p_turn{b}", [P, 512]) for b in range(B)]
        p_proj = [ps(f"p_proj{b}", [P, 512]) for b in range(B)]
        tile_ready, turn_psum, turn_ready, proj_ready, proj_used, biased = (
            sem(n) for n in ("tile_ready", "turn_psum", "turn_ready", "proj_ready", "proj_used", "biased"))

        def x_tile(t, b):
            return x[:, ds(t + b * TPB, 1), :].rearrange("p a e -> p (a e)")

        with nc.Block() as block:
            @block.gpsimd
            def _(pool):
                pool.sem_inc(turn_psum, B)
                pool.sem_inc(proj_used, B)
                with pool.Fori(0, TPB) as t:
                    for b in range(B):
                        pool.wait_ge(turn_psum, t * B + b + 1)
                        pool.tensor_copy(tile[b][:, :].rearrange("p (g c) -> p g c", g=GPB),
                                         attn[:, b * GPB:(b + 1) * GPB, ds(t, 1), :].rearrange("p g t c -> p (g t) c")
                                         ).then_inc(tile_ready, 1)
                        pool.tensor_tensor(x_tile(t, b), x_tile(t, b), bias[:, :], ALU.add).then_inc(biased, 1)

            @block.tensor
            def _(pe):
                with pe.Fori(0, TPB) as t:
                    for b in range(B):
                        pe.wait_ge(tile_ready, t * B + b + 1)
                        for h in range(EH):
                            mm = pe.transpose(p_turn[b][:, h * P:(h + 1) * P], tile[b][:, h * P:(h + 1) * P], ident[:, :])
                        mm.then_inc(turn_psum, 1)
                    for b in range(B):
                        pe.wait_ge(turn_ready, t * B + b + 1)
                        pe.wait_ge(proj_used, t * B + b + 1)
                        for h in range(EH):
                            mm = pe.matmul(p_proj[b][:, 0:E], turned[b][:, h, :], w[:, h, :],
                                           start=h == 0, stop=h == EH - 1)
                        mm.then_inc(proj_ready, 1)

            @block.scalar
            def _(act):
                with act.Fori(0, TPB) as t:
                    for b in range(B):
                        act.wait_ge(turn_psum, t * B + b + 1 + B)
                        act.copy(turned[b][:, :, :], p_turn[b][:, 0:E].rearrange("p (h c) -> p h c", h=EH)
                                 ).then_inc(turn_ready, 1)

            @block.vector
            def _(dve):
                with dve.Fori(0, TPB) as t:
                    for b in range(B):
                        dve.wait_ge(proj_ready, t * B + b + 1)
                        dve.wait_ge(biased, t * B + b + 1)
                        dve.tensor_tensor(x_tile(t, b), p_proj[b][:, 0:E], x_tile(t, b), ALU.add
                                          ).then_inc(proj_used, 1)


def normalise_and_turn(nc, tag, x, mean, rstd, ident, xt):
    with ExitStack() as ctx:
        sb = lambda n, s, d=F32: ctx.enter_context(nc.sbuf_tensor(tag + n, s, d))
        ps = lambda n, s, d=F32: ctx.enter_context(nc.psum_tensor(tag + n, s, d))
        sem = lambda n: ctx.enter_context(nc.semaphore(tag + n))
        xn = [sb(f"xn{i}", [P, E]) for i in range(4)]
        p_turn = [ps(f"p_turn{i}", [P, 512]) for i in range(2)]
        xn_ready, turned, taken = sem("xn_ready"), sem("turned"), sem("taken")
        with nc.Block() as block:
            @block.vector
            def _(dve):
                dve.sem_inc(turned, 2)
                dve.sem_inc(taken, 2)
                with dve.Fori(0, TILES // 4) as r:
                    for i in range(4):
                        if i % 2 == 0:
                            dve.wait_ge(turned, r * 2 + i // 2 + 1)
                        dve.tensor_scalar(xn[i][:, :], x[:, ds(r * 4 + i, 1), :].rearrange("p a e -> p (a e)"),
                                          mean[:, ds(r * 4 + i, 1)], rstd[:, ds(r * 4 + i, 1)],
                                          ALU.subtract, ALU.mult).then_inc(xn_ready, 1)

            @block.tensor
            def _(pe):
                with pe.Fori(0, TILES // 4) as r:
                    for j in range(2):
                        pe.wait_ge(xn_ready, r * 4 + 2 * j + 2)
                        pe.wait_ge(taken, r * 2 + j + 1)
                        for i in range(2):
                            for h in range(EH):
                                mm = pe.transpose(p_turn[j][:, (h * 2 + i) * P:(h * 2 + i + 1) * P],
                                                  xn[2 * j + i][:, h * P:(h + 1) * P], ident[:, :])
                        mm.then_inc(turned, 1)

            @block.scalar
            def _(act):
                with act.Fori(0, TILES // 4) as r:
                    for j in range(2):
                        act.wait_ge(turned, r * 2 + j + 3)
                        act.copy(xt[:, :, ds(r, 1), 1 + 2 * j * P:1 + 2 * (j + 1) * P].rearrange("p h r c -> p (h r) c"),
                                 p_turn[j][:, :].rearrange("p (h c) -> p h c", h=EH)).then_inc(taken, 1)


EXPERTS, TOPK, HIDDEN, SHARED_HIDDEN = 8, 2, 176, 352
WIDTH = EXPERTS * HIDDEN + SHARED_HIDDEN
MT = -(-WIDTH // P)
TB = 512
NB = B * S // TB
SLICES = EXPERTS + 1


def router_phase(nc, xt, wr, ident, ident16, priority, gates_t):
    with ExitStack() as ctx:
        sb = lambda n, s, d=F32: ctx.enter_context(nc.sbuf_tensor("ro_" + n, s, d))
        ps = lambda n, s, d=F32: ctx.enter_context(nc.psum_tensor("ro_" + n, s, d))
        sem = lambda n: ctx.enter_context(nc.semaphore("ro_" + n))
        logits_t = sb("logits_t", [EXPERTS, NB, TB])
        T3 = [P, TILES, EXPERTS]
        work = {n: sb(n, T3) for n in "gate shifted pick1 pick2 left order kept rest".split()}
        row = {n: sb(n, [P, TILES]) for n in "top sum first top2 first2 total inv".split()}
        parts = sb("parts", [P, TILES, 3, SLICES], BF16)
        p_logits = ps("p_logits", [P, NB, TB])
        p_tok = ps("p_tok", [P, 512])
        p_gates = ps("p_gates", [P, 1024])
        chain_s, logits_ready, logits_in, tok_ready, shifted_ready, exp_ready, parts_ready, gates_ready = (
            sem(n) for n in "chain logits_ready logits_in tok_ready shifted_ready exp_ready parts_ready gates_ready".split())

        def rows(name):
            return row[name][:, :].unsqueeze(2).to_broadcast(T3)

        with nc.Block() as block:
            @block.tensor
            def _(pe):
                for n in range(NB):
                    for h in range(EH):
                        mm = pe.matmul(p_logits[0:EXPERTS, n, :], wr[:, h, :], xt[:, h, n, 1:],
                                       start=h == 0, stop=h == EH - 1)
                mm.then_inc(logits_ready, 1)
                pe.wait_ge(logits_in, 1)
                for t in range(TILES):
                    mm = pe.transpose(p_tok[:, t * EXPERTS:(t + 1) * EXPERTS],
                                      logits_t[:, t // 4, (t % 4) * P:(t % 4 + 1) * P], ident[0:EXPERTS, 0:EXPERTS])
                mm.then_inc(tok_ready, 1)
                pe.wait_ge(parts_ready, 1)
                for t in range(TILES):
                    mm = pe.transpose(p_gates[:, :].bitcast(BF16)[0:3 * SLICES, t * P:(t + 1) * P],
                                      parts[:, t, :, :].rearrange("p a b -> p (a b)"), ident16[:, :])
                mm.then_inc(gates_ready, 1)

            @block.scalar
            def _(act):
                act.wait_ge(logits_ready, 1)
                act.copy(logits_t[:, :, :], p_logits[0:EXPERTS, :, :]).then_inc(logits_in, 1)
                act.wait_ge(shifted_ready, 1)
                act.activation(work["gate"][:, :, :], work["shifted"][:, :, :], ACT.Exp).then_inc(exp_ready, 1)
                act.wait_ge(gates_ready, 1)
                act.copy(gates_t[:, :], p_gates[:, :].bitcast(BF16)[0:3 * SLICES, :])

            @block.vector
            def _(dve):
                c = Chain(dve, chain_s)
                w = {n: t[:, :, :] for n, t in work.items()}
                tok = p_tok[:, 0:TILES * EXPERTS].rearrange("p (t e) -> p t e", e=EXPERTS)
                order = priority[:, :].unsqueeze(1).to_broadcast(T3)

                def pick(values, top, first, out):
                    c.link(dve.tensor_reduce(row[top][:, :], values, AX.X, ALU.max))
                    c.link(dve.tensor_tensor(out, values, rows(top), ALU.is_equal))
                    c.link(dve.tensor_tensor(w["order"], out, order, ALU.mult))
                    c.link(dve.tensor_reduce(row[first][:, :], w["order"], AX.X, ALU.max))
                    c.link(dve.tensor_tensor(out, w["order"], rows(first), ALU.is_equal))

                c.link(dve.memset(parts[:, :, :, :], 0.0))
                c.link(dve.memset(parts[:, :, 0, EXPERTS:SLICES], 1.0))
                dve.wait_ge(tok_ready, 1)
                c.link(dve.tensor_reduce(row["top"][:, :], tok, AX.X, ALU.max))
                dve.tensor_tensor(w["shifted"], tok, rows("top"), ALU.subtract).then_inc(shifted_ready, 1)
                dve.wait_ge(exp_ready, 1)
                c.link(dve.tensor_reduce(row["sum"][:, :], w["gate"], AX.X, ALU.add))
                c.link(dve.reciprocal(row["inv"][:, :], row["sum"][:, :]))
                c.link(dve.tensor_tensor(w["gate"], w["gate"], rows("inv"), ALU.mult))
                pick(w["gate"], "top", "first", w["pick1"])
                c.link(dve.scalar_tensor_tensor(w["left"], w["pick1"], -2.0, w["gate"], ALU.mult, ALU.add))
                pick(w["left"], "top2", "first2", w["pick2"])
                c.link(dve.tensor_tensor(w["pick1"], w["pick1"], w["pick2"], ALU.add))
                c.link(dve.tensor_tensor(w["kept"], w["gate"], w["pick1"], ALU.mult))
                c.link(dve.tensor_reduce(row["total"][:, :], w["kept"], AX.X, ALU.add))
                c.link(dve.tensor_scalar(row["total"][:, :], row["total"][:, :], 1e-20, None, ALU.add))
                c.link(dve.reciprocal(row["inv"][:, :], row["total"][:, :]))
                c.link(dve.tensor_tensor(w["kept"], w["kept"], rows("inv"), ALU.mult))
                c.link(dve.tensor_copy(parts[:, :, 0, 0:EXPERTS], w["kept"]))
                c.link(dve.tensor_tensor(w["rest"], w["kept"], parts[:, :, 0, 0:EXPERTS], ALU.subtract))
                c.link(dve.tensor_copy(parts[:, :, 1, 0:EXPERTS], w["rest"]))
                dve.tensor_tensor(parts[:, :, 2, 0:EXPERTS], w["rest"], parts[:, :, 1, 0:EXPERTS],
                                  ALU.subtract).then_inc(parts_ready, 1)


def moe_phase(nc, x, xt, gates_t, select, w_gate, w_up, w_down):
    with ExitStack() as ctx:
        sb = lambda n, s, d=F32: ctx.enter_context(nc.sbuf_tensor("moe_" + n, s, d))
        ps = lambda n, s, d=F32: ctx.enter_context(nc.psum_tensor("moe_" + n, s, d))
        sem = lambda n: ctx.enter_context(nc.semaphore("moe_" + n))
        act_out = [sb(f"act{i}", [P, TB]) for i in range(2)]
        prod = [sb(f"prod{i}", [P, TB]) for i in range(2)]
        hidden = [sb(f"hidden{i}", [P, TB]) for i in range(2)]
        p_gate, p_up, p_sel = ([ps(f"{n}{i}", [P, TB]) for i in range(2)] for n in ("p_gate", "p_up", "p_sel"))
        p_down = ps("p_down", [P, TB // P, E])
        gate_ready, up_ready, sel_ready, act_ready, prod_ready, hidden_ready, down_ready, down_used = (
            sem(n) for n in "gate_ready up_ready sel_ready act_ready prod_ready hidden_ready down_ready down_used".split())

        def rows(m):
            return min(P, WIDTH - m * P)

        with nc.Block() as block:
            @block.tensor
            def _(pe):
                with pe.Fori(0, NB) as n:
                    def down(m):
                        pe.wait_ge(hidden_ready, n * MT + m + 1)
                        if m == 0:
                            pe.wait_ge(down_used, n + 1)
                        for t in range(TB // P):
                            mm = pe.matmul(p_down[:, t, :], hidden[m % 2][0:rows(m), t * P:(t + 1) * P],
                                           w_down[0:rows(m), m, :], start=m == 0 and t % 2 == 0,
                                           stop=m == MT - 1, skip_group_check=True)
                        mm.then_inc(down_ready, 1)

                    for m in range(MT):
                        k, i = rows(m), m % 2
                        cols = slice(m * P, m * P + k)
                        if m >= 2:
                            pe.wait_ge(hidden_ready, n * MT + m - 1)
                        for bank, w, ready in ((p_gate, w_gate, gate_ready), (p_up, w_up, up_ready)):
                            for h in range(EH):
                                mm = pe.matmul(bank[i][0:k, :], w[:, h, cols],
                                               xt[:, h, ds(n, 1), 1:].rearrange("p n c -> p (n c)"),
                                               start=h == 0, stop=h == EH - 1)
                            mm.then_inc(ready, 1)
                        pe.matmul(p_sel[i][0:k, :], select[:, cols], gates_t[:, ds(n * TB, TB)],
                                  start=True, stop=True).then_inc(sel_ready, 1)
                        if m >= 1:
                            down(m - 1)
                    down(MT - 1)

            @block.scalar
            def _(act):
                with act.Fori(0, NB) as n:
                    for m in range(MT):
                        k, i = rows(m), m % 2
                        act.wait_ge(gate_ready, n * MT + m + 1)
                        if m >= 2:
                            act.wait_ge(prod_ready, n * MT + m - 1)
                        act.activation(act_out[i][0:k, :], p_gate[i][0:k, :], ACT.Silu).then_inc(act_ready, 1)

            @block.vector
            def _(dve):
                dve.sem_inc(down_used, 1)
                with dve.Fori(0, NB) as n:
                    for m in range(MT):
                        k, i = rows(m), m % 2
                        dve.wait_ge(up_ready, n * MT + m + 1)
                        dve.wait_ge(act_ready, n * MT + m + 1)
                        dve.tensor_tensor(prod[i][0:k, :], p_up[i][0:k, :], act_out[i][0:k, :],
                                          ALU.mult).then_inc(prod_ready, 1)
                        dve.wait_ge(prod_ready, n * MT + m + 1)
                        dve.wait_ge(sel_ready, n * MT + m + 1)
                        if m >= 2:
                            dve.wait_ge(down_ready, n * MT + m - 1)
                        dve.tensor_tensor(hidden[i][0:k, :], p_sel[i][0:k, :], prod[i][0:k, :],
                                          ALU.mult).then_inc(hidden_ready, 1)
                    dve.wait_ge(down_ready, n * MT + MT)
                    tiles = x[:, ds(n * 4, 4), :]
                    dve.tensor_tensor(tiles, p_down[:, :, :], tiles, ALU.add).then_inc(down_used, 1)


RH, RN = 4, 64
L = 64
KAPPA = float(np.exp(-0.5))
CPB = TB // L
VECTORS = "x_w x_a x_g x_r x_v x_k w0 a0 k_k k_a r_k gn_scale gn_offset".split()
VEC = {n: i for i, n in enumerate(VECTORS + ["keep_a"])}
MIXES = "w a g r v k".split()


def time_mix_phase(nc, xt, vec, weights, head_ones, chunk_carry, out):
    with ExitStack() as ctx:
        sb = lambda n, s, d=F32: ctx.enter_context(nc.sbuf_tensor("tm_" + n, s, d))
        ps = lambda n, s, d=F32: ctx.enter_context(nc.psum_tensor("tm_" + n, s, d))
        sem = lambda n: ctx.enter_context(nc.semaphore("tm_" + n))
        HT = [P, EH, TB]
        xx = sb("xx", HT)
        xm = [sb(f"xm{i}", HT) for i in range(2)]
        low_w, low_a, low_g = sb("low_w", [64, TB]), sb("low_a", [64, TB]), sb("low_g", [P, TB])
        sig, aa, cum, kn, sq, up = (sb(n, HT) for n in ("sig", "aa", "cum", "kn", "sq", "up"))
        down = sb("down", [P, EH, CPB, L + 1])
        p_low = [ps(f"p_low{i}", [P, TB]) for i in range(2)]
        p_full = [ps(f"p_full{i}", HT) for i in range(2)]
        p_sum = ps("p_sum", HT)
        s = {n: sem(n) for n in ("chain mix_ready mix_used low_ready full_ready full_used block_done cum_ready "
                                 "sq_ready sum_ready clamp_ready root_ready rk_ready exp_ready act_chain").split()}
        full = lambda t: t[:, :, :]
        blk = lambda t, n: t[:, :, ds(n, 1), :].rearrange("p h n c -> p (h n) c")
        bump = {"chunks": lambda t: t.rearrange("p h (c l) -> p h c l", l=L)}

        def v_(name, h):
            return vec[:, h, VEC[name]:VEC[name] + 1]

        def half_of(name, h, n):
            return out[name][:, h, ds(n, 1), :].rearrange("p n c -> p (n c)")

        with nc.Block() as block:
            @block.vector
            def _(dve):
                c = Chain(dve, s["chain"])
                dve.sem_inc(s["mix_used"], 2)
                dve.sem_inc(s["full_used"], 2)
                dve.sem_inc(s["block_done"], 1)
                c.link(dve.memset(down[:, :, :, 0:1], 1.0))
                c.link(dve.memset(xt[:, :, :, 0:1], 0.0))
                c.link(dve.tensor_copy(xt[:, :, 1::2, 0], xt[:, :, 0::2, TB]))
                c.link(dve.tensor_scalar(vec[:, :, VEC["keep_a"]:VEC["keep_a"] + 1], vec[:, :, VEC["k_a"]:VEC["k_a"] + 1],
                                         -1.0, 1.0, ALU.mult, ALU.add))
                with dve.Fori(0, NB) as n:
                    c.loop(n, 24)
                    now = xt[:, :, ds(n, 1), 1:].rearrange("p h n c -> p (h n) c")
                    before = xt[:, :, ds(n, 1), 0:TB].rearrange("p h n c -> p (h n) c")
                    c.link(dve.tensor_tensor(full(xx), before, now, ALU.subtract))
                    for i, name in enumerate(MIXES):
                        dve.wait_ge(s["mix_used"], n * 6 + i + 1)
                        for h in range(EH):
                            mix = dve.scalar_tensor_tensor(
                                xm[i % 2][:, h, :], xx[:, h, :], v_("x_" + name, h),
                                xt[:, h, ds(n, 1), 1:].rearrange("p n c -> p (n c)"), ALU.mult, ALU.add)
                            if h == 0:
                                c.mark(mix)
                        mix.then_inc(s["mix_ready"], 1)
                    dve.wait_ge(s["full_used"], n * 6 + 3)
                    c.link(dve.tensor_tensor_scan(cum[:, 0, :], chunk_carry[:, :], sig[:, 0, :], 0.0, ALU.mult, ALU.add))
                    dve.tensor_tensor_scan(cum[:, 1, :], chunk_carry[:, :], sig[:, 1, :], 0.0, ALU.mult,
                                           ALU.add).then_inc(s["cum_ready"], 1)
                    dve.wait_ge(s["full_used"], n * 6 + 4)
                    for h in range(EH):
                        c.link(dve.tensor_scalar(xx[:, h, :], aa[:, h, :], v_("k_a", h), v_("keep_a", h), ALU.mult, ALU.add))
                    dve.wait_ge(s["full_used"], n * 6 + 8)
                    c.link(dve.tensor_scalar(kn[:, 0, :], half_of("kt", 0, n), v_("k_k", 0), None, ALU.mult))
                    c.link(dve.tensor_scalar(kn[:, 1, :], half_of("kt", 1, n), v_("k_k", 1), None, ALU.mult))
                    c.mark(dve.tensor_tensor(full(xx), full(xx), blk(out["kt"], n), ALU.mult))
                    dve.tensor_tensor(full(sq), full(kn), full(kn), ALU.mult).then_inc(s["sq_ready"], 1)
                    dve.wait_ge(s["sum_ready"], n * 2 + 1)
                    dve.tensor_scalar(full(sq), full(p_sum), 1e-24, None, ALU.max).then_inc(s["clamp_ready"], 1)
                    c.wait()
                    dve.wait_ge(s["mix_used"], n * 6 + 8)
                    c.link(dve.scalar_tensor_tensor(xm[0][:, 0, :], half_of("rt", 0, n), v_("r_k", 0), xx[:, 0, :], ALU.mult, ALU.mult))
                    dve.scalar_tensor_tensor(xm[0][:, 1, :], half_of("rt", 1, n), v_("r_k", 1), xx[:, 1, :], ALU.mult,
                                             ALU.mult).then_inc(s["rk_ready"], 1)
                    dve.wait_ge(s["root_ready"], n + 1)
                    c.link(dve.reciprocal(full(sq), full(sq)))
                    c.link(dve.tensor_tensor(full(kn), full(kn), full(sq), ALU.mult))
                    dve.wait_ge(s["exp_ready"], n * 2 + 1)
                    c.link(dve.tensor_tensor(bump["chunks"](blk(out["rt"], n)), bump["chunks"](blk(out["rt"], n)), down[:, :, :, 1:], ALU.mult))
                    for h in range(EH):
                        c.link(dve.scalar_tensor_tensor(
                            out["at"][:, h, ds(n, 1), :].rearrange("p n (c l) -> p (n c) l", l=L),
                            kn[:, h, :].rearrange("p (c l) -> p c l", l=L), -1.0, down[:, h, :, 0:L], ALU.mult, ALU.mult))
                    c.link(dve.tensor_copy(out["chunk_decay"][:, :, ds(n, 1), :].rearrange("p h n c -> p (h n) c"),
                                           down[:, :, :, L]))
                    c.link(dve.tensor_tensor(full(aa), full(kn), full(aa), ALU.mult))
                    dve.wait_ge(s["exp_ready"], n * 2 + 2)
                    c.link(dve.tensor_tensor(blk(out["bt"], n), full(aa), full(up), ALU.mult))
                    c.link(dve.tensor_tensor(blk(out["kt"], n), full(xx), full(up), ALU.mult))
                    dve.wait_ge(s["sum_ready"], n * 2 + 2)
                    c.link(dve.tensor_tensor(blk(out["bonus"], n), full(p_sum), blk(out["vt"], n), ALU.mult))
                    dve.sem_inc(s["block_done"], 1)
                c.end(NB)

            @block.tensor
            def _(pe):
                with pe.Fori(0, NB) as n:
                    def first(i):
                        name = MIXES[i]
                        pe.wait_ge(s["mix_ready"], n * 6 + i + 1)
                        if i < 3:
                            m = {"w": 64, "a": 64, "g": P}[name]
                            for h in range(EH):
                                mm = pe.matmul(p_low[i % 2][0:m, :], weights[name + "1"][:, h, :], xm[i % 2][:, h, :],
                                               start=h == 0, stop=h == EH - 1)
                        else:
                            pe.wait_ge(s["full_used"], n * 6 + i + 1)
                            for o in range(EH):
                                for h in range(EH):
                                    mm = pe.matmul(p_full[i % 2][:, o, :], weights[name][:, h, o * P:(o + 1) * P],
                                                   xm[i % 2][:, h, :], start=h == 0, stop=h == EH - 1)
                        mm.then_inc(s["mix_used"], 1)

                    def second(i):
                        pe.wait_ge(s["low_ready"], n * 3 + i + 1)
                        pe.wait_ge(s["full_used"], n * 6 + i + 1)
                        low, w = ((low_w, weights["w2"]), (low_a, weights["a2"]), (low_g, weights["g2"]))[i]
                        for o in range(EH):
                            mm = pe.matmul(p_full[i % 2][:, o, :], w[:, o * P:(o + 1) * P], low[:, :], start=True, stop=True)
                        mm.then_inc(s["full_ready"], 1)

                    def head_sums(src):
                        for o in range(EH):
                            mm = pe.matmul(p_sum[:, o, :], head_ones[:, :], src[:, o, :], start=True, stop=True)
                        mm.then_inc(s["sum_ready"], 1)

                    first(0)
                    first(1)
                    second(0)
                    first(2)
                    second(1)
                    second(2)
                    for i in (3, 4, 5):
                        first(i)
                    pe.wait_ge(s["sq_ready"], n + 1)
                    head_sums(sq)
                    pe.wait_ge(s["clamp_ready"], n + 1)
                    pe.wait_ge(s["rk_ready"], n + 1)
                    head_sums(xm[0])

            @block.scalar
            def _(act):
                with act.Fori(0, NB) as n:
                    def low(i, dst, func):
                        act.wait_ge(s["mix_used"], n * 6 + i + 3)
                        src = p_low[i % 2][0:dst.shape[0], :]
                        ins = act.copy(dst[:, :], src) if func is None else act.activation(dst[:, :], src, func)
                        ins.then_inc(s["low_ready"], 1)

                    def take(i, dst, bias=None):
                        if i < 3:
                            act.wait_ge(s["full_ready"], n * 3 + i + 1)
                        else:
                            act.wait_ge(s["mix_used"], n * 6 + i + 3)
                        if bias is None:
                            act.copy(dst, p_full[i % 2][:, :, :]).then_inc(s["full_used"], 1)
                        else:
                            act.activation(dst[:, 0, :], p_full[i % 2][:, 0, :], ACT.Sigmoid, bias=v_(bias, 0))
                            act.activation(dst[:, 1, :], p_full[i % 2][:, 1, :], ACT.Sigmoid, bias=v_(bias, 1)
                                           ).then_inc(s["full_used"], 1)

                    act.wait_ge(s["block_done"], n + 1)
                    low(0, low_w, ACT.Tanh)
                    low(1, low_a, None)
                    take(0, sig, "w0")
                    low(2, low_g, ACT.Sigmoid)
                    take(1, aa, "a0")
                    take(2, blk(out["gt"], n))
                    take(3, blk(out["rt"], n))
                    take(4, blk(out["vt"], n))
                    take(5, blk(out["kt"], n))
                    act.wait_ge(s["clamp_ready"], n + 1)
                    act.activation(full(sq), full(sq), ACT.Sqrt).then_inc(s["root_ready"], 1)
                    act.wait_ge(s["cum_ready"], n + 1)
                    for h in range(EH):
                        ins = act.activation(down[:, h, :, 1:], cum[:, h, :].rearrange("p (c l) -> p c l", l=L),
                                             ACT.Exp, scale=-KAPPA)
                    ins.then_inc(s["exp_ready"], 1)
                    act.activation(full(up), full(cum), ACT.Exp, scale=KAPPA).then_inc(s["exp_ready"], 1)


LEVELS = [1 << i for i in range(L.bit_length() - 1)]
HALF_CHUNKS = P // L


def marks_of(*names):
    return {n: i + 1 for i, n in enumerate(names)} | {"each": len(names)}


INNER = [m for m in LEVELS if m > 1]
PE_MARKS = marks_of("turn", "a1", "a2", "a3", "w0", *[f"{k}{m}" for m in INNER for k in ("z", "xz", "zy")
                                                      if not (k == "xz" and m == INNER[-1])],
                    "ta", "r", "yv", "gh0", "gh1", "ys0", "hop0", "ys1", "hop1")
DVE_MARKS = marks_of("a1e", "a1o", "a2e", "a2o", "x1e", "x1o", "x1", "y1m", "y1",
                     *[f"{k}{m}" for m in INNER for k in ("z", "x", "y") if not (k == "x" and m == INNER[-1])],
                     "r", "gh0", "g0", "gh1", "g1", "st0a", "st0", "st1a", "st1")
ACT_MARKS = marks_of("tok", "w0", "ta", "y")


def recurrence_phase(nc, data, ident, masks, level_masks, level1_t, head_ones, yt):
    with ExitStack() as ctx:
        sb = lambda n, s, d=F32: [ctx.enter_context(nc.sbuf_tensor(f"rc_{n}{b}", s, d)) for b in range(B)]
        sem = lambda n: [ctx.enter_context(nc.semaphore(f"rc_{n}{b}")) for b in range(B)]
        bank = [[ctx.enter_context(nc.psum_tensor(f"rc_bank{b}_{i}", [P, 512], F32)) for i in range(4)] for b in range(B)]
        bt, kt, vt = sb("bt", [P, EH, P]), sb("kt", [P, EH, P]), sb("vt", [P, EH, P])
        ar = sb("ar", [P, EH, 2 * P])
        tok_b, tok_k, tok_v = sb("tok_b", [P, E]), sb("tok_k", [P, E]), sb("tok_v", [P, E])
        aw = sb("aw", [P, RH, 2 * RN])
        ab = sb("ab", [P, 2, EH, 2, P])
        ak = sb("ak", [P, 2, EH, 2, P])
        X, Y, Z = sb("X", [P, RH, P]), sb("Y", [P, RH, P]), sb("Z", [P, RH, P])
        ta = sb("ta", [P, EH, 2, P])
        rh = sb("rh", [P, EH, P])
        gh = [sb(f"gh{c}_", [P, EH, 2, P]) for c in range(2)]
        state = [sb(f"state{c}_", [P, EH, P]) for c in range(2)]
        made, dve_did, act_did, staged = sem("made"), sem("dve_did"), sem("act_did"), sem("staged")

        def flat(t):
            return t[:, :, :, :].rearrange("p h n c -> p h (n c)")

        def src(name, t, b):
            return flat(data[name])[:, :, ds(t * P + b * S, P)]

        def pe_wait(pe, t, b, dve=None, act=None):
            if dve:
                pe.wait_ge(dve_did[b], t * DVE_MARKS["each"] + DVE_MARKS[dve])
            if act:
                pe.wait_ge(act_did[b], t * ACT_MARKS["each"] + ACT_MARKS[act])

        def heads():
            return [(h, h // 2, h % 2) for h in range(RH)]

        def head_rows(par):
            return slice(par * RN, par * RN + RN)

        with nc.Block() as block:
            @block.tensor
            def _(pe):
                def turn(t, b):
                    pe.wait_ge(staged[b], t + 1)
                    for n, (a, c) in enumerate(((bt, kt), (ar, vt))):
                        for h in range(EH):
                            pe.transpose(bank[b][n][:, h * P:(h + 1) * P], a[b][:, h, 0:P], ident[:, :])
                            mm = pe.transpose(bank[b][n][:, (2 + h) * P:(3 + h) * P], c[b][:, h, :], ident[:, :])
                    mm.then_inc(made[b], 1)

                def against(rows_of, banks, width, rhs):
                    def stage(t, b):
                        for h, half, par in heads():
                            r = head_rows(par)
                            mm = pe.matmul(bank[b][banks[par]][:, half * width:(half + 1) * width],
                                           rows_of[b][r, half, 0:P], rhs[b][r, half, 0:width],
                                           start=True, stop=True, skip_group_check=True)
                        mm.then_inc(made[b], 1)
                    return stage

                def a1(t, b):
                    against(bt, (2, 3), 2 * P, ar)(t, b)

                def a2(t, b):
                    pe_wait(pe, t, b, act="tok")
                    against(kt, (0, 1), 2 * P, ar)(t, b)

                def a3(t, b):
                    pe_wait(pe, t, b, dve="a1o")
                    against(ar, (2, 3), P, bt)(t, b)

                def per_head(n, lhs, rhs, width=P):
                    def stage(t, b):
                        for h, half, par in heads():
                            mm = pe.matmul(bank[b][n][:, h * width:(h + 1) * width], lhs(b, h, half, par),
                                           rhs(b, h, half, par), start=True, stop=True)
                        mm.then_inc(made[b], 1)
                    return stage

                def w0(t, b):
                    pe_wait(pe, t, b, dve="a2o")
                    per_head(0, lambda b, h, half, par: ak[b][:, par, half, 0, :],
                             lambda b, h, half, par: tok_v[b][:, h * RN:(h + 1) * RN], RN)(t, b)

                def z(m):
                    def stage(t, b):
                        pe_wait(pe, t, b, dve="x1" if m == 2 else f"x{m // 2}")
                        per_head(1, lambda b, h, half, par: ab[b][:, par, half, 0, :],
                                 lambda b, h, half, par: X[b][:, h, :])(t, b)
                    return stage

                def xz(m):
                    def stage(t, b):
                        pe_wait(pe, t, b, dve=f"z{m}")
                        per_head(2, lambda b, h, half, par: Y[b][:, h, :], lambda b, h, half, par: Z[b][:, h, :])(t, b)
                    return stage

                def zy(m):
                    def stage(t, b):
                        pe_wait(pe, t, b, dve=f"z{m}")
                        per_head(3, lambda b, h, half, par: Z[b][:, h, :], lambda b, h, half, par: Y[b][:, h, :])(t, b)
                    return stage

                def ta_(t, b):
                    pe_wait(pe, t, b, dve=f"y{INNER[-1]}", act="w0")
                    per_head(0, lambda b, h, half, par: Y[b][:, h, :], lambda b, h, half, par: aw[b][:, h, :])(t, b)

                def r_(t, b):
                    pe_wait(pe, t, b, act="ta")
                    for h, half, par in heads():
                        mm = pe.matmul(bank[b][1][head_rows(par), half * P:(half + 1) * P],
                                       ta[b][:, half, 0, head_rows(par)], ab[b][:, par, half, 1, :],
                                       start=half == 0, stop=True, skip_group_check=True)
                    mm.then_inc(made[b], 1)

                def yv(t, b):
                    for h, half, par in heads():
                        out = bank[b][2][head_rows(par), half * P:(half + 1) * P]
                        pe.matmul(out, ta[b][:, half, 1, head_rows(par)], ab[b][:, par, half, 1, :],
                                  start=half == 0, stop=False, skip_group_check=True)
                        mm = pe.matmul(out, tok_v[b][:, h * RN:(h + 1) * RN], ak[b][:, par, half, 1, :],
                                       start=False, stop=True, skip_group_check=True)
                    mm.then_inc(made[b], 1)

                def gh_(c):
                    def stage(t, b):
                        dst, rows = bank[b][(3, 0)[c]], slice(c * L, (c + 1) * L)
                        for half in range(EH):
                            cols = slice(half * P, (half + 1) * P)
                            at = half * 2 * P
                            pe.matmul(dst[:, at:at + P], ta[b][rows, half, 0, :], tok_b[b][rows, cols],
                                      start=True, stop=True)
                            pe.matmul(dst[:, at + P:at + 2 * P], tok_b[b][rows, cols], ta[b][rows, half, 1, :],
                                      start=True, stop=False)
                            mm = pe.matmul(dst[:, at + P:at + 2 * P], tok_k[b][rows, cols], tok_v[b][rows, cols],
                                           start=False, stop=True)
                        mm.then_inc(made[b], 1)
                    return stage

                def ys(c):
                    def stage(t, b):
                        if c == 0:
                            pe.wait_ge(dve_did[b], t * DVE_MARKS["each"] + DVE_MARKS["r"])
                        else:
                            pe_wait(pe, t, b, dve="st0")
                        for half in range(EH):
                            mm = pe.matmul(bank[b][2][:, half * P + c * L:half * P + (c + 1) * L],
                                           state[c][b][:, half, :], rh[b][:, half, c * L:(c + 1) * L],
                                           start=False, stop=True, skip_group_check=True)
                        mm.then_inc(made[b], 1)
                    return stage

                def hop(c):
                    def stage(t, b):
                        pe_wait(pe, t, b, dve=f"g{c}")
                        for half in range(EH):
                            mm = pe.matmul(bank[b][1][:, half * P:(half + 1) * P], gh[c][b][:, half, 0, :],
                                           state[c][b][:, half, :], start=True, stop=True)
                        mm.then_inc(made[b], 1)
                    return stage

                stages = [turn, a1, a2, a3, w0]
                for m in INNER:
                    stages += [z(m), zy(m)] if m == INNER[-1] else [z(m), xz(m), zy(m)]
                def settle(t, b):
                    pe_wait(pe, t, b, dve="st1", act="y")

                stages += [ta_, r_, yv, gh_(0), gh_(1), ys(0), hop(0), ys(1), hop(1), settle]
                with pe.Fori(0, TPB) as t:
                    for stage in stages:
                        for b in range(B):
                            stage(t, b)

            @block.vector
            def _(dve):
                def did(b, ins):
                    ins.then_inc(dve_did[b], 1)

                def own(t, b, name):
                    dve.wait_ge(dve_did[b], t * DVE_MARKS["each"] + DVE_MARKS[name])

                def need(t, b, name):
                    dve.wait_ge(made[b], t * PE_MARKS["each"] + PE_MARKS[name])

                def masked(stage_name, dst, banks):
                    def stage(t, b):
                        need(t, b, stage_name)
                        for par in range(2):
                            did(b, dve.tensor_tensor(
                                dst[b][:, par, :, :, :].rearrange("p h k c -> p h (k c)"),
                                bank[b][banks[par]][:, :].rearrange("p (h c) -> p h c", h=EH),
                                masks[:, :].unsqueeze(1).to_broadcast([P, EH, 2 * P]), ALU.mult))
                    return stage

                eye = ident[:, :].unsqueeze(1).to_broadcast([P, RH, P])

                def x1(t, b):
                    need(t, b, "a3")
                    for par in range(2):
                        did(b, dve.tensor_tensor(
                            X[b][:, par::2, :], bank[b][2 + par][:, 0:2 * P].rearrange("p (h c) -> p h c", h=EH),
                            level_masks[:, 0, :].unsqueeze(1).to_broadcast([P, EH, P]), ALU.mult))
                    own(t, b, "x1o")
                    did(b, dve.tensor_tensor(X[b][:, :, :], X[b][:, :, :], eye, ALU.add))

                def y1(t, b):
                    did(b, dve.tensor_tensor(
                        Y[b][:, :, :].rearrange("p (h q) c -> p q h c", q=2), ab[b][:, :, :, 0, :],
                        level1_t[:, :].unsqueeze(1).unsqueeze(1).to_broadcast([P, 2, EH, P]), ALU.mult))
                    own(t, b, "y1m")
                    did(b, dve.tensor_tensor(Y[b][:, :, :], Y[b][:, :, :], eye, ALU.add))

                def z(m):
                    def stage(t, b):
                        need(t, b, f"z{m}")
                        did(b, dve.tensor_tensor(
                            Z[b][:, :, :], bank[b][1][:, :].rearrange("p (h c) -> p h c", h=RH),
                            level_masks[:, LEVELS.index(m), :].unsqueeze(1).to_broadcast([P, RH, P]), ALU.mult))
                    return stage

                def grow(kind, buf, n, m):
                    def stage(t, b):
                        need(t, b, {"x": "xz", "y": "zy"}[kind] + str(m))
                        did(b, dve.tensor_tensor(buf[b][:, :, :], bank[b][n][:, :].rearrange("p (h c) -> p h c", h=RH),
                                                 buf[b][:, :, :], ALU.add))
                    return stage

                def r_(t, b):
                    need(t, b, "r")
                    did(b, dve.tensor_tensor(rh[b][:, :, :], bank[b][1][:, 0:2 * P].rearrange("p (h c) -> p h c", h=EH),
                                             src("rt", t, b), ALU.add))

                def gh_(c):
                    def stage(t, b):
                        need(t, b, f"gh{c}")
                        did(b, dve.tensor_tensor(
                            gh[c][b][:, :, :, :].rearrange("p h k c -> p (h k) c"),
                            bank[b][(3, 0)[c]][:, :].rearrange("p (h c) -> p h c", c=P),
                            head_ones[:, :].unsqueeze(1).to_broadcast([P, 2 * EH, P]), ALU.mult))
                        own(t, b, f"gh{c}")
                        did(b, dve.tensor_tensor(gh[c][b][:, :, 0, :], gh[c][b][:, :, 0, :],
                                                 ident[:, :].unsqueeze(1).to_broadcast([P, EH, P]), ALU.add))
                    return stage

                def advance(c):
                    def stage(t, b):
                        need(t, b, f"hop{c}")
                        dst = state[1 - c][b]
                        did(b, dve.tensor_tensor(dst[:, :, :], bank[b][1][:, 0:2 * P].rearrange("p (h c) -> p h c", h=EH),
                                                 gh[c][b][:, :, 1, :], ALU.add))
                        own(t, b, f"st{c}a")
                        decay = flat(data["chunk_decay"])[:, :, ds(t * HALF_CHUNKS + (b * S // L + c), 1)]
                        did(b, dve.tensor_tensor(dst[:, :, :], dst[:, :, :], decay.to_broadcast([P, EH, P]), ALU.mult))
                    return stage

                stages = [masked("a1", ab, (2, 3)), masked("a2", ak, (0, 1)), x1, y1]
                for m in INNER:
                    stages.append(z(m))
                    if m != INNER[-1]:
                        stages.append(grow("x", X, 2, m))
                    stages.append(grow("y", Y, 3, m))
                stages += [r_, gh_(0), gh_(1), advance(0), advance(1)]
                with dve.Fori(0, TPB) as t:
                    for stage in stages:
                        for b in range(B):
                            stage(t, b)

            @block.scalar
            def _(act):
                def need(t, b, name):
                    act.wait_ge(made[b], t * PE_MARKS["each"] + PE_MARKS[name])

                def tok(t, b):
                    need(t, b, "turn")
                    act.copy(tok_b[b][:, :], bank[b][0][:, 0:E])
                    act.copy(tok_k[b][:, :], bank[b][0][:, E:2 * E])
                    act.copy(aw[b][:, :, 0:RN], bank[b][1][:, 0:E].rearrange("p (h c) -> p h c", h=RH))
                    act.copy(tok_v[b][:, :], bank[b][1][:, E:2 * E]).then_inc(act_did[b], 1)

                def w0(t, b):
                    need(t, b, "w0")
                    act.copy(aw[b][:, :, RN:2 * RN], bank[b][0][:, 0:E].rearrange("p (h c) -> p h c", h=RH)
                             ).then_inc(act_did[b], 1)

                def ta_(t, b):
                    need(t, b, "ta")
                    for half in range(EH):
                        ins = act.copy(ta[b][:, half, :, :].rearrange("p k (q c) -> p q k c", q=2),
                                       bank[b][0][:, half * 2 * P:(half + 1) * 2 * P].rearrange(
                                           "p (q k c) -> p q k c", q=2, k=2))
                    ins.then_inc(act_did[b], 1)

                def y_(t, b):
                    need(t, b, "ys1")
                    act.copy(flat(yt)[:, :, ds(t * P + b * S, P)],
                             bank[b][2][:, 0:2 * P].rearrange("p (h c) -> p h c", h=EH)).then_inc(act_did[b], 1)

                with act.Fori(0, TPB) as t:
                    for stage in (tok, w0, ta_, y_):
                        for b in range(B):
                            stage(t, b)

            @block.gpsimd
            def _(pool):
                def stage(t, b):
                    pool.tensor_copy(ar[b][:, :, 0:P], src("at", t, b))
                    pool.tensor_copy(ar[b][:, :, P:2 * P], src("rt", t, b))
                    pool.tensor_copy(vt[b][:, :, :], src("vt", t, b))
                    pool.tensor_copy(kt[b][:, :, :], src("kt", t, b))
                    pool.tensor_copy(bt[b][:, :, :], src("bt", t, b)).then_inc(staged[b], 1)

                for b in range(B):
                    pool.memset(state[0][b][:, :, :], 0.0)
                    stage(0, b)
                with pool.Fori(0, TPB - 1) as t:
                    for b in range(B):
                        pool.wait_ge(made[b], t * PE_MARKS["each"] + PE_MARKS["a3"])
                        stage(t + 1, b)


def gate_and_project(nc, data, vec, w, x):
    with ExitStack() as ctx:
        sb = lambda n, s, d=F32: ctx.enter_context(nc.sbuf_tensor("gp_" + n, s, d))
        ps = lambda n, s, d=F32: ctx.enter_context(nc.psum_tensor("gp_" + n, s, d))
        sem = lambda n: ctx.enter_context(nc.semaphore("gp_" + n))
        gated = [sb(f"gated{i}", [P, EH, TB]) for i in range(2)]
        p_proj = [ps(f"p_proj{i}", [P, TB // P, E]) for i in range(2)]
        scaled_ready, gated_ready, proj_ready, proj_used = (
            sem(n) for n in "scaled_ready gated_ready proj_ready proj_used".split())

        def rows(name, h, n):
            return data[name][:, h, ds(n, 1), :].rearrange("p n c -> p (n c)")

        def v_(name, h):
            return vec[:, h, VEC[name]:VEC[name] + 1]

        with nc.Block() as block:
            @block.vector
            def _(dve):
                dve.sem_inc(proj_ready, 2)
                with dve.Fori(0, NB // 2) as r:
                    for i in range(2):
                        n = r * 2 + i
                        dve.wait_ge(proj_ready, r * 2 + i + 1)
                        for h in range(EH):
                            dve.scalar_tensor_tensor(gated[i][:, h, :], rows("yt", h, n), v_("gn_scale", h),
                                                     rows("bonus", h, n), ALU.mult, ALU.add).then_inc(scaled_ready, 1)
                        for h in range(EH):
                            dve.wait_ge(scaled_ready, (r * 2 + i) * EH + h + 1)
                            dve.scalar_tensor_tensor(gated[i][:, h, :], gated[i][:, h, :], v_("gn_offset", h),
                                                     rows("gt", h, n), ALU.add, ALU.mult).then_inc(gated_ready, 1)
                    for i in range(2):
                        dve.wait_ge(proj_ready, r * 2 + i + 3)
                        tiles = x[:, ds((r * 2 + i) * (TB // P), TB // P), :]
                        dve.tensor_tensor(tiles, p_proj[i][:, :, :], tiles, ALU.add).then_inc(proj_used, 1)

            @block.tensor
            def _(pe):
                pe.sem_inc(proj_used, 2)
                with pe.Fori(0, NB // 2) as r:
                    for i in range(2):
                        pe.wait_ge(gated_ready, (r * 2 + i + 1) * EH)
                        pe.wait_ge(proj_used, r * 2 + i + 1)
                        for t in range(TB // P):
                            for h in range(EH):
                                mm = pe.matmul(p_proj[i][:, t, :], gated[i][:, h, t * P:(t + 1) * P], w[:, h, :],
                                               start=h == 0 and t % 2 == 0, stop=h == EH - 1, skip_group_check=True)
                        mm.then_inc(proj_ready, 1)


FFN = 2 * E
FT = FFN // P
TIE = 2.0 ** -25


def switch_phase(nc, xt, w_switch, ident, masks):
    with ExitStack() as ctx:
        sb = lambda n, s, d=F32: ctx.enter_context(nc.sbuf_tensor("sw_" + n, s, d))
        ps = lambda n, s, d=F32: ctx.enter_context(nc.psum_tensor("sw_" + n, s, d))
        sem = lambda n: ctx.enter_context(nc.semaphore("sw_" + n))
        logits_t = sb("logits_t", [2, NB, TB])
        tok = sb("tok", [P, TILES, 2])
        lead = sb("lead", [P, TILES])
        p_logits = ps("p_logits", [P, NB, TB])
        p_tok = ps("p_tok", [P, 512])
        logits_ready, logits_in, tok_ready, chain_s = (sem(n) for n in "logits_ready logits_in tok_ready chain".split())
        with nc.Block() as block:
            @block.tensor
            def _(pe):
                for n in range(NB):
                    for h in range(EH):
                        mm = pe.matmul(p_logits[0:2, n, :], w_switch[:, h, :], xt[:, h, n, 1:],
                                       start=h == 0, stop=h == EH - 1)
                mm.then_inc(logits_ready, 1)
                pe.wait_ge(logits_in, 1)
                for t in range(TILES):
                    mm = pe.transpose(p_tok[:, t * 2:(t + 1) * 2],
                                      logits_t[:, t // 4, (t % 4) * P:(t % 4 + 1) * P], ident[0:2, 0:2])
                mm.then_inc(tok_ready, 1)

            @block.scalar
            def _(act):
                act.wait_ge(logits_ready, 1)
                act.copy(logits_t[:, :, :], p_logits[0:2, :, :]).then_inc(logits_in, 1)

            @block.vector
            def _(dve):
                c = Chain(dve, chain_s)
                dve.wait_ge(tok_ready, 1)
                c.link(dve.tensor_copy(tok[:, :, :].rearrange("p t e -> p (t e)"), p_tok[:, 0:2 * TILES]))
                c.link(dve.tensor_tensor(lead[:, :], tok[:, :, 1], tok[:, :, 0], ALU.subtract))
                dve.tensor_scalar(masks[:, :, 1], lead[:, :], TIE, None, ALU.is_gt)
                dve.tensor_scalar(masks[:, :, 0], lead[:, :], TIE, None, ALU.is_le)


def switched_ffn_phase(nc, x, xt, masks, w_in, b_in, w_out, b_out):
    with ExitStack() as ctx:
        sb = lambda n, s, d=F32: ctx.enter_context(nc.sbuf_tensor("ff_" + n, s, d))
        ps = lambda n, s, d=F32: ctx.enter_context(nc.psum_tensor("ff_" + n, s, d))
        sem = lambda n: ctx.enter_context(nc.semaphore("ff_" + n))
        hidden = [sb(f"hidden{i}", [P, TB]) for i in range(2)]
        p_in = [ps(f"p_in{i}", [P, TB]) for i in range(2)]
        p_out = [ps(f"p_out{e}", [P, TB // P, E]) for e in range(2)]
        in_ready, hidden_ready, out_ready, out_used, biased, chain_s = (
            sem(n) for n in "in_ready hidden_ready out_ready out_used biased chain".split())
        HT = 2 * FT
        TPN = TB // P

        with nc.Block() as block:
            @block.tensor
            def _(pe):
                pe.sem_inc(out_used, 2)
                with pe.Fori(0, NB) as n:
                    def out(m):
                        e = m // FT
                        pe.wait_ge(hidden_ready, n * HT + m + 1)
                        if m % FT == 0:
                            pe.wait_ge(out_used, n * 2 + e + 1)
                        for t in range(TPN):
                            mm = pe.matmul(p_out[e][:, t, :], hidden[m % 2][:, t * P:(t + 1) * P], w_out[:, m, :],
                                           start=m % FT == 0 and t % 2 == 0, stop=m % FT == FT - 1,
                                           skip_group_check=True)
                        mm.then_inc(out_ready, 1)

                    for m in range(HT):
                        if m >= 2:
                            pe.wait_ge(hidden_ready, n * HT + m - 1)
                        for h in range(EH):
                            mm = pe.matmul(p_in[m % 2][:, :], w_in[:, h, m * P:(m + 1) * P],
                                           xt[:, h, ds(n, 1), 1:].rearrange("p n c -> p (n c)"),
                                           start=h == 0, stop=h == EH - 1)
                        mm.then_inc(in_ready, 1)
                        if m >= 1:
                            out(m - 1)
                    out(HT - 1)

            @block.scalar
            def _(act):
                act.sem_inc(out_ready, 2)
                with act.Fori(0, NB) as n:
                    for m in range(HT):
                        act.wait_ge(in_ready, n * HT + m + 1)
                        act.wait_ge(out_ready, n * HT + m + 1)
                        act.activation(hidden[m % 2][:, :], p_in[m % 2][:, :], ACT.Gelu if m < FT else ACT.Relu,
                                       bias=b_in[:, m:m + 1]).then_inc(hidden_ready, 1)

            @block.vector
            def _(dve):
                c = Chain(dve, chain_s)
                with dve.Fori(0, NB) as n:
                    c.loop(n, 4 * TPN)
                    at = lambda t: x[:, ds(n * TPN + t, 1), :].rearrange("p a e -> p (a e)")
                    mask = lambda t, e: masks[:, ds(n * TPN + t, 1), e]
                    for e in range(2):
                        for t in range(TPN):
                            if e:
                                c.wait(t + 1)
                            c.mark(dve.scalar_tensor_tensor(at(t), b_out[:, e, :], mask(t, e), at(t), ALU.mult, ALU.add))
                    for e in range(2):
                        dve.wait_ge(out_ready, n * HT + (e + 1) * FT + 2)
                        for t in range(TPN):
                            c.wait((1 + e) * TPN + t + 1)
                            c.mark(dve.scalar_tensor_tensor(at(t), p_out[e][:, t, :], mask(t, e), at(t), ALU.mult, ALU.add))
                        c.wait()
                        dve.sem_inc(out_used, 1)


def start_loads(nc, done, pairs):
    with nc.Block() as block:
        @block.sync
        def _(sp):
            for dst, src in pairs:
                sp.dma_start(dst, src).then_inc(done, 16)
    return len(pairs)


def finish_loads(nc, done, count):
    with nc.Block() as block:
        @block.sync
        def _(sp):
            sp.wait_ge(done, count * 16)


def halves(dram):
    return dram.rearrange("(h p) n -> p h n", p=P)


def two_blocks_program(nc, d, out):
    with ExitStack() as ctx:
        def sb_in(scope):
            return lambda n, s, dt=F32: scope.enter_context(nc.sbuf_tensor(n, s, dt))
        sb, sem = sb_in(ctx), lambda n: ctx.enter_context(nc.semaphore(n))
        start_loaded, moe_loaded, mix_loaded, rec_loaded, ffn_loaded, stored = (
            sem(n) for n in "start_loaded moe_loaded mix_loaded rec_loaded ffn_loaded stored".split())
        x = sb("x", [P, TILES, E])
        ident, ident16 = sb("ident", [P, P]), sb("ident16", [P, P], BF16)
        mean, rstd, eps = sb("mean", [P, TILES]), sb("rstd", [P, TILES]), sb("eps", [P, 1])
        head_ones = sb("head_ones", [P, P])
        vec = sb("vec", [P, EH, len(VECTORS) + 1])
        vec_in = vec[:, :, 0:len(VECTORS)]

        with ExitStack() as block0:
            sb0 = sb_in(block0)
            attn = sb0("attn", [P, UNITS, TPB, GROUP * HD])
            w_proj, b_proj = sb0("w_proj", [P, EH, E]), sb0("b_proj", [P, E])
            w_router, priority = sb0("w_router", [P, EH, EXPERTS]), sb0("priority", [P, EXPERTS])
            with ExitStack() as attention:
                sba = sb_in(attention)
                qparts, kparts = (sba(n, [P, 3, UNITS, TPB, GROUP * HD], BF16) for n in ("qparts", "kparts"))
                v = sba("v", [P, 1, UNITS, TPB, GROUP * HD])
                causal, anticausal = sba("causal", [P, P]), sba("anticausal", [P, P])
                causal16, anticausal16 = sba("causal16", [P, P], BF16), sba("anticausal16", [P, P], BF16)
                abias, shift0 = sba("abias", [P, NQC * TPB]), sba("shift0", [P, TPB])
                key_alibi = sba("key_alibi", [P, TPB, 2])
                with ExitStack() as projection:
                    sbp = sb_in(projection)
                    w_qkv, b_qkv = sbp("w_qkv", [P, EH, 3 * E]), sbp("b_qkv", [P, 3 * E])
                    count = start_loads(nc, start_loaded, [
                        (x[:, :, :], d["x"].rearrange("(t p) e -> p t e", p=P)),
                        (ident[:, :], d["ident"]),
                        (w_qkv[:, :, :], halves(d["w_qkv"])), (b_qkv[:, :], d["b_qkv"]),
                        (causal[:, :], d["causal"]), (anticausal[:, :], d["anticausal"]),
                        (abias[:, :], d["abias"]), (shift0[:, :], d["shift0"]),
                        (key_alibi[:, :, :], d["key_alibi"]),
                        (w_proj[:, :, :], halves(d["w_proj"])), (b_proj[:, :], d["b_proj"]),
                        (w_router[:, :, :], halves(d["w_router"])), (priority[:, :], d["priority"]),
                        (head_ones[:, :], d["head_ones"]), (vec_in, d["vectors"])])
                    finish_loads(nc, start_loaded, count)
                    with nc.Block() as block:
                        @block.vector
                        def _(dve):
                            dve.memset(eps[:, :], EPS)
                            dve.tensor_copy(ident16[:, :], ident[:, :])
                            dve.tensor_copy(causal16[:, :], causal[:, :])
                            dve.tensor_copy(anticausal16[:, :], anticausal[:, :])
                            dve.tensor_scalar(b_qkv[:, 0:E], b_qkv[:, 0:E], HD ** -0.5, None, ALU.mult)
                    layernorm_stats(nc, "ln1_", x, mean, rstd, eps)
                    qkv_phase(nc, x, mean, rstd, ident, w_qkv, b_qkv, qparts, kparts, v)
                attention_phase(nc, ident, ident16, causal16, anticausal16, abias, shift0, key_alibi,
                                qparts, kparts, v, attn)
            select32, select = sb0("select32", [3 * SLICES, WIDTH]), sb0("select", [3 * SLICES, WIDTH], BF16)
            w_gate, w_up = sb0("w_gate", [P, EH, WIDTH]), sb0("w_up", [P, EH, WIDTH])
            w_down = sb0("w_down", [P, MT, E])
            whole = WIDTH // P
            count = start_loads(nc, moe_loaded, [
                (select32[:, :], d["select"]), (w_gate[:, :, :], halves(d["w_gate"])),
                (w_up[:, :, :], halves(d["w_up"])),
                (w_down[:, 0:whole, :], d["w_down"][0:whole * P, :].rearrange("(m p) e -> p m e", p=P)),
                (w_down[0:WIDTH - whole * P, whole, :], d["w_down"][whole * P:WIDTH, :])])
            project_attention(nc, attn, x, b_proj, ident, w_proj)
            layernorm_stats(nc, "ln2_", x, mean, rstd, eps)
            xt = sb0("xt_moe", [P, EH, NB, TB + 1])
            gates_t = sb0("gates_t", [3 * SLICES, B * S], BF16)
            normalise_and_turn(nc, "nt2_", x, mean, rstd, ident, xt)
            router_phase(nc, xt, w_router, ident, ident16, priority, gates_t)
            finish_loads(nc, moe_loaded, count)
            with nc.Block() as block:
                @block.vector
                def _(dve):
                    dve.tensor_copy(select[:, :], select32[:, :])
            moe_phase(nc, x, xt, gates_t, select, w_gate, w_up, w_down)

        w_out = sb("w_out", [P, EH, E])
        data = {n: sb(n, [P, EH, NB, TB]) for n in "rt at bt kt vt gt bonus".split()}
        data["chunk_decay"] = sb("chunk_decay", [P, EH, NB, CPB])
        data["yt"] = data["vt"]
        with ExitStack() as mixing:
            sbm = sb_in(mixing)
            weights = {n: sbm("w_" + n, [P, EH, k]) for n, k in
                       (("w1", 64), ("a1", 64), ("g1", P), ("r", E), ("k", E), ("v", E))}
            weights |= {n: sbm("w_" + n, [k, E]) for n, k in (("w2", 64), ("a2", 64), ("g2", P))}
            carry = sbm("carry", [P, TB])
            xt = sbm("xt_mix", [P, EH, NB, TB + 1])
            count = start_loads(nc, mix_loaded, [
                (w[:, :, :], halves(d["mix_" + n])) if len(w.shape) == 3 else (w[:, :], d["mix_" + n])
                for n, w in weights.items()] + [(carry[:, :], d["carry"]), (w_out[:, :, :], halves(d["w_out"]))])
            layernorm_stats(nc, "ln3_", x, mean, rstd, eps)
            normalise_and_turn(nc, "nt3_", x, mean, rstd, ident, xt)
            finish_loads(nc, mix_loaded, count)
            time_mix_phase(nc, xt, vec, weights, head_ones, carry, data)
        with ExitStack() as recurrence:
            sbr = sb_in(recurrence)
            chunk_masks, level_masks, level1_t = (
                sbr("chunk_masks", [P, 2 * P]), sbr("level_masks", [P, len(LEVELS), P]), sbr("level1_t", [P, P]))
            count = start_loads(nc, rec_loaded, [(chunk_masks[:, :], d["chunk_masks"]),
                                                 (level_masks[:, :, :], d["level_masks"]), (level1_t[:, :], d["level1_t"])])
            finish_loads(nc, rec_loaded, count)
            recurrence_phase(nc, data, ident, chunk_masks, level_masks, level1_t, head_ones, data["yt"])
        w_switch = sb("w_switch", [P, EH, 2])
        w_in, b_in = sb("w_in", [P, EH, 2 * FFN]), sb("b_in", [P, 2 * FT])
        w_back, b_back = sb("w_back", [P, 2 * FT, E]), sb("b_back", [P, 2, E])
        branch, xt = sb("branch", [P, TILES, 2]), sb("xt_ffn", [P, EH, NB, TB + 1])
        count = start_loads(nc, ffn_loaded, [
            (w_switch[:, :, :], halves(d["w_switch"])), (w_in[:, :, :], halves(d["ffn_in"])), (b_in[:, :], d["ffn_b_in"]),
            (w_back[:, :, :], halves(d["ffn_back"])), (b_back[:, :, :], d["ffn_b_back"])])
        gate_and_project(nc, data, vec, w_out, x)
        layernorm_stats(nc, "ln4_", x, mean, rstd, eps)
        normalise_and_turn(nc, "nt4_", x, mean, rstd, ident, xt)
        finish_loads(nc, ffn_loaded, count)
        switch_phase(nc, xt, w_switch, ident, branch)
        switched_ffn_phase(nc, x, xt, branch, w_in, b_in, w_back, b_back)
        with nc.Block() as block:
            @block.sync
            def _(sp):
                sp.dma_start(out.rearrange("(t p) e -> p t e", p=P), x[:, :, :]).then_inc(stored, 16)
                sp.wait_ge(stored, 16)


def shape_constants():
    p = np.arange(P)
    f = np.float32
    key = np.arange(TPB)[None] * P + p[:, None]
    abias = np.stack([SLOPE * (kt * P + p - (c * QC + QC // 2)) for c in range(NQC) for kt in range(TPB)], 1)
    shift0 = [SLOPE * (QC * (t * P // QC) + QC // 2) for t in range(TPB)]
    line = (SLOPE * key).astype(f)
    high = (line.view(np.uint32) & 0xffff0000).view(f)
    row, col = p[:, None], p[None]
    same = row // L == col // L
    joins = [(row // (2 * m) == col // (2 * m)) & (row % (2 * m) >= m) & (col % (2 * m) < m) for m in LEVELS]
    hidden_slice = np.minimum(np.arange(WIDTH) // HIDDEN, EXPERTS)
    select = np.tile(hidden_slice[None] == np.arange(SLICES)[:, None], (3, 1))
    consts = dict(
        ident=np.eye(P), causal=np.where(col <= row, 0, NEG), anticausal=np.where(row <= col, 0, NEG),
        abias=abias, shift0=np.tile(shift0, (P, 1)), key_alibi=np.stack([high, line - high], -1),
        head_ones=row // RN == col // RN, priority=np.tile(EXPERTS - np.arange(EXPERTS), (P, 1)), select=select,
        carry=np.tile(np.arange(TB) % L != 0, (P, 1)),
        chunk_masks=np.concatenate([same & (row < col), same & (row <= col)], 1),
        level_masks=np.stack(joins, 1), level1_t=joins[0].T)
    return {n: np.ascontiguousarray(a, dtype=f) for n, a in consts.items()}


def kernel(**inputs):
    import concourse.bacc as bacc
    from concourse.bass_utils import run_bass_kernel_spmd

    def on_every_row(a):
        return np.broadcast_to(a, (P,) + a.shape)

    def side_by_side(a):
        return a.transpose(1, 0, 2).reshape(a.shape[1], -1)

    z = {n: np.asarray(a) for n, a in inputs.items()}
    a0, f0 = (lambda n: z["L0_attn_" + n]), (lambda n: z["L0_ffn_" + n])
    a1, f1 = (lambda n: z["L1_attn_" + n]), (lambda n: z["L1_ffn_" + n])
    arrays = shape_constants()
    arrays |= dict(
        x=a0("hidden_states").reshape(B * S, E), w_qkv=a0("W_attn"), b_qkv=on_every_row(a0("b_attn")),
        w_proj=a0("W_proj"), b_proj=on_every_row(a0("b_proj")), w_router=f0("router_w").T,
        w_gate=np.concatenate([side_by_side(f0("wg")), f0("sg")], 1),
        w_up=np.concatenate([side_by_side(f0("wu")), f0("su")], 1),
        w_down=np.concatenate([f0("wd").reshape(-1, E), f0("sd")], 0),
        vectors=np.stack([a1(n).reshape(EH, P).T for n in VECTORS], -1),
        w_out=a1("W_o"), w_switch=f1("Wg").T,
        ffn_in=np.concatenate([f1("W0a").T, f1("W1a").T], 1), ffn_back=np.concatenate([f1("W0b").T, f1("W1b").T], 0),
        ffn_b_in=np.concatenate([f1("b0a"), f1("b1a")]).reshape(2 * FT, P).T,
        ffn_b_back=on_every_row(np.stack([f1("b0b"), f1("b1b")])))
    arrays |= {"mix_" + n: a1(n) for n in ("w1", "a1", "g1", "w2", "a2", "g2")}
    arrays |= {"mix_" + n: a1("W_" + n) for n in "rkv"}

    nc = bacc.Bacc("TRN2", target_bir_lowering=False, num_devices=1)
    feeds, dram = {}, {}
    for name, a in arrays.items():
        a = np.ascontiguousarray(a)
        feeds[f"in_{name}_dram"] = a
        dram[name] = nc.dram_tensor(f"in_{name}_dram", a.shape, mybir.dt.from_np(a.dtype), kind="ExternalInput").ap()
    out = nc.dram_tensor("out_0_dram", (B * S, E), F32, kind="ExternalOutput").ap()
    two_blocks_program(nc, dram, out)
    result = run_bass_kernel_spmd(nc, [feeds], core_ids=[0])
    return result.results[0]["out_0_dram"].reshape(B, S, E)
```

```python
from contextlib import ExitStack

import numpy as np

import concourse.bass as bass
from concourse import mybir

ALU = mybir.AluOpType
ACT = mybir.ActivationFunctionType
AX = mybir.AxisListType
F32 = mybir.dt.float32
BF16 = mybir.dt.bfloat16
U32 = mybir.dt.uint32
ds = bass.ds

P = 128
B, S, E = 2, 1024, 256
TILES = B * S // P
TPB = S // P
EH = E // P
HEADS, HD = 32, 8
GROUP = 4
UNITS = B * HEADS // GROUP
GPB = HEADS // GROUP
SLOPE = 2.0 ** (-8.0 / HEADS)
NEG = -1e30
EPS = 1e-5
QC = 512
NQC = S // QC


class Chain:

    def __init__(self, eng, sem):
        self.eng, self.sem, self.done, self.round = eng, sem, 0, None

    def loop(self, i, each):
        self.round, self.each, self.start = i, each, self.done

    def end(self, rounds):
        assert self.done - self.start == self.each, self.done - self.start
        self.round, self.done = None, self.start + self.each * rounds

    def mark(self, ins):
        ins.then_inc(self.sem, 1)
        self.done += 1
        return self.done

    def wait(self, mark=None):
        mark = self.done if mark is None else mark
        self.eng.wait_ge(self.sem, mark if self.round is None else self.round * self.each + mark)

    def link(self, ins):
        self.mark(ins)
        self.wait()


def layernorm_stats(nc, tag, x, mean, rstd, eps):
    with ExitStack() as ctx:
        sb = lambda n, s, d=F32: ctx.enter_context(nc.sbuf_tensor(tag + n, s, d))
        sem = lambda n: ctx.enter_context(nc.semaphore(tag + n))
        stats = sb("stats", [P, TILES, 6])
        half, diff, var, std = (sb(n, [P, TILES]) for n in ("half", "diff", "var", "std"))
        chain_s, var_ready, std_ready = sem("chain"), sem("var_ready"), sem("std_ready")
        with nc.Block() as block:
            @block.vector
            def _(dve):
                c = Chain(dve, chain_s)
                with dve.Fori(0, TILES) as i:
                    c.loop(i, 1)
                    c.mark(dve.bn_stats(stats[:, ds(i, 1), :], x[:, ds(i, 1), :]))
                c.end(TILES)
                c.wait()
                c.link(dve.tensor_tensor(half[:, :], stats[:, :, 1], stats[:, :, 4], ALU.add))
                c.link(dve.tensor_tensor(diff[:, :], stats[:, :, 1], stats[:, :, 4], ALU.subtract))
                c.link(dve.tensor_tensor(var[:, :], stats[:, :, 2], stats[:, :, 5], ALU.add))
                c.link(dve.tensor_scalar(mean[:, :], half[:, :], 0.5, None, ALU.mult))
                c.link(dve.scalar_tensor_tensor(diff[:, :], diff[:, :], 0.25, diff[:, :], ALU.mult, ALU.mult))
                dve.scalar_tensor_tensor(var[:, :], var[:, :], 1.0 / E, diff[:, :], ALU.mult,
                                         ALU.add).then_inc(var_ready, 1)
                dve.wait_ge(std_ready, 1)
                dve.reciprocal(rstd[:, :], std[:, :])

            @block.scalar
            def _(act):
                act.wait_ge(var_ready, 1)
                act.activation(std[:, :], var[:, :], ACT.Sqrt, bias=eps[:, 0:1]).then_inc(std_ready, 1)


def qkv_phase(nc, x, mean, rstd, ident, w, bias, qparts, kparts, v):
    with ExitStack() as ctx:
        sb = lambda n, s, d=F32: ctx.enter_context(nc.sbuf_tensor("qkv_" + n, s, d))
        ps = lambda n, s, d=F32: ctx.enter_context(nc.psum_tensor("qkv_" + n, s, d))
        sem = lambda n: ctx.enter_context(nc.semaphore("qkv_" + n))
        xn = [sb(f"xn{b}", [P, E]) for b in range(B)]
        xt = [sb(f"xt{b}", [P, EH, P]) for b in range(B)]
        qk = [sb(f"qk{b}", [P, 2 * E]) for b in range(B)]
        rest = [sb(f"rest{b}", [P, 2 * E]) for b in range(B)]
        pt = [ps(f"pt{b}", [P, 512]) for b in range(B)]
        pq = [ps(f"pq{b}", [P, 1024]) for b in range(B)]
        names = "xn_ready xt_psum xt_ready proj_ready qk_ready high_ready rest_ready mid_ready low_done proj_used"
        s = {n: sem(n) for n in names.split()}
        scale = HD ** -0.5

        def parts_at(t, buf, part, b):
            return buf[:, part, b * GPB:(b + 1) * GPB, ds(t, 1), :].rearrange("p g t c -> p (g t) c")

        def rounds(step):
            def program(eng):
                step(eng, -1, True, False)
                step(eng, 0, True, False)
                with eng.Fori(0, TPB - 2) as r:
                    step(eng, r + 1, True, True)
                step(eng, TPB - 1, False, True)
                step(eng, TPB, False, True)
            return program

        def now(t):
            return not (isinstance(t, int) and t in (-1, TPB))

        def vector_step(dve, t, more, before):
            for b in range(B if more else 0):
                if now(t):
                    dve.wait_ge(s["xt_psum"], t * B + (b + 1))
                tile = t + (b * TPB + 1)
                dve.tensor_scalar(xn[b][:, :], x[:, ds(tile, 1), :].rearrange("p a e -> p (a e)"),
                                  mean[:, ds(tile, 1)], rstd[:, ds(tile, 1)],
                                  ALU.subtract, ALU.mult).then_inc(s["xn_ready"], 1)
            for b in range(B):
                if now(t):
                    dve.wait_ge(s["proj_ready"], t * B + (b + 1))
                    dve.scalar_tensor_tensor(qk[b][:, 0:E], pq[b][:, 0:E], scale, bias[:, 0:E],
                                             ALU.mult, ALU.add).then_inc(s["qk_ready"], 1)
                    dve.tensor_tensor(qk[b][:, E:2 * E], pq[b][:, E:2 * E], bias[:, E:2 * E],
                                      ALU.add).then_inc(s["qk_ready"], 1)
                    dve.tensor_tensor(parts_at(t, v, 0, b),
                                      pq[b][:, 2 * E:3 * E].rearrange("p (g c) -> p g c", g=GPB),
                                      bias[:, 2 * E:3 * E].rearrange("p (g c) -> p g c", g=GPB),
                                      ALU.add).then_inc(s["proj_used"], 1)
                if before:
                    dve.wait_ge(s["mid_ready"], (t - 1) * B + (b + 1))
                    for n, buf in enumerate((qparts, kparts)):
                        dve.tensor_tensor(parts_at(t - 1, buf, 2, b),
                                          rest[b][:, n * E:(n + 1) * E].rearrange("p (g c) -> p g c", g=GPB),
                                          parts_at(t - 1, buf, 1, b), ALU.subtract).then_inc(s["low_done"], 1)
                if now(t):
                    dve.wait_ge(s["high_ready"], (t * B + (b + 1)) * 2)
                    if before:
                        dve.wait_ge(s["low_done"], ((t - 1) * B + (b + 1)) * 2)
                    for n, buf in enumerate((qparts, kparts)):
                        dve.tensor_tensor(rest[b][:, n * E:(n + 1) * E].rearrange("p (g c) -> p g c", g=GPB),
                                          qk[b][:, n * E:(n + 1) * E].rearrange("p (g c) -> p g c", g=GPB),
                                          parts_at(t, buf, 0, b), ALU.subtract).then_inc(s["rest_ready"], 1)

        def scalar_step(act, t, more, before):
            for b in range(B):
                if now(t):
                    act.wait_ge(s["qk_ready"], (t * B + (b + 1)) * 2)
                    for n, buf in enumerate((qparts, kparts)):
                        act.copy(parts_at(t, buf, 0, b),
                                 qk[b][:, n * E:(n + 1) * E].rearrange("p (g c) -> p g c", g=GPB)
                                 ).then_inc(s["high_ready"], 1)
                if more:
                    act.wait_ge(s["xt_psum"], (t + 1) * B + (b + 1))
                    act.copy(xt[b][:, :, :], pt[b][:, 0:E].rearrange("p (h c) -> p h c", h=EH)
                             ).then_inc(s["xt_ready"], 1)

        def pool_step(pool, t, more, before):
            for b in range(B if now(t) else 0):
                pool.wait_ge(s["rest_ready"], (t * B + (b + 1)) * 2)
                for n, buf in enumerate((qparts, kparts)):
                    last = pool.tensor_copy(parts_at(t, buf, 1, b),
                                            rest[b][:, n * E:(n + 1) * E].rearrange("p (g c) -> p g c", g=GPB))
                last.then_inc(s["mid_ready"], 1)

        def tensor_step(pe, t, more, before):
            for b in range(B if now(t) else 0):
                pe.wait_ge(s["xt_ready"], t * B + (b + 1))
                if before:
                    pe.wait_ge(s["proj_used"], (t - 1) * B + (b + 1))
                for lo, hi in ((0, 512), (512, 768)):
                    for h in range(EH):
                        mm = pe.matmul(pq[b][:, lo:hi], xt[b][:, h, :], w[:, h, lo:hi],
                                       start=h == 0, stop=h == EH - 1)
                mm.then_inc(s["proj_ready"], 1)
            for b in range(B if more else 0):
                pe.wait_ge(s["xn_ready"], (t + 1) * B + (b + 1))
                for h in range(EH):
                    mm = pe.transpose(pt[b][:, h * P:(h + 1) * P], xn[b][:, h * P:(h + 1) * P], ident[:, :])
                mm.then_inc(s["xt_psum"], 1)

        with nc.Block() as block:
            @block.vector
            def _(dve):
                rounds(vector_step)(dve)

            @block.scalar
            def _(act):
                rounds(scalar_step)(act)

            @block.gpsimd
            def _(pool):
                rounds(pool_step)(pool)

            @block.tensor
            def _(pe):
                rounds(tensor_step)(pe)


ROWS = 64
PRODUCTS = 6
SHIFT_ROW = PRODUCTS * HD
ALIBI_ROW = SHIFT_ROW + 3
CROWS = 5
KEY_ORDER = [(0, 1, 3, 2), (0, 7, 1, 6, 2, 5, 3, 4)]
STEPS = [(c, kt) for c in range(NQC) for kt in KEY_ORDER[c]]
LAST0 = len(KEY_ORDER[0]) - 1
FILLS = [([(3, 0, 4)], 40, 1, 4), ([(4, 0, 4)], 16, 1, 4), ([(5, 0, 4)], 48, 1, 4), ([(6, 0, 4)], 27, 1, 4),
         ([(7, 0, 4)], 56, 1, 4), ([(7, 4, 4)], 60, 1, 4), ([(0, 0, 1), (2, 0, 3)], 7, 1, 4),
         ([(4, 4, 1), (6, 4, 3)], 23, 1, 4), ([(1, 0, 2), (5, 4, 2)], 32, 20, 2)]
SLOTS = 72
PAIR_FILLS = 2 * len(FILLS)
FILLS_PER_STEP = [3, 4, 2, 3, 4, 2, 5, 3, 5, 5, 0, 0]


def slot_events(kind):
    extra = {0: ["turn 0", "prev", "turn 1"], 1: ["turn 2"], 2: ["turn 3"], 3: ["out_prev"],
             6: ["out_now"], 8: ["shift 0"]}
    ev, fill = [], 0

    def fills(count):
        nonlocal fill
        for _ in range(count):
            ev.append(("fill", fill // PAIR_FILLS, fill % PAIR_FILLS))
            fill += 1
            if fill % PAIR_FILLS == 0:
                ev.append(("max", fill // PAIR_FILLS - 1))

    for k in range(len(STEPS)):
        step = []
        if "s" in kind:
            step.append(("scores", k, 0))
        for name in extra.get(k, []):
            what, _, arg = name.partition(" ")
            if what in ("turn", "shift") and "m" in kind:
                step.append((what, int(arg)))
            if what == "prev" and "p" in kind:
                step += [("pv", len(STEPS) - 1, 1), ("take", 1, 1)]
            if what == "out_prev" and "p" in kind:
                step.append(("out", 1, 1))
            if what == "out_now" and "s" in kind:
                step.append(("out", 0, 0))
        if "s" in kind:
            step.append(("scores", k, 1))
            if k >= 1:
                step.append(("pv", k - 1, 0))
            if k == LAST0 + 1:
                step.append(("take", 0, 0))
        left = FILLS_PER_STEP[k] if "m" in kind else 0
        after = [n for n, e in enumerate(step) if e[0] in ("scores", "turn", "pv", "out")
                 and not any(x == ("turn", 1) for x in step[n + 1:])]
        for n, e in enumerate(step):
            ev.append(e)
            if n in after:
                now = -(-left // (len(after) - after.index(n)))
                fills(now)
                left -= now
        fills(left)
    if "m" in kind:
        ev.append(("shift", 1))
    return ev


SHARED = ("turn", "shift", "out")


def shared_uses(kind):
    return sum(e[0] in SHARED for e in slot_events(kind))


def shared_place(events, n, u):
    before = sum(e[0] in SHARED for e in events[:n])
    first, second, full = shared_uses("m"), shared_uses("sm"), shared_uses("psm")
    if isinstance(u, int) and u <= 0:
        return before + (first if u == 0 else 0)
    if isinstance(u, int) and u == UNITS:
        return first + second + (UNITS - 2) * full + shared_uses("ps") + before
    return (u - 1) * full + (first + second + before)


def attention_phase(nc, ident, ident16, causal16, anticausal16, abias, shift0, key_alibi, qparts, kparts, v, attn):
    with ExitStack() as ctx:
        sb = lambda n, s, d=F32: ctx.enter_context(nc.sbuf_tensor("at_" + n, s, d))
        ps = lambda n, s, d=F32: ctx.enter_context(nc.psum_tensor("at_" + n, s, d))
        sem = lambda n: ctx.enter_context(nc.semaphore("at_" + n))
        qstack, kstack = (sb(n, [P, TPB, GROUP, ROWS], BF16) for n in ("qstack", "kstack"))
        qt = [sb(f"qt{i}", [P, 2, S], BF16) for i in range(2)]
        kt_ = [sb(f"kt{i}", [P, 2, S], BF16) for i in range(2)]
        vs = [sb(f"vs{i}", [P, TPB, GROUP, 32]) for i in range(2)]
        probs = [sb(f"probs{i}", [P, GROUP, QC]) for i in range(2)]
        block_max = sb("block_max", [P, GROUP, SLOTS])
        row_max = sb("row_max", [P, GROUP, TPB])
        shift = sb("shift", [P, 2, 2, TPB])
        rest = sb("rest", [P, 2, 2, TPB])
        shift16 = sb("shift16", [P, 2, 2, CROWS, TPB], BF16)
        rows16 = [sb(f"rows16{i}", [2 * CROWS * TPB, P], BF16) for i in range(2)]
        ot = sb("ot", [P, QC])
        rden = sb("rden", [P, QC // P, GROUP])
        p_score = [ps(f"p_score{i}", [P, 2, QC]) for i in range(2)]
        p_fill = [ps(f"p_fill{i}", [P, QC]) for i in range(2)]
        p_out = ps("p_out", [P, QC])
        p_shared = ps("p_shared", [P, QC])
        shared16 = p_shared[:, :].bitcast(BF16)
        s = {n: sem(n) for n in ("preset stack_ready v_ready shared_full shared_used fill_ready fill_used "
                                 "max_ready shift_ready rows0 rows1 scores_ready exp_done pv_done "
                                 "out_taken pool_chain dve_chain").split()}
        rows_loaded = [s["rows0"], s["rows1"]]
        NS = len(STEPS)
        DIAG = [k for k, (c, kt) in enumerate(STEPS) if kt * P >= c * QC]

        def left(k):
            c, kt = STEPS[k]
            return max(0, kt * P - c * QC)

        def slots(slot):
            def program(eng):
                slot(eng, -1, 1, "m")
                slot(eng, 0, 0, "sm")
                with eng.Fori(0, UNITS // 2 - 2) as r:
                    slot(eng, r * 2 + 1, 1, "psm")
                    slot(eng, r * 2 + 2, 0, "psm")
                slot(eng, UNITS - 3, 1, "psm")
                slot(eng, UNITS - 2, 0, "psm")
                slot(eng, UNITS - 1, 1, "ps")
                slot(eng, UNITS, 0, "p")
            return program

        def early(u, k=0):
            return isinstance(u, int) and u == 0 and k < 2

        def tensor_slot(pe, u, par, kind):
            ev, nxt = slot_events(kind), 1 - par
            for n, e in enumerate(ev):
                if e[0] in SHARED:
                    before = shared_place(ev, n, u)
                    if not (isinstance(before, int) and before == 0):
                        pe.wait_ge(s["shared_used"], before)
                if e[0] == "turn":
                    if e[1] == 0:
                        pe.wait_ge(s["stack_ready"], u + 2)
                    stack, pair = (qstack, kstack)[e[1] % 2], e[1] // 2
                    for t in range(TPB):
                        mm = pe.transpose(shared16[:, t * P:(t + 1) * P],
                                          stack[:, t, 2 * pair:2 * pair + 2, :].rearrange("p h r -> p (h r)"),
                                          ident16[:, :])
                    mm.then_inc(s["shared_full"], 1)
                elif e[0] == "fill":
                    pair, f = e[1:]
                    at, h = f // 2, f % 2
                    if pair * PAIR_FILLS + f >= 2:
                        pe.wait_ge(s["fill_used"], (u + 1) * 2 * PAIR_FILLS + pair * PAIR_FILLS + f - 1)
                    if f == 0:
                        pe.wait_ge(s["shared_used"], shared_place(ev, ev.index(("turn", 2 * pair + 1)), u) + 1)
                    bank, col = p_fill[f % 2], 0
                    for t, b0, nb in FILLS[at][0]:
                        diag = b0 + nb == t + 1
                        mm = pe.matmul(bank[:, col:col + nb * P], qt[nxt][h * ROWS:(h + 1) * ROWS, pair, t * P:(t + 1) * P],
                                       kt_[nxt][h * ROWS:(h + 1) * ROWS, pair, b0 * P:(b0 + nb) * P],
                                       start=col == 0, stop=not diag, skip_group_check=True)
                        col += nb * P
                        if diag:
                            mm = pe.matmul(bank[:, col - P:col], ident16[:, :], causal16[:, :],
                                           start=False, stop=True, skip_group_check=True)
                    mm.then_inc(s["fill_ready"], 1)
                elif e[0] == "shift":
                    pe.wait_ge(s["shift_ready"], (u + 1) * 2 + e[1] + 1)
                    pe.transpose(shared16[0:2 * CROWS * TPB, 0:P],
                                 shift16[:, e[1], :, :, :].rearrange("p h r t -> p (h r t)"),
                                 ident16[:, :]).then_inc(s["shared_full"], 1)
                elif e[0] == "scores":
                    k, pair = e[1:]
                    c, kt = STEPS[k]
                    if k == 0:
                        pe.wait_ge(rows_loaded[pair], (u + 1) * 32)
                    if k or not early(u):
                        pe.wait_ge(s["exp_done"], u * 2 * NS + 2 * (k - 1) + pair + 1)
                    for h in range(2):
                        mm = pe.matmul(p_score[pair][:, h, left(k):QC],
                                       kt_[par][h * ROWS:(h + 1) * ROWS, pair, kt * P:(kt + 1) * P],
                                       qt[par][h * ROWS:(h + 1) * ROWS, pair, c * QC + left(k):(c + 1) * QC],
                                       start=True, stop=k not in DIAG, skip_group_check=True)
                        if k in DIAG:
                            mm = pe.matmul(p_score[pair][:, h, left(k):left(k) + P], ident16[:, :], anticausal16[:, :],
                                           start=False, stop=True, skip_group_check=True)
                    mm.then_inc(s["scores_ready"], 1)
                elif e[0] == "pv":
                    k, unit = e[1], u - e[2]
                    c, kt = STEPS[k]
                    if k == 0:
                        pe.wait_ge(s["v_ready"], u + 1)
                    if kt == KEY_ORDER[c][0] and (c or not early(u)):
                        pe.wait_ge(s["out_taken"], unit * NQC + c)
                    pe.wait_ge(s["exp_done"], unit * 2 * NS + 2 * k + 2)
                    for h in range(GROUP):
                        mm = pe.matmul(p_out[32 * h:32 * h + 32, left(k):QC], vs[nxt if e[2] else par][:, kt, h, :],
                                       probs[k % 2][:, h, left(k):QC], start=kt == KEY_ORDER[c][0],
                                       stop=kt == KEY_ORDER[c][-1], skip_group_check=True)
                    mm.then_inc(s["pv_done"], 1)
                elif e[0] == "out":
                    pe.wait_ge(s["out_taken"], (u - e[2]) * NQC + e[1] + 1)
                    for t in range(QC // P):
                        mm = pe.transpose(p_shared[:, t * P:(t + 1) * P], ot[:, t * P:(t + 1) * P], ident[:, :])
                    mm.then_inc(s["shared_full"], 1)

        def scalar_slot(act, u, par, kind):
            ev, nxt = slot_events(kind), 1 - par
            for n, e in enumerate(ev):
                if e[0] == "turn" and e[1] % 2 == 0:
                    act.wait_ge(s["shared_full"], shared_place(ev, n, u) + 1)
                    act.copy(qt[nxt][:, e[1] // 2, :], shared16[:, 0:S]).then_inc(s["shared_used"], 1)
                elif e[0] == "shift":
                    act.wait_ge(s["shared_full"], shared_place(ev, n, u) + 1)
                    act.copy(rows16[e[1]][:, :], shared16[0:2 * CROWS * TPB, 0:P]).then_inc(s["shared_used"], 1)
                elif e[0] == "scores":
                    k, pair = e[1:]
                    c, kt = STEPS[k]
                    act.wait_ge(s["scores_ready"], u * 2 * NS + 2 * k + pair + 1)
                    if not early(u, k):
                        act.wait_ge(s["pv_done"], u * NS + (k - 1))
                    act.activation(probs[k % 2][:, 2 * pair:2 * pair + 2, left(k):QC],
                                   p_score[pair][:, :, left(k):QC], ACT.Exp,
                                   bias=abias[:, c * TPB + kt:c * TPB + kt + 1]).then_inc(s["exp_done"], 1)
                elif e[0] == "take":
                    act.wait_ge(s["pv_done"], (u - e[2]) * NS + (NS if e[1] else LAST0 + 1))
                    act.copy(ot[:, :], p_out[:, :]).then_inc(s["out_taken"], 1)

        def vector_slot(dve, u, par, kind):
            ev, nxt = slot_events(kind), 1 - par
            for n, e in enumerate(ev):
                if e[0] == "turn" and e[1] % 2:
                    dve.wait_ge(s["shared_full"], shared_place(ev, n, u) + 1)
                    dve.tensor_copy(kt_[nxt][:, e[1] // 2, :], shared16[:, 0:S]).then_inc(s["shared_used"], 1)
                elif e[0] == "fill":
                    pair, f = e[1:]
                    (_, first, step, count), h = FILLS[f // 2], 2 * pair + f % 2
                    dve.wait_ge(s["fill_ready"], (u + 1) * 2 * PAIR_FILLS + pair * PAIR_FILLS + f + 1)
                    if step == 1:
                        dst, src = block_max[:, h, first:first + count], p_fill[f % 2][:, :].rearrange("p (a c) -> p a c", c=P)
                    else:
                        dst = block_max[:, h, first:first + 2 * step].rearrange("p (a c) -> p a c", c=step)[:, :, 0:count]
                        src = p_fill[f % 2][:, :].rearrange("p (a b c) -> p a b c", a=2, c=P)
                    dve.tensor_reduce(dst, src, AX.X, ALU.max).then_inc(s["fill_used"], 1)
                elif e[0] == "max":
                    pair = e[1]
                    dve.wait_ge(s["fill_used"], (u + 1) * 2 * PAIR_FILLS + (pair + 1) * PAIR_FILLS)
                    dve.tensor_reduce(row_max[:, 2 * pair:2 * pair + 2, :].rearrange("p h (j e) -> p h e j", e=2),
                                      block_max[:, 2 * pair:2 * pair + 2, 0:64].rearrange(
                                          "p h (e j c) -> p h e j c", e=2, j=TPB // 2),
                                      AX.X, ALU.max).then_inc(s["max_ready"], 1)
                elif e[0] == "out":
                    dve.wait_ge(s["shared_full"], shared_place(ev, n, u) + 1)
                    view = p_shared[:, :].rearrange("p (t h r) -> p t h r", t=QC // P, h=GROUP)
                    dve.reciprocal(rden[:, :, :], view[:, :, :, HD]).then_inc(s["dve_chain"], 1)
                    unit = u - e[2]
                    dve.wait_ge(s["dve_chain"], unit * NQC + e[1] + 1)
                    dve.tensor_tensor(
                        attn[:, ds(unit, 1), 4 * e[1]:4 * e[1] + 4, :].rearrange("p u t (h r) -> p (u t) h r", r=HD),
                        view[:, :, :, 0:HD], rden[:, :, :].unsqueeze(3).to_broadcast([P, QC // P, GROUP, HD]),
                        ALU.mult).then_inc(s["shared_used"], 1)

        def build_stack(pool, u):
            for stack, parts, places in ((qstack, qparts, ((0, 0, 3, 1), (1, 3, 6, 2), (2, 4, 5, 1))),
                                         (kstack, kparts, ((0, 2, 5, 1), (1, 1, 6, 4), (2, 0, 1, 1)))):
                view = stack[:, :, :, 0:PRODUCTS * HD].rearrange("p t g (r c) -> p (t g) r c", c=HD)
                for part, lo, hi, step in places:
                    dst = view[:, :, lo:hi:step, :]
                    src = parts[:, part, ds(u, 1), :, :].rearrange("p u t (g c) -> p (u t g) c", c=HD)
                    last = pool.tensor_copy(dst, src.unsqueeze(2).to_broadcast(list(dst.shape)))
            last.then_inc(s["stack_ready"], 1)

        def pool_slot(pool, u, par, kind):
            ev, nxt = slot_events(kind), 1 - par
            maxima = "m" in kind
            if maxima:
                if "p" in kind:
                    pool.wait_ge(s["pv_done"], u * NS)
                pool.tensor_copy(vs[nxt][:, :, :, 0:HD],
                                 v[:, 0, ds(u + 1, 1), :, :].rearrange("p u t (g c) -> p (u t) g c", c=HD)
                                 ).then_inc(s["v_ready"], 1)
            more = maxima and not (isinstance(u, int) and u == UNITS - 2)
            for n, e in enumerate(ev):
                if e == ("turn", 3):
                    if more:
                        pool.wait_ge(s["shared_full"], shared_place(ev, ev.index(("turn", 3)), u) + 1)
                        build_stack(pool, u + 2)
                if e[0] == "max":
                    pair = e[1]
                    pool.wait_ge(s["max_ready"], (u + 1) * 2 + pair + 1)
                    base = [(u + 1) * 8 + 4 * pair]

                    def link(ins):
                        ins.then_inc(s["pool_chain"], 1)
                        base[0] = base[0] + 1
                        pool.wait_ge(s["pool_chain"], base[0])
                    cut = shift16[:, pair, :, :, :]
                    own, top = shift0[:, :].unsqueeze(1).to_broadcast([P, 2, TPB]), row_max[:, 2 * pair:2 * pair + 2, :]
                    link(pool.tensor_tensor(shift[:, pair, :, :], own, top, ALU.subtract))
                    link(pool.tensor_tensor(cut[:, :, 0, :], own, top, ALU.subtract))
                    link(pool.tensor_tensor(rest[:, pair, :, :], shift[:, pair, :, :], cut[:, :, 0, :], ALU.subtract))
                    link(pool.tensor_tensor(cut[:, :, 1, :], shift[:, pair, :, :], cut[:, :, 0, :], ALU.subtract))
                    pool.tensor_tensor(cut[:, :, 2, :], rest[:, pair, :, :], cut[:, :, 1, :], ALU.subtract
                                       ).then_inc(s["shift_ready"], 1)

        def sync_slot(sp, u, par, kind):
            ev, nxt = slot_events(kind), 1 - par
            for n, e in enumerate(ev):
                if e[0] == "shift":
                    sp.wait_ge(s["shared_used"], shared_place(ev, n, u) + 1)
                    for h in range(2):
                        at = h * ROWS + SHIFT_ROW
                        sp.dma_start(qt[nxt][at:at + CROWS, e[1], :],
                                     rows16[e[1]][h * CROWS * TPB:(h + 1) * CROWS * TPB, :]
                                     ).then_inc(rows_loaded[e[1]], 16)

        with nc.Block() as block:
            @block.vector
            def _(dve):
                dve.memset(block_max[:, :, :], NEG)
                for i in range(2):
                    dve.memset(vs[i][:, :, :, HD + 1:32], 0.0)
                    dve.memset(vs[i][:, :, :, HD:HD + 1], 1.0)

            @block.gpsimd
            def _(pool):
                done = 0
                for ins in (lambda: pool.memset(qstack[:, :, :, SHIFT_ROW:ROWS], 0.0),
                            lambda: pool.memset(qstack[:, :, :, ALIBI_ROW:ALIBI_ROW + 2], 1.0),
                            lambda: pool.memset(kstack[:, :, :, SHIFT_ROW:ROWS], 0.0),
                            lambda: pool.memset(kstack[:, :, :, SHIFT_ROW:SHIFT_ROW + 3], 1.0),
                            lambda: pool.memset(shift16[:, :, :, :, :], 0.0),
                            lambda: pool.tensor_copy(kstack[:, :, :, ALIBI_ROW:ALIBI_ROW + 2],
                                                     key_alibi[:, :, :].unsqueeze(2).to_broadcast([P, TPB, GROUP, 2]))):
                    ins().then_inc(s["preset"], 1)
                    done += 1
                    pool.wait_ge(s["preset"], done)
        with nc.Block() as block:
            @block.tensor
            def _(pe):
                slots(tensor_slot)(pe)

            @block.scalar
            def _(act):
                slots(scalar_slot)(act)

            @block.vector
            def _(dve):
                slots(vector_slot)(dve)

            @block.gpsimd
            def _(pool):
                build_stack(pool, 0)
                slots(pool_slot)(pool)

            @block.sync
            def _(sp):
                slots(sync_slot)(sp)


def project_attention(nc, attn, x, bias, ident, w):
    with ExitStack() as ctx:
        sb = lambda n, s, d=F32: ctx.enter_context(nc.sbuf_tensor("pa_" + n, s, d))
        ps = lambda n, s, d=F32: ctx.enter_context(nc.psum_tensor("pa_" + n, s, d))
        sem = lambda n: ctx.enter_context(nc.semaphore("pa_" + n))
        tile = [sb(f"tile{b}", [P, E]) for b in range(B)]
        turned = [sb(f"turned{b}", [P, EH, P]) for b in range(B)]
        p_turn = [ps(f"p_turn{b}", [P, 512]) for b in range(B)]
        p_proj = [ps(f"p_proj{b}", [P, 512]) for b in range(B)]
        tile_ready, turn_psum, turn_ready, proj_ready, proj_used, biased = (
            sem(n) for n in ("tile_ready", "turn_psum", "turn_ready", "proj_ready", "proj_used", "biased"))

        def x_tile(t, b):
            return x[:, ds(t + b * TPB, 1), :].rearrange("p a e -> p (a e)")

        with nc.Block() as block:
            @block.gpsimd
            def _(pool):
                pool.sem_inc(turn_psum, B)
                pool.sem_inc(proj_used, B)
                with pool.Fori(0, TPB) as t:
                    for b in range(B):
                        pool.wait_ge(turn_psum, t * B + b + 1)
                        pool.tensor_copy(tile[b][:, :].rearrange("p (g c) -> p g c", g=GPB),
                                         attn[:, b * GPB:(b + 1) * GPB, ds(t, 1), :].rearrange("p g t c -> p (g t) c")
                                         ).then_inc(tile_ready, 1)
                        pool.tensor_tensor(x_tile(t, b), x_tile(t, b), bias[:, :], ALU.add).then_inc(biased, 1)

            @block.tensor
            def _(pe):
                with pe.Fori(0, TPB) as t:
                    for b in range(B):
                        pe.wait_ge(tile_ready, t * B + b + 1)
                        for h in range(EH):
                            mm = pe.transpose(p_turn[b][:, h * P:(h + 1) * P], tile[b][:, h * P:(h + 1) * P], ident[:, :])
                        mm.then_inc(turn_psum, 1)
                    for b in range(B):
                        pe.wait_ge(turn_ready, t * B + b + 1)
                        pe.wait_ge(proj_used, t * B + b + 1)
                        for h in range(EH):
                            mm = pe.matmul(p_proj[b][:, 0:E], turned[b][:, h, :], w[:, h, :],
                                           start=h == 0, stop=h == EH - 1)
                        mm.then_inc(proj_ready, 1)

            @block.scalar
            def _(act):
                with act.Fori(0, TPB) as t:
                    for b in range(B):
                        act.wait_ge(turn_psum, t * B + b + 1 + B)
                        act.copy(turned[b][:, :, :], p_turn[b][:, 0:E].rearrange("p (h c) -> p h c", h=EH)
                                 ).then_inc(turn_ready, 1)

            @block.vector
            def _(dve):
                with dve.Fori(0, TPB) as t:
                    for b in range(B):
                        dve.wait_ge(proj_ready, t * B + b + 1)
                        dve.wait_ge(biased, t * B + b + 1)
                        dve.tensor_tensor(x_tile(t, b), p_proj[b][:, 0:E], x_tile(t, b), ALU.add
                                          ).then_inc(proj_used, 1)


def normalise_and_turn(nc, tag, x, mean, rstd, ident, xt):
    with ExitStack() as ctx:
        sb = lambda n, s, d=F32: ctx.enter_context(nc.sbuf_tensor(tag + n, s, d))
        ps = lambda n, s, d=F32: ctx.enter_context(nc.psum_tensor(tag + n, s, d))
        sem = lambda n: ctx.enter_context(nc.semaphore(tag + n))
        xn = [sb(f"xn{i}", [P, E]) for i in range(4)]
        p_turn = [ps(f"p_turn{i}", [P, 512]) for i in range(2)]
        xn_ready, turned, taken = sem("xn_ready"), sem("turned"), sem("taken")
        with nc.Block() as block:
            @block.vector
            def _(dve):
                dve.sem_inc(turned, 2)
                dve.sem_inc(taken, 2)
                with dve.Fori(0, TILES // 4) as r:
                    for i in range(4):
                        if i % 2 == 0:
                            dve.wait_ge(turned, r * 2 + i // 2 + 1)
                        dve.tensor_scalar(xn[i][:, :], x[:, ds(r * 4 + i, 1), :].rearrange("p a e -> p (a e)"),
                                          mean[:, ds(r * 4 + i, 1)], rstd[:, ds(r * 4 + i, 1)],
                                          ALU.subtract, ALU.mult).then_inc(xn_ready, 1)

            @block.tensor
            def _(pe):
                with pe.Fori(0, TILES // 4) as r:
                    for j in range(2):
                        pe.wait_ge(xn_ready, r * 4 + 2 * j + 2)
                        pe.wait_ge(taken, r * 2 + j + 1)
                        for i in range(2):
                            for h in range(EH):
                                mm = pe.transpose(p_turn[j][:, (h * 2 + i) * P:(h * 2 + i + 1) * P],
                                                  xn[2 * j + i][:, h * P:(h + 1) * P], ident[:, :])
                        mm.then_inc(turned, 1)

            @block.scalar
            def _(act):
                with act.Fori(0, TILES // 4) as r:
                    for j in range(2):
                        act.wait_ge(turned, r * 2 + j + 3)
                        act.copy(xt[:, :, ds(r, 1), 1 + 2 * j * P:1 + 2 * (j + 1) * P].rearrange("p h r c -> p (h r) c"),
                                 p_turn[j][:, :].rearrange("p (h c) -> p h c", h=EH)).then_inc(taken, 1)


EXPERTS, TOPK, HIDDEN, SHARED_HIDDEN = 8, 2, 176, 352
WIDTH = EXPERTS * HIDDEN + SHARED_HIDDEN
MT = -(-WIDTH // P)
TB = 512
NB = B * S // TB
SLICES = EXPERTS + 1


def router_phase(nc, xt, wr, ident, ident16, priority, gates_t):
    with ExitStack() as ctx:
        sb = lambda n, s, d=F32: ctx.enter_context(nc.sbuf_tensor("ro_" + n, s, d))
        ps = lambda n, s, d=F32: ctx.enter_context(nc.psum_tensor("ro_" + n, s, d))
        sem = lambda n: ctx.enter_context(nc.semaphore("ro_" + n))
        logits_t = sb("logits_t", [EXPERTS, NB, TB])
        T3 = [P, TILES, EXPERTS]
        work = {n: sb(n, T3) for n in "gate shifted pick1 pick2 left order kept rest".split()}
        row = {n: sb(n, [P, TILES]) for n in "top sum first top2 first2 total inv".split()}
        parts = sb("parts", [P, TILES, 3, SLICES], BF16)
        p_logits = ps("p_logits", [P, NB, TB])
        p_tok = ps("p_tok", [P, 512])
        p_gates = ps("p_gates", [P, 1024])
        chain_s, logits_ready, logits_in, tok_ready, shifted_ready, exp_ready, parts_ready, gates_ready = (
            sem(n) for n in "chain logits_ready logits_in tok_ready shifted_ready exp_ready parts_ready gates_ready".split())

        def rows(name):
            return row[name][:, :].unsqueeze(2).to_broadcast(T3)

        with nc.Block() as block:
            @block.tensor
            def _(pe):
                for n in range(NB):
                    for h in range(EH):
                        mm = pe.matmul(p_logits[0:EXPERTS, n, :], wr[:, h, :], xt[:, h, n, 1:],
                                       start=h == 0, stop=h == EH - 1)
                mm.then_inc(logits_ready, 1)
                pe.wait_ge(logits_in, 1)
                for t in range(TILES):
                    mm = pe.transpose(p_tok[:, t * EXPERTS:(t + 1) * EXPERTS],
                                      logits_t[:, t // 4, (t % 4) * P:(t % 4 + 1) * P], ident[0:EXPERTS, 0:EXPERTS])
                mm.then_inc(tok_ready, 1)
                pe.wait_ge(parts_ready, 1)
                for t in range(TILES):
                    mm = pe.transpose(p_gates[:, :].bitcast(BF16)[0:3 * SLICES, t * P:(t + 1) * P],
                                      parts[:, t, :, :].rearrange("p a b -> p (a b)"), ident16[:, :])
                mm.then_inc(gates_ready, 1)

            @block.scalar
            def _(act):
                act.wait_ge(logits_ready, 1)
                act.copy(logits_t[:, :, :], p_logits[0:EXPERTS, :, :]).then_inc(logits_in, 1)
                act.wait_ge(shifted_ready, 1)
                act.activation(work["gate"][:, :, :], work["shifted"][:, :, :], ACT.Exp).then_inc(exp_ready, 1)
                act.wait_ge(gates_ready, 1)
                act.copy(gates_t[:, :], p_gates[:, :].bitcast(BF16)[0:3 * SLICES, :])

            @block.vector
            def _(dve):
                c = Chain(dve, chain_s)
                w = {n: t[:, :, :] for n, t in work.items()}
                tok = p_tok[:, 0:TILES * EXPERTS].rearrange("p (t e) -> p t e", e=EXPERTS)
                order = priority[:, :].unsqueeze(1).to_broadcast(T3)

                def pick(values, top, first, out):
                    c.link(dve.tensor_reduce(row[top][:, :], values, AX.X, ALU.max))
                    c.link(dve.tensor_tensor(out, values, rows(top), ALU.is_equal))
                    c.link(dve.tensor_tensor(w["order"], out, order, ALU.mult))
                    c.link(dve.tensor_reduce(row[first][:, :], w["order"], AX.X, ALU.max))
                    c.link(dve.tensor_tensor(out, w["order"], rows(first), ALU.is_equal))

                c.link(dve.memset(parts[:, :, :, :], 0.0))
                c.link(dve.memset(parts[:, :, 0, EXPERTS:SLICES], 1.0))
                dve.wait_ge(tok_ready, 1)
                c.link(dve.tensor_reduce(row["top"][:, :], tok, AX.X, ALU.max))
                dve.tensor_tensor(w["shifted"], tok, rows("top"), ALU.subtract).then_inc(shifted_ready, 1)
                dve.wait_ge(exp_ready, 1)
                c.link(dve.tensor_reduce(row["sum"][:, :], w["gate"], AX.X, ALU.add))
                c.link(dve.reciprocal(row["inv"][:, :], row["sum"][:, :]))
                c.link(dve.tensor_tensor(w["gate"], w["gate"], rows("inv"), ALU.mult))
                pick(w["gate"], "top", "first", w["pick1"])
                c.link(dve.scalar_tensor_tensor(w["left"], w["pick1"], -2.0, w["gate"], ALU.mult, ALU.add))
                pick(w["left"], "top2", "first2", w["pick2"])
                c.link(dve.tensor_tensor(w["pick1"], w["pick1"], w["pick2"], ALU.add))
                c.link(dve.tensor_tensor(w["kept"], w["gate"], w["pick1"], ALU.mult))
                c.link(dve.tensor_reduce(row["total"][:, :], w["kept"], AX.X, ALU.add))
                c.link(dve.tensor_scalar(row["total"][:, :], row["total"][:, :], 1e-20, None, ALU.add))
                c.link(dve.reciprocal(row["inv"][:, :], row["total"][:, :]))
                c.link(dve.tensor_tensor(w["kept"], w["kept"], rows("inv"), ALU.mult))
                c.link(dve.tensor_copy(parts[:, :, 0, 0:EXPERTS], w["kept"]))
                c.link(dve.tensor_tensor(w["rest"], w["kept"], parts[:, :, 0, 0:EXPERTS], ALU.subtract))
                c.link(dve.tensor_copy(parts[:, :, 1, 0:EXPERTS], w["rest"]))
                dve.tensor_tensor(parts[:, :, 2, 0:EXPERTS], w["rest"], parts[:, :, 1, 0:EXPERTS],
                                  ALU.subtract).then_inc(parts_ready, 1)


def moe_phase(nc, x, xt, gates_t, select, w_gate, w_up, w_down):
    with ExitStack() as ctx:
        sb = lambda n, s, d=F32: ctx.enter_context(nc.sbuf_tensor("moe_" + n, s, d))
        ps = lambda n, s, d=F32: ctx.enter_context(nc.psum_tensor("moe_" + n, s, d))
        sem = lambda n: ctx.enter_context(nc.semaphore("moe_" + n))
        act_out = [sb(f"act{i}", [P, TB]) for i in range(2)]
        prod = [sb(f"prod{i}", [P, TB]) for i in range(2)]
        hidden = [sb(f"hidden{i}", [P, TB]) for i in range(2)]
        p_gate, p_up, p_sel = ([ps(f"{n}{i}", [P, TB]) for i in range(2)] for n in ("p_gate", "p_up", "p_sel"))
        p_down = ps("p_down", [P, TB // P, E])
        gate_ready, up_ready, sel_ready, act_ready, prod_ready, hidden_ready, down_ready, down_used = (
            sem(n) for n in "gate_ready up_ready sel_ready act_ready prod_ready hidden_ready down_ready down_used".split())

        def rows(m):
            return min(P, WIDTH - m * P)

        with nc.Block() as block:
            @block.tensor
            def _(pe):
                with pe.Fori(0, NB) as n:
                    def down(m):
                        pe.wait_ge(hidden_ready, n * MT + m + 1)
                        if m == 0:
                            pe.wait_ge(down_used, n + 1)
                        for t in range(TB // P):
                            mm = pe.matmul(p_down[:, t, :], hidden[m % 2][0:rows(m), t * P:(t + 1) * P],
                                           w_down[0:rows(m), m, :], start=m == 0 and t % 2 == 0,
                                           stop=m == MT - 1, skip_group_check=True)
                        mm.then_inc(down_ready, 1)

                    for m in range(MT):
                        k, i = rows(m), m % 2
                        cols = slice(m * P, m * P + k)
                        if m >= 2:
                            pe.wait_ge(hidden_ready, n * MT + m - 1)
                        for bank, w, ready in ((p_gate, w_gate, gate_ready), (p_up, w_up, up_ready)):
                            for h in range(EH):
                                mm = pe.matmul(bank[i][0:k, :], w[:, h, cols],
                                               xt[:, h, ds(n, 1), 1:].rearrange("p n c -> p (n c)"),
                                               start=h == 0, stop=h == EH - 1)
                            mm.then_inc(ready, 1)
                        pe.matmul(p_sel[i][0:k, :], select[:, cols], gates_t[:, ds(n * TB, TB)],
                                  start=True, stop=True).then_inc(sel_ready, 1)
                        if m >= 1:
                            down(m - 1)
                    down(MT - 1)

            @block.scalar
            def _(act):
                with act.Fori(0, NB) as n:
                    for m in range(MT):
                        k, i = rows(m), m % 2
                        act.wait_ge(gate_ready, n * MT + m + 1)
                        if m >= 2:
                            act.wait_ge(prod_ready, n * MT + m - 1)
                        act.activation(act_out[i][0:k, :], p_gate[i][0:k, :], ACT.Silu).then_inc(act_ready, 1)

            @block.vector
            def _(dve):
                dve.sem_inc(down_used, 1)
                with dve.Fori(0, NB) as n:
                    for m in range(MT):
                        k, i = rows(m), m % 2
                        dve.wait_ge(up_ready, n * MT + m + 1)
                        dve.wait_ge(act_ready, n * MT + m + 1)
                        dve.tensor_tensor(prod[i][0:k, :], p_up[i][0:k, :], act_out[i][0:k, :],
                                          ALU.mult).then_inc(prod_ready, 1)
                        dve.wait_ge(prod_ready, n * MT + m + 1)
                        dve.wait_ge(sel_ready, n * MT + m + 1)
                        if m >= 2:
                            dve.wait_ge(down_ready, n * MT + m - 1)
                        dve.tensor_tensor(hidden[i][0:k, :], p_sel[i][0:k, :], prod[i][0:k, :],
                                          ALU.mult).then_inc(hidden_ready, 1)
                    dve.wait_ge(down_ready, n * MT + MT)
                    tiles = x[:, ds(n * 4, 4), :]
                    dve.tensor_tensor(tiles, p_down[:, :, :], tiles, ALU.add).then_inc(down_used, 1)


RH, RN = 4, 64
L = 64
KAPPA = float(np.exp(-0.5))
CPB = TB // L
VECTORS = "x_w x_a x_g x_r x_v x_k w0 a0 k_k k_a r_k gn_scale gn_offset".split()
VEC = {n: i for i, n in enumerate(VECTORS + ["keep_a"])}
MIXES = "w a g r v k".split()


def time_mix_phase(nc, xt, vec, weights, head_spread, head_columns, head_ones, chunk_carry, out):
    with ExitStack() as ctx:
        sb = lambda n, s, d=F32: ctx.enter_context(nc.sbuf_tensor("tm_" + n, s, d))
        ps = lambda n, s, d=F32: ctx.enter_context(nc.psum_tensor("tm_" + n, s, d))
        sem = lambda n: ctx.enter_context(nc.semaphore("tm_" + n))
        HT = [P, EH, TB]
        QT = TB // 2
        xx = sb("xx", HT)
        xm = [sb(f"xm{i}", HT) for i in range(2)]
        low_w, low_a, low_g = sb("low_w", [64, TB]), sb("low_a", [64, TB]), sb("low_g", [P, TB])
        cum, kn, sq, up, coef = (sb(n, HT) for n in ("cum", "kn", "sq", "up", "coef"))
        norm = sb("norm", [P, QT])
        down = sb("down", [P, EH, CPB, L + 1])
        p_low = [ps(f"p_low{i}", [P, TB]) for i in range(2)]
        p_full = [ps(f"p_full{i}", HT) for i in range(2)]
        p_sum = ps("p_sum", HT)
        s = {n: sem(n) for n in ("chain mix_ready mix_used low_ready full_ready full_used cum_ready sq_ready "
                                 "small_ready clamp_ready root_ready inv_ready spread_ready spread_used rk_ready "
                                 "bonus_ready bonus_used exp_ready bt_ready at_done scaled").split()}
        full = lambda t: t[:, :, :]
        blk = lambda name, n: out[name][:, :, ds(n, 1), :].rearrange("p h n c -> p (h n) c")
        chunks = lambda t: t.rearrange("p h (c l) -> p h c l", l=L)

        def v_(name, h):
            return vec[:, h, VEC[name]:VEC[name] + 1]

        def half_of(name, h, n):
            return out[name][:, h, ds(n, 1), :].rearrange("p n c -> p (n c)")

        def rounds(step):
            def program(eng):
                step(eng, 0, None)
                with eng.Fori(0, NB - 1) as n:
                    step(eng, n + 1, n)
                step(eng, None, NB - 1)
            return program

        with nc.Block() as block:
            @block.vector
            def _(dve):
                c = Chain(dve, s["chain"])
                for name, count in (("mix_used", 2), ("full_used", 2), ("bonus_used", 1), ("bonus_ready", 1),
                                    ("exp_ready", 2), ("at_done", 1), ("scaled", 1)):
                    dve.sem_inc(s[name], count)
                c.link(dve.memset(down[:, :, :, 0:1], 1.0))
                c.link(dve.memset(xt[:, :, :, 0:1], 0.0))
                c.link(dve.tensor_copy(xt[:, :, 1::2, 0], xt[:, :, 0::2, TB]))
                c.link(dve.tensor_scalar(vec[:, :, VEC["keep_a"]:VEC["keep_a"] + 1], vec[:, :, VEC["k_a"]:VEC["k_a"] + 1],
                                         -1.0, 1.0, ALU.mult, ALU.add))

                def step(front, back):
                    m, n = front, back

                    def mix(i):
                        if m is None:
                            return
                        dve.wait_ge(s["mix_used"], m * 6 + i + 1)
                        for h in range(EH):
                            ins = dve.scalar_tensor_tensor(
                                xm[i % 2][:, h, :], xx[:, h, :], v_("x_" + MIXES[i], h),
                                xt[:, h, ds(m, 1), 1:].rearrange("p n c -> p (n c)"), ALU.mult, ALU.add)
                            if h == 0:
                                c.mark(ins)
                        ins.then_inc(s["mix_ready"], 1)

                    if m is not None:
                        if n is not None:
                            dve.wait_ge(s["mix_ready"], m * 6)
                        c.wait()
                        difference = c.mark(dve.tensor_tensor(
                            full(xx), xt[:, :, ds(m, 1), 0:TB].rearrange("p h n c -> p (h n) c"),
                            xt[:, :, ds(m, 1), 1:].rearrange("p h n c -> p (h n) c"), ALU.subtract))
                    if n is not None:
                        dve.wait_ge(s["exp_ready"], n * 2 + 2)
                        dve.wait_ge(s["full_used"], n * 6 + 3)
                        for h in range(EH):
                            ins = dve.tensor_tensor_scan(cum[:, h, :], chunk_carry[:, :], half_of("bonus", h, n), 0.0,
                                                         ALU.mult, ALU.add)
                            if h == 0:
                                c.mark(ins)
                        ins.then_inc(s["cum_ready"], 1)
                    if m is not None:
                        c.wait(difference)
                    mix(0)
                    mix(1)
                    if n is not None:
                        dve.wait_ge(s["bonus_ready"], n + 1)
                        dve.wait_ge(s["full_used"], n * 6 + 4)
                        for h in range(EH):
                            c.mark(dve.tensor_scalar(coef[:, h, :], half_of("bt", h, n), v_("k_a", h), v_("keep_a", h),
                                                     ALU.mult, ALU.add))
                        dve.wait_ge(s["full_used"], n * 6 + 8)
                        for h in range(EH):
                            c.mark(dve.tensor_scalar(kn[:, h, :], half_of("kt", h, n), v_("k_k", h), None, ALU.mult))
                        c.wait()
                        dve.tensor_tensor(full(sq), full(kn), full(kn), ALU.mult).then_inc(s["sq_ready"], 1)
                        c.mark(dve.tensor_tensor(blk("kt", n), full(coef), blk("kt", n), ALU.mult))
                    mix(2)
                    if n is not None:
                        c.wait()
                        for h in range(EH):
                            ins = dve.scalar_tensor_tensor(coef[:, h, :], half_of("rt", h, n), v_("r_k", h),
                                                           half_of("kt", h, n), ALU.mult, ALU.mult)
                            if h == 0:
                                c.mark(ins)
                        ins.then_inc(s["rk_ready"], 1)
                    mix(3)
                    if n is not None:
                        dve.wait_ge(s["small_ready"], n + 1)
                        dve.tensor_scalar(norm[:, :], p_sum[:, 0, 0:QT], 1e-24, None, ALU.max).then_inc(s["clamp_ready"], 1)
                    mix(4)
                    if n is not None:
                        dve.wait_ge(s["root_ready"], n + 1)
                        dve.reciprocal(norm[:, :], norm[:, :]).then_inc(s["inv_ready"], 1)
                    mix(5)
                    if n is not None:
                        dve.wait_ge(s["spread_ready"], n + 1)
                        dve.tensor_tensor(full(kn), full(kn), full(p_sum), ALU.mult).then_inc(s["spread_used"], 1)
                        dve.wait_ge(s["spread_used"], n + 1)
                        dve.tensor_tensor(blk("bt", n), full(kn), blk("bt", n), ALU.mult).then_inc(s["bt_ready"], 1)
                        dve.wait_ge(s["exp_ready"], n * 2 + 4)
                        for h in range(EH):
                            c.mark(dve.scalar_tensor_tensor(
                                out["at"][:, h, ds(n, 1), :].rearrange("p n (c l) -> p (n c) l", l=L),
                                kn[:, h, :].rearrange("p (c l) -> p c l", l=L), -1.0, down[:, h, :, 0:L],
                                ALU.mult, ALU.mult))
                        c.mark(dve.tensor_copy(out["chunk_decay"][:, :, ds(n, 1), :].rearrange("p h n c -> p (h n) c"),
                                               down[:, :, :, L]))
                        c.wait()
                        dve.sem_inc(s["at_done"], 1)
                        dve.wait_ge(s["bonus_ready"], n + 2)
                        dve.tensor_tensor(blk("bonus", n), full(p_sum), blk("vt", n), ALU.mult).then_inc(s["bonus_used"], 1)

                step(0, None)
                with dve.Fori(0, NB - 1) as n:
                    c.loop(n, 7 + 10)
                    step(n + 1, n)
                c.end(NB - 1)
                step(None, NB - 1)

            @block.gpsimd
            def _(pool):
                with pool.Fori(0, NB) as n:
                    pool.wait_ge(s["exp_ready"], n * 2 + 4)
                    pool.wait_ge(s["rk_ready"], n + 1)
                    pool.tensor_tensor(chunks(blk("rt", n)), chunks(blk("rt", n)), down[:, :, :, 1:], ALU.mult)
                    pool.tensor_tensor(blk("kt", n), blk("kt", n), full(up), ALU.mult)
                    pool.wait_ge(s["bt_ready"], n + 1)
                    pool.tensor_tensor(blk("bt", n), blk("bt", n), full(up), ALU.mult).then_inc(s["scaled"], 1)

            def tensor_step(pe, m, n):
                def first(i):
                    if m is None:
                        return
                    name = MIXES[i]
                    pe.wait_ge(s["mix_ready"], m * 6 + i + 1)
                    if i < 3:
                        rows = {"w": 64, "a": 64, "g": P}[name]
                        for h in range(EH):
                            mm = pe.matmul(p_low[i % 2][0:rows, :], weights[name + "1"][:, h, :], xm[i % 2][:, h, :],
                                           start=h == 0, stop=h == EH - 1)
                    else:
                        pe.wait_ge(s["full_used"], m * 6 + i + 1)
                        for o in range(EH):
                            for h in range(EH):
                                mm = pe.matmul(p_full[i % 2][:, o, :], weights[name][:, h, o * P:(o + 1) * P],
                                               xm[i % 2][:, h, :], start=h == 0, stop=h == EH - 1)
                    mm.then_inc(s["mix_used"], 1)

                def second(i):
                    if m is None:
                        return
                    pe.wait_ge(s["low_ready"], m * 3 + i + 1)
                    pe.wait_ge(s["full_used"], m * 6 + i + 1)
                    low, w = ((low_w, weights["w2"]), (low_a, weights["a2"]), (low_g, weights["g2"]))[i]
                    for o in range(EH):
                        mm = pe.matmul(p_full[i % 2][:, o, :], w[:, o * P:(o + 1) * P], low[:, :], start=True, stop=True)
                    mm.then_inc(s["full_ready"], 1)

                first(0)
                first(1)
                if n is not None:
                    pe.wait_ge(s["sq_ready"], n + 1)
                    pe.wait_ge(s["bonus_used"], n + 1)
                    for h in range(EH):
                        for j in range(2):
                            g = 32 * (2 * h + j)
                            mm = pe.matmul(p_sum[g:g + 32, 0, 0:QT], head_columns[:, :], sq[:, h, j * QT:(j + 1) * QT],
                                           start=True, stop=True, skip_group_check=True)
                    mm.then_inc(s["small_ready"], 1)
                second(0)
                first(2)
                second(1)
                second(2)
                if n is not None:
                    pe.wait_ge(s["inv_ready"], n + 1)
                    for h in range(EH):
                        for j in range(2):
                            mm = pe.matmul(p_sum[:, h, j * QT:(j + 1) * QT], head_spread[:, 2 * h + j, :], norm[:, :],
                                           start=True, stop=True, skip_group_check=True)
                    mm.then_inc(s["spread_ready"], 1)
                first(3)
                if n is not None:
                    pe.wait_ge(s["spread_used"], n + 1)
                    pe.wait_ge(s["rk_ready"], n + 1)
                    for o in range(EH):
                        mm = pe.matmul(p_sum[:, o, :], head_ones[:, :], coef[:, o, :], start=True, stop=True)
                    mm.then_inc(s["bonus_ready"], 1)
                first(4)
                first(5)

            @block.tensor
            def _(pe):
                rounds(tensor_step)(pe)

            def scalar_step(act, m, n):
                def low(i, dst, func):
                    act.wait_ge(s["mix_used"], m * 6 + i + 3)
                    src = p_low[i % 2][0:dst.shape[0], :]
                    ins = act.copy(dst[:, :], src) if func is None else act.activation(dst[:, :], src, func)
                    ins.then_inc(s["low_ready"], 1)

                def take(i, dst, bias=None):
                    if i < 3:
                        act.wait_ge(s["full_ready"], m * 3 + i + 1)
                    else:
                        act.wait_ge(s["mix_used"], m * 6 + i + 3)
                    if bias is None:
                        act.copy(blk(dst, m), p_full[i % 2][:, :, :]).then_inc(s["full_used"], 1)
                    else:
                        act.activation(half_of(dst, 0, m), p_full[i % 2][:, 0, :], ACT.Sigmoid, bias=v_(bias, 0))
                        act.activation(half_of(dst, 1, m), p_full[i % 2][:, 1, :], ACT.Sigmoid, bias=v_(bias, 1)
                                       ).then_inc(s["full_used"], 1)

                if n is not None:
                    act.wait_ge(s["cum_ready"], n + 1)
                    act.wait_ge(s["at_done"], n + 1)
                    act.wait_ge(s["scaled"], n + 1)
                    for h in range(EH):
                        ins = act.activation(down[:, h, :, 1:], cum[:, h, :].rearrange("p (c l) -> p c l", l=L),
                                             ACT.Exp, scale=-KAPPA)
                    ins.then_inc(s["exp_ready"], 1)
                    act.activation(full(up), full(cum), ACT.Exp, scale=KAPPA).then_inc(s["exp_ready"], 1)
                if m is not None:
                    low(0, low_w, ACT.Tanh)
                    low(1, low_a, None)
                    take(0, "bonus", "w0")
                    low(2, low_g, ACT.Sigmoid)
                    take(1, "bt", "a0")
                if n is not None:
                    act.wait_ge(s["clamp_ready"], n + 1)
                    act.activation(norm[:, :], norm[:, :], ACT.Sqrt).then_inc(s["root_ready"], 1)
                if m is not None:
                    take(2, "gt")
                    take(3, "rt")
                    take(4, "vt")
                    take(5, "kt")

            @block.scalar
            def _(act):
                rounds(scalar_step)(act)


LEVELS = [1 << i for i in range(L.bit_length() - 1)]
HALF_CHUNKS = P // L


def marks_of(*names):
    return {n: i + 1 for i, n in enumerate(names)} | {"each": len(names)}


INNER = [m for m in LEVELS if m > 1]
PE_MARKS = marks_of("turn", "a1", "a2", "a3", "w0", *[f"{k}{m}" for m in INNER for k in ("z", "xz", "zy")
                                                      if not (k == "xz" and m == INNER[-1])],
                    "ta", "r", "yv", "gh0", "gh1", "ys0", "hop0", "ys1", "hop1")
DVE_MARKS = marks_of("a1e", "a1o", "a2e", "a2o", "x1e", "x1o", "x1", "y1m", "y1",
                     *[f"{k}{m}" for m in INNER for k in ("z", "x", "y") if not (k == "x" and m == INNER[-1])],
                     "r", "gh0", "g0", "gh1", "g1", "st0a", "st0", "st1a", "st1")
ACT_MARKS = marks_of("tok", "w0", "ta", "y")


def recurrence_phase(nc, data, ident, masks, level_masks, level1_t, head_ones, yt):
    with ExitStack() as ctx:
        sb = lambda n, s, d=F32: [ctx.enter_context(nc.sbuf_tensor(f"rc_{n}{b}", s, d)) for b in range(B)]
        sem = lambda n: [ctx.enter_context(nc.semaphore(f"rc_{n}{b}")) for b in range(B)]
        bank = [[ctx.enter_context(nc.psum_tensor(f"rc_bank{b}_{i}", [P, 512], F32)) for i in range(4)] for b in range(B)]
        bt, kt, vt = sb("bt", [P, EH, P]), sb("kt", [P, EH, P]), sb("vt", [P, EH, P])
        ar = sb("ar", [P, EH, 2 * P])
        tok_b, tok_k, tok_v = sb("tok_b", [P, E]), sb("tok_k", [P, E]), sb("tok_v", [P, E])
        aw = sb("aw", [P, RH, 2 * RN])
        ab = sb("ab", [P, 2, EH, 2, P])
        ak = sb("ak", [P, 2, EH, 2, P])
        X, Y, Z = sb("X", [P, RH, P]), sb("Y", [P, RH, P]), sb("Z", [P, RH, P])
        ta = sb("ta", [P, EH, 2, P])
        rh = sb("rh", [P, EH, P])
        gh = [sb(f"gh{c}_", [P, EH, 2, P]) for c in range(2)]
        state = [sb(f"state{c}_", [P, EH, P]) for c in range(2)]
        made, dve_did, act_did, staged = sem("made"), sem("dve_did"), sem("act_did"), sem("staged")

        def flat(t):
            return t[:, :, :, :].rearrange("p h n c -> p h (n c)")

        def src(name, t, b):
            return flat(data[name])[:, :, ds(t * P + b * S, P)]

        def pe_wait(pe, t, b, dve=None, act=None):
            if dve:
                pe.wait_ge(dve_did[b], t * DVE_MARKS["each"] + DVE_MARKS[dve])
            if act:
                pe.wait_ge(act_did[b], t * ACT_MARKS["each"] + ACT_MARKS[act])

        def heads():
            return [(h, h // 2, h % 2) for h in range(RH)]

        def head_rows(par):
            return slice(par * RN, par * RN + RN)

        with nc.Block() as block:
            @block.tensor
            def _(pe):
                def turn(t, b):
                    pe.wait_ge(staged[b], t + 1)
                    for n, (a, c) in enumerate(((bt, kt), (ar, vt))):
                        for h in range(EH):
                            pe.transpose(bank[b][n][:, h * P:(h + 1) * P], a[b][:, h, 0:P], ident[:, :])
                            mm = pe.transpose(bank[b][n][:, (2 + h) * P:(3 + h) * P], c[b][:, h, :], ident[:, :])
                    mm.then_inc(made[b], 1)

                def against(rows_of, banks, width, rhs):
                    def stage(t, b):
                        for h, half, par in heads():
                            r = head_rows(par)
                            mm = pe.matmul(bank[b][banks[par]][:, half * width:(half + 1) * width],
                                           rows_of[b][r, half, 0:P], rhs[b][r, half, 0:width],
                                           start=True, stop=True, skip_group_check=True)
                        mm.then_inc(made[b], 1)
                    return stage

                def a1(t, b):
                    against(bt, (2, 3), 2 * P, ar)(t, b)

                def a2(t, b):
                    pe_wait(pe, t, b, act="tok")
                    against(kt, (0, 1), 2 * P, ar)(t, b)

                def a3(t, b):
                    pe_wait(pe, t, b, dve="a1o")
                    against(ar, (2, 3), P, bt)(t, b)

                def per_head(n, lhs, rhs, width=P):
                    def stage(t, b):
                        for h, half, par in heads():
                            mm = pe.matmul(bank[b][n][:, h * width:(h + 1) * width], lhs(b, h, half, par),
                                           rhs(b, h, half, par), start=True, stop=True)
                        mm.then_inc(made[b], 1)
                    return stage

                def w0(t, b):
                    pe_wait(pe, t, b, dve="a2o")
                    per_head(0, lambda b, h, half, par: ak[b][:, par, half, 0, :],
                             lambda b, h, half, par: tok_v[b][:, h * RN:(h + 1) * RN], RN)(t, b)

                def z(m):
                    def stage(t, b):
                        pe_wait(pe, t, b, dve="x1" if m == 2 else f"x{m // 2}")
                        per_head(1, lambda b, h, half, par: ab[b][:, par, half, 0, :],
                                 lambda b, h, half, par: X[b][:, h, :])(t, b)
                    return stage

                def xz(m):
                    def stage(t, b):
                        pe_wait(pe, t, b, dve=f"z{m}")
                        per_head(2, lambda b, h, half, par: Y[b][:, h, :], lambda b, h, half, par: Z[b][:, h, :])(t, b)
                    return stage

                def zy(m):
                    def stage(t, b):
                        pe_wait(pe, t, b, dve=f"z{m}")
                        per_head(3, lambda b, h, half, par: Z[b][:, h, :], lambda b, h, half, par: Y[b][:, h, :])(t, b)
                    return stage

                def ta_(t, b):
                    pe_wait(pe, t, b, dve=f"y{INNER[-1]}", act="w0")
                    per_head(0, lambda b, h, half, par: Y[b][:, h, :], lambda b, h, half, par: aw[b][:, h, :])(t, b)

                def r_(t, b):
                    pe_wait(pe, t, b, act="ta")
                    for h, half, par in heads():
                        mm = pe.matmul(bank[b][1][head_rows(par), half * P:(half + 1) * P],
                                       ta[b][:, half, 0, head_rows(par)], ab[b][:, par, half, 1, :],
                                       start=half == 0, stop=True, skip_group_check=True)
                    mm.then_inc(made[b], 1)

                def yv(t, b):
                    for h, half, par in heads():
                        out = bank[b][2][head_rows(par), half * P:(half + 1) * P]
                        pe.matmul(out, ta[b][:, half, 1, head_rows(par)], ab[b][:, par, half, 1, :],
                                  start=half == 0, stop=False, skip_group_check=True)
                        mm = pe.matmul(out, tok_v[b][:, h * RN:(h + 1) * RN], ak[b][:, par, half, 1, :],
                                       start=False, stop=True, skip_group_check=True)
                    mm.then_inc(made[b], 1)

                def gh_(c):
                    def stage(t, b):
                        dst, rows = bank[b][(3, 0)[c]], slice(c * L, (c + 1) * L)
                        for half in range(EH):
                            cols = slice(half * P, (half + 1) * P)
                            at = half * 2 * P
                            pe.matmul(dst[:, at:at + P], ta[b][rows, half, 0, :], tok_b[b][rows, cols],
                                      start=True, stop=True)
                            pe.matmul(dst[:, at + P:at + 2 * P], tok_b[b][rows, cols], ta[b][rows, half, 1, :],
                                      start=True, stop=False)
                            mm = pe.matmul(dst[:, at + P:at + 2 * P], tok_k[b][rows, cols], tok_v[b][rows, cols],
                                           start=False, stop=True)
                        mm.then_inc(made[b], 1)
                    return stage

                def ys(c):
                    def stage(t, b):
                        if c == 0:
                            pe.wait_ge(dve_did[b], t * DVE_MARKS["each"] + DVE_MARKS["r"])
                        else:
                            pe_wait(pe, t, b, dve="st0")
                        for half in range(EH):
                            mm = pe.matmul(bank[b][2][:, half * P + c * L:half * P + (c + 1) * L],
                                           state[c][b][:, half, :], rh[b][:, half, c * L:(c + 1) * L],
                                           start=False, stop=True, skip_group_check=True)
                        mm.then_inc(made[b], 1)
                    return stage

                def hop(c):
                    def stage(t, b):
                        pe_wait(pe, t, b, dve=f"g{c}")
                        for half in range(EH):
                            mm = pe.matmul(bank[b][1][:, half * P:(half + 1) * P], gh[c][b][:, half, 0, :],
                                           state[c][b][:, half, :], start=True, stop=True)
                        mm.then_inc(made[b], 1)
                    return stage

                stages = [turn, a1, a2, a3, w0]
                for m in INNER:
                    stages += [z(m), zy(m)] if m == INNER[-1] else [z(m), xz(m), zy(m)]
                def settle(t, b):
                    pe_wait(pe, t, b, dve="st1", act="y")

                stages += [ta_, r_, yv, gh_(0), gh_(1), ys(0), hop(0), ys(1), hop(1), settle]
                with pe.Fori(0, TPB) as t:
                    for stage in stages:
                        for b in range(B):
                            stage(t, b)

            @block.vector
            def _(dve):
                def did(b, ins):
                    ins.then_inc(dve_did[b], 1)

                def own(t, b, name):
                    dve.wait_ge(dve_did[b], t * DVE_MARKS["each"] + DVE_MARKS[name])

                def need(t, b, name):
                    dve.wait_ge(made[b], t * PE_MARKS["each"] + PE_MARKS[name])

                def masked(stage_name, dst, banks):
                    def stage(t, b):
                        need(t, b, stage_name)
                        for par in range(2):
                            did(b, dve.tensor_tensor(
                                dst[b][:, par, :, :, :].rearrange("p h k c -> p h (k c)"),
                                bank[b][banks[par]][:, :].rearrange("p (h c) -> p h c", h=EH),
                                masks[:, :].unsqueeze(1).to_broadcast([P, EH, 2 * P]), ALU.mult))
                    return stage

                eye = ident[:, :].unsqueeze(1).to_broadcast([P, RH, P])

                def x1(t, b):
                    need(t, b, "a3")
                    for par in range(2):
                        did(b, dve.tensor_tensor(
                            X[b][:, par::2, :], bank[b][2 + par][:, 0:2 * P].rearrange("p (h c) -> p h c", h=EH),
                            level_masks[:, 0, :].unsqueeze(1).to_broadcast([P, EH, P]), ALU.mult))
                    own(t, b, "x1o")
                    did(b, dve.tensor_tensor(X[b][:, :, :], X[b][:, :, :], eye, ALU.add))

                def y1(t, b):
                    did(b, dve.tensor_tensor(
                        Y[b][:, :, :].rearrange("p (h q) c -> p q h c", q=2), ab[b][:, :, :, 0, :],
                        level1_t[:, :].unsqueeze(1).unsqueeze(1).to_broadcast([P, 2, EH, P]), ALU.mult))
                    own(t, b, "y1m")
                    did(b, dve.tensor_tensor(Y[b][:, :, :], Y[b][:, :, :], eye, ALU.add))

                def z(m):
                    def stage(t, b):
                        need(t, b, f"z{m}")
                        did(b, dve.tensor_tensor(
                            Z[b][:, :, :], bank[b][1][:, :].rearrange("p (h c) -> p h c", h=RH),
                            level_masks[:, LEVELS.index(m), :].unsqueeze(1).to_broadcast([P, RH, P]), ALU.mult))
                    return stage

                def grow(kind, buf, n, m):
                    def stage(t, b):
                        need(t, b, {"x": "xz", "y": "zy"}[kind] + str(m))
                        did(b, dve.tensor_tensor(buf[b][:, :, :], bank[b][n][:, :].rearrange("p (h c) -> p h c", h=RH),
                                                 buf[b][:, :, :], ALU.add))
                    return stage

                def r_(t, b):
                    need(t, b, "r")
                    did(b, dve.tensor_tensor(rh[b][:, :, :], bank[b][1][:, 0:2 * P].rearrange("p (h c) -> p h c", h=EH),
                                             src("rt", t, b), ALU.add))

                def gh_(c):
                    def stage(t, b):
                        need(t, b, f"gh{c}")
                        did(b, dve.tensor_tensor(
                            gh[c][b][:, :, :, :].rearrange("p h k c -> p (h k) c"),
                            bank[b][(3, 0)[c]][:, :].rearrange("p (h c) -> p h c", c=P),
                            head_ones[:, :].unsqueeze(1).to_broadcast([P, 2 * EH, P]), ALU.mult))
                        own(t, b, f"gh{c}")
                        did(b, dve.tensor_tensor(gh[c][b][:, :, 0, :], gh[c][b][:, :, 0, :],
                                                 ident[:, :].unsqueeze(1).to_broadcast([P, EH, P]), ALU.add))
                    return stage

                def advance(c):
                    def stage(t, b):
                        need(t, b, f"hop{c}")
                        dst = state[1 - c][b]
                        did(b, dve.tensor_tensor(dst[:, :, :], bank[b][1][:, 0:2 * P].rearrange("p (h c) -> p h c", h=EH),
                                                 gh[c][b][:, :, 1, :], ALU.add))
                        own(t, b, f"st{c}a")
                        decay = flat(data["chunk_decay"])[:, :, ds(t * HALF_CHUNKS + (b * S // L + c), 1)]
                        did(b, dve.tensor_tensor(dst[:, :, :], dst[:, :, :], decay.to_broadcast([P, EH, P]), ALU.mult))
                    return stage

                stages = [masked("a1", ab, (2, 3)), masked("a2", ak, (0, 1)), x1, y1]
                for m in INNER:
                    stages.append(z(m))
                    if m != INNER[-1]:
                        stages.append(grow("x", X, 2, m))
                    stages.append(grow("y", Y, 3, m))
                stages += [r_, gh_(0), gh_(1), advance(0), advance(1)]
                with dve.Fori(0, TPB) as t:
                    for stage in stages:
                        for b in range(B):
                            stage(t, b)

            @block.scalar
            def _(act):
                def need(t, b, name):
                    act.wait_ge(made[b], t * PE_MARKS["each"] + PE_MARKS[name])

                def tok(t, b):
                    need(t, b, "turn")
                    act.copy(tok_b[b][:, :], bank[b][0][:, 0:E])
                    act.copy(tok_k[b][:, :], bank[b][0][:, E:2 * E])
                    act.copy(aw[b][:, :, 0:RN], bank[b][1][:, 0:E].rearrange("p (h c) -> p h c", h=RH))
                    act.copy(tok_v[b][:, :], bank[b][1][:, E:2 * E]).then_inc(act_did[b], 1)

                def w0(t, b):
                    need(t, b, "w0")
                    act.copy(aw[b][:, :, RN:2 * RN], bank[b][0][:, 0:E].rearrange("p (h c) -> p h c", h=RH)
                             ).then_inc(act_did[b], 1)

                def ta_(t, b):
                    need(t, b, "ta")
                    for half in range(EH):
                        ins = act.copy(ta[b][:, half, :, :].rearrange("p k (q c) -> p q k c", q=2),
                                       bank[b][0][:, half * 2 * P:(half + 1) * 2 * P].rearrange(
                                           "p (q k c) -> p q k c", q=2, k=2))
                    ins.then_inc(act_did[b], 1)

                def y_(t, b):
                    need(t, b, "ys1")
                    act.copy(flat(yt)[:, :, ds(t * P + b * S, P)],
                             bank[b][2][:, 0:2 * P].rearrange("p (h c) -> p h c", h=EH)).then_inc(act_did[b], 1)

                with act.Fori(0, TPB) as t:
                    for stage in (tok, w0, ta_, y_):
                        for b in range(B):
                            stage(t, b)

            @block.gpsimd
            def _(pool):
                def stage(t, b):
                    pool.tensor_copy(ar[b][:, :, 0:P], src("at", t, b))
                    pool.tensor_copy(ar[b][:, :, P:2 * P], src("rt", t, b))
                    pool.tensor_copy(vt[b][:, :, :], src("vt", t, b))
                    pool.tensor_copy(kt[b][:, :, :], src("kt", t, b))
                    pool.tensor_copy(bt[b][:, :, :], src("bt", t, b)).then_inc(staged[b], 1)

                for b in range(B):
                    pool.memset(state[0][b][:, :, :], 0.0)
                    stage(0, b)
                with pool.Fori(0, TPB - 1) as t:
                    for b in range(B):
                        pool.wait_ge(made[b], t * PE_MARKS["each"] + PE_MARKS["a3"])
                        stage(t + 1, b)


def gate_and_project(nc, data, vec, w, x):
    with ExitStack() as ctx:
        sb = lambda n, s, d=F32: ctx.enter_context(nc.sbuf_tensor("gp_" + n, s, d))
        ps = lambda n, s, d=F32: ctx.enter_context(nc.psum_tensor("gp_" + n, s, d))
        sem = lambda n: ctx.enter_context(nc.semaphore("gp_" + n))
        gated = [sb(f"gated{i}", [P, EH, TB]) for i in range(2)]
        p_proj = [ps(f"p_proj{i}", [P, TB // P, E]) for i in range(2)]
        scaled_ready, gated_ready, proj_ready, proj_used = (
            sem(n) for n in "scaled_ready gated_ready proj_ready proj_used".split())

        def rows(name, h, n):
            return data[name][:, h, ds(n, 1), :].rearrange("p n c -> p (n c)")

        def v_(name, h):
            return vec[:, h, VEC[name]:VEC[name] + 1]

        with nc.Block() as block:
            @block.vector
            def _(dve):
                dve.sem_inc(proj_ready, 2)
                with dve.Fori(0, NB // 2) as r:
                    for i in range(2):
                        n = r * 2 + i
                        dve.wait_ge(proj_ready, r * 2 + i + 1)
                        for h in range(EH):
                            dve.scalar_tensor_tensor(gated[i][:, h, :], rows("yt", h, n), v_("gn_scale", h),
                                                     rows("bonus", h, n), ALU.mult, ALU.add).then_inc(scaled_ready, 1)
                        for h in range(EH):
                            dve.wait_ge(scaled_ready, (r * 2 + i) * EH + h + 1)
                            dve.scalar_tensor_tensor(gated[i][:, h, :], gated[i][:, h, :], v_("gn_offset", h),
                                                     rows("gt", h, n), ALU.add, ALU.mult).then_inc(gated_ready, 1)
                    for i in range(2):
                        dve.wait_ge(proj_ready, r * 2 + i + 3)
                        tiles = x[:, ds((r * 2 + i) * (TB // P), TB // P), :]
                        dve.tensor_tensor(tiles, p_proj[i][:, :, :], tiles, ALU.add).then_inc(proj_used, 1)

            @block.tensor
            def _(pe):
                pe.sem_inc(proj_used, 2)
                with pe.Fori(0, NB // 2) as r:
                    for i in range(2):
                        pe.wait_ge(gated_ready, (r * 2 + i + 1) * EH)
                        pe.wait_ge(proj_used, r * 2 + i + 1)
                        for t in range(TB // P):
                            for h in range(EH):
                                mm = pe.matmul(p_proj[i][:, t, :], gated[i][:, h, t * P:(t + 1) * P], w[:, h, :],
                                               start=h == 0 and t % 2 == 0, stop=h == EH - 1, skip_group_check=True)
                        mm.then_inc(proj_ready, 1)


FFN = 2 * E
FT = FFN // P
TIE = 2.0 ** -25


def switch_phase(nc, xt, w_switch, ident, masks):
    with ExitStack() as ctx:
        sb = lambda n, s, d=F32: ctx.enter_context(nc.sbuf_tensor("sw_" + n, s, d))
        ps = lambda n, s, d=F32: ctx.enter_context(nc.psum_tensor("sw_" + n, s, d))
        sem = lambda n: ctx.enter_context(nc.semaphore("sw_" + n))
        logits_t = sb("logits_t", [2, NB, TB])
        tok = sb("tok", [P, TILES, 2])
        lead = sb("lead", [P, TILES])
        p_logits = ps("p_logits", [P, NB, TB])
        p_tok = ps("p_tok", [P, 512])
        logits_ready, logits_in, tok_ready, chain_s = (sem(n) for n in "logits_ready logits_in tok_ready chain".split())
        with nc.Block() as block:
            @block.tensor
            def _(pe):
                for n in range(NB):
                    for h in range(EH):
                        mm = pe.matmul(p_logits[0:2, n, :], w_switch[:, h, :], xt[:, h, n, 1:],
                                       start=h == 0, stop=h == EH - 1)
                mm.then_inc(logits_ready, 1)
                pe.wait_ge(logits_in, 1)
                for t in range(TILES):
                    mm = pe.transpose(p_tok[:, t * 2:(t + 1) * 2],
                                      logits_t[:, t // 4, (t % 4) * P:(t % 4 + 1) * P], ident[0:2, 0:2])
                mm.then_inc(tok_ready, 1)

            @block.scalar
            def _(act):
                act.wait_ge(logits_ready, 1)
                act.copy(logits_t[:, :, :], p_logits[0:2, :, :]).then_inc(logits_in, 1)

            @block.vector
            def _(dve):
                c = Chain(dve, chain_s)
                dve.wait_ge(tok_ready, 1)
                c.link(dve.tensor_copy(tok[:, :, :].rearrange("p t e -> p (t e)"), p_tok[:, 0:2 * TILES]))
                c.link(dve.tensor_tensor(lead[:, :], tok[:, :, 1], tok[:, :, 0], ALU.subtract))
                dve.tensor_scalar(masks[:, :, 1], lead[:, :], TIE, None, ALU.is_gt)
                dve.tensor_scalar(masks[:, :, 0], lead[:, :], TIE, None, ALU.is_le)


def switched_ffn_phase(nc, x, xt, masks, w_in, b_in, w_out, b_out):
    with ExitStack() as ctx:
        sb = lambda n, s, d=F32: ctx.enter_context(nc.sbuf_tensor("ff_" + n, s, d))
        ps = lambda n, s, d=F32: ctx.enter_context(nc.psum_tensor("ff_" + n, s, d))
        sem = lambda n: ctx.enter_context(nc.semaphore("ff_" + n))
        hidden = [sb(f"hidden{i}", [P, TB]) for i in range(2)]
        p_in = [ps(f"p_in{i}", [P, TB]) for i in range(2)]
        p_out = [ps(f"p_out{e}", [P, TB // P, E]) for e in range(2)]
        in_ready, hidden_ready, out_ready, out_used, biased, chain_s = (
            sem(n) for n in "in_ready hidden_ready out_ready out_used biased chain".split())
        HT = 2 * FT
        TPN = TB // P

        with nc.Block() as block:
            @block.tensor
            def _(pe):
                pe.sem_inc(out_used, 2)
                with pe.Fori(0, NB) as n:
                    def out(m):
                        e = m // FT
                        pe.wait_ge(hidden_ready, n * HT + m + 1)
                        if m % FT == 0:
                            pe.wait_ge(out_used, n * 2 + e + 1)
                        for t in range(TPN):
                            mm = pe.matmul(p_out[e][:, t, :], hidden[m % 2][:, t * P:(t + 1) * P], w_out[:, m, :],
                                           start=m % FT == 0 and t % 2 == 0, stop=m % FT == FT - 1,
                                           skip_group_check=True)
                        mm.then_inc(out_ready, 1)

                    for m in range(HT):
                        if m >= 2:
                            pe.wait_ge(hidden_ready, n * HT + m - 1)
                        for h in range(EH):
                            mm = pe.matmul(p_in[m % 2][:, :], w_in[:, h, m * P:(m + 1) * P],
                                           xt[:, h, ds(n, 1), 1:].rearrange("p n c -> p (n c)"),
                                           start=h == 0, stop=h == EH - 1)
                        mm.then_inc(in_ready, 1)
                        if m >= 1:
                            out(m - 1)
                    out(HT - 1)

            @block.scalar
            def _(act):
                act.sem_inc(out_ready, 2)
                with act.Fori(0, NB) as n:
                    for m in range(HT):
                        act.wait_ge(in_ready, n * HT + m + 1)
                        act.wait_ge(out_ready, n * HT + m + 1)
                        act.activation(hidden[m % 2][:, :], p_in[m % 2][:, :], ACT.Gelu if m < FT else ACT.Relu,
                                       bias=b_in[:, m:m + 1]).then_inc(hidden_ready, 1)

            @block.vector
            def _(dve):
                c = Chain(dve, chain_s)
                with dve.Fori(0, NB) as n:
                    c.loop(n, 4 * TPN)
                    at = lambda t: x[:, ds(n * TPN + t, 1), :].rearrange("p a e -> p (a e)")
                    mask = lambda t, e: masks[:, ds(n * TPN + t, 1), e]
                    for e in range(2):
                        for t in range(TPN):
                            if e:
                                c.wait(t + 1)
                            c.mark(dve.scalar_tensor_tensor(at(t), b_out[:, e, :], mask(t, e), at(t), ALU.mult, ALU.add))
                    for e in range(2):
                        dve.wait_ge(out_ready, n * HT + (e + 1) * FT + 2)
                        for t in range(TPN):
                            c.wait((1 + e) * TPN + t + 1)
                            c.mark(dve.scalar_tensor_tensor(at(t), p_out[e][:, t, :], mask(t, e), at(t), ALU.mult, ALU.add))
                        c.wait()
                        dve.sem_inc(out_used, 1)


def start_loads(nc, done, pairs):
    with nc.Block() as block:
        @block.sync
        def _(sp):
            for dst, src in pairs:
                sp.dma_start(dst, src).then_inc(done, 16)
    return len(pairs)


def finish_loads(nc, done, count):
    with nc.Block() as block:
        @block.sync
        def _(sp):
            sp.wait_ge(done, count * 16)


def halves(dram):
    return dram.rearrange("(h p) n -> p h n", p=P)


def two_blocks_program(nc, d, out):
    with ExitStack() as ctx:
        def sb_in(scope):
            return lambda n, s, dt=F32: scope.enter_context(nc.sbuf_tensor(n, s, dt))
        sb, sem = sb_in(ctx), lambda n: ctx.enter_context(nc.semaphore(n))
        start_loaded, moe_loaded, mix_loaded, rec_loaded, ffn_loaded, stored = (
            sem(n) for n in "start_loaded moe_loaded mix_loaded rec_loaded ffn_loaded stored".split())
        x = sb("x", [P, TILES, E])
        ident, ident16 = sb("ident", [P, P]), sb("ident16", [P, P], BF16)
        mean, rstd, eps = sb("mean", [P, TILES]), sb("rstd", [P, TILES]), sb("eps", [P, 1])
        head_ones = sb("head_ones", [P, P])
        vec = sb("vec", [P, EH, len(VECTORS) + 1])
        vec_in = vec[:, :, 0:len(VECTORS)]

        with ExitStack() as block0:
            sb0 = sb_in(block0)
            attn = sb0("attn", [P, UNITS, TPB, GROUP * HD])
            w_proj, b_proj = sb0("w_proj", [P, EH, E]), sb0("b_proj", [P, E])
            w_router, priority = sb0("w_router", [P, EH, EXPERTS]), sb0("priority", [P, EXPERTS])
            with ExitStack() as attention:
                sba = sb_in(attention)
                qparts, kparts = (sba(n, [P, 3, UNITS, TPB, GROUP * HD], BF16) for n in ("qparts", "kparts"))
                v = sba("v", [P, 1, UNITS, TPB, GROUP * HD])
                causal, anticausal = sba("causal", [P, P]), sba("anticausal", [P, P])
                causal16, anticausal16 = sba("causal16", [P, P], BF16), sba("anticausal16", [P, P], BF16)
                abias, shift0 = sba("abias", [P, NQC * TPB]), sba("shift0", [P, TPB])
                key_alibi = sba("key_alibi", [P, TPB, 2])
                with ExitStack() as projection:
                    sbp = sb_in(projection)
                    w_qkv, b_qkv = sbp("w_qkv", [P, EH, 3 * E]), sbp("b_qkv", [P, 3 * E])
                    count = start_loads(nc, start_loaded, [
                        (x[:, :, :], d["x"].rearrange("(t p) e -> p t e", p=P)),
                        (ident[:, :], d["ident"]),
                        (w_qkv[:, :, :], halves(d["w_qkv"])), (b_qkv[:, :], d["b_qkv"]),
                        (causal[:, :], d["causal"]), (anticausal[:, :], d["anticausal"]),
                        (abias[:, :], d["abias"]), (shift0[:, :], d["shift0"]),
                        (key_alibi[:, :, :], d["key_alibi"]),
                        (w_proj[:, :, :], halves(d["w_proj"])), (b_proj[:, :], d["b_proj"]),
                        (w_router[:, :, :], halves(d["w_router"])), (priority[:, :], d["priority"]),
                        (head_ones[:, :], d["head_ones"]), (vec_in, d["vectors"])])
                    finish_loads(nc, start_loaded, count)
                    with nc.Block() as block:
                        @block.vector
                        def _(dve):
                            dve.memset(eps[:, :], EPS)
                            dve.tensor_copy(ident16[:, :], ident[:, :])
                            dve.tensor_copy(causal16[:, :], causal[:, :])
                            dve.tensor_copy(anticausal16[:, :], anticausal[:, :])
                            dve.tensor_scalar(b_qkv[:, 0:E], b_qkv[:, 0:E], HD ** -0.5, None, ALU.mult)
                    layernorm_stats(nc, "ln1_", x, mean, rstd, eps)
                    qkv_phase(nc, x, mean, rstd, ident, w_qkv, b_qkv, qparts, kparts, v)
                attention_phase(nc, ident, ident16, causal16, anticausal16, abias, shift0, key_alibi,
                                qparts, kparts, v, attn)
            select32, select = sb0("select32", [3 * SLICES, WIDTH]), sb0("select", [3 * SLICES, WIDTH], BF16)
            w_gate, w_up = sb0("w_gate", [P, EH, WIDTH]), sb0("w_up", [P, EH, WIDTH])
            w_down = sb0("w_down", [P, MT, E])
            whole = WIDTH // P
            count = start_loads(nc, moe_loaded, [
                (select32[:, :], d["select"]), (w_gate[:, :, :], halves(d["w_gate"])),
                (w_up[:, :, :], halves(d["w_up"])),
                (w_down[:, 0:whole, :], d["w_down"][0:whole * P, :].rearrange("(m p) e -> p m e", p=P)),
                (w_down[0:WIDTH - whole * P, whole, :], d["w_down"][whole * P:WIDTH, :])])
            project_attention(nc, attn, x, b_proj, ident, w_proj)
            layernorm_stats(nc, "ln2_", x, mean, rstd, eps)
            xt = sb0("xt_moe", [P, EH, NB, TB + 1])
            gates_t = sb0("gates_t", [3 * SLICES, B * S], BF16)
            normalise_and_turn(nc, "nt2_", x, mean, rstd, ident, xt)
            router_phase(nc, xt, w_router, ident, ident16, priority, gates_t)
            finish_loads(nc, moe_loaded, count)
            with nc.Block() as block:
                @block.vector
                def _(dve):
                    dve.tensor_copy(select[:, :], select32[:, :])
            moe_phase(nc, x, xt, gates_t, select, w_gate, w_up, w_down)

        w_out = sb("w_out", [P, EH, E])
        data = {n: sb(n, [P, EH, NB, TB]) for n in "rt at bt kt vt gt bonus".split()}
        data["chunk_decay"] = sb("chunk_decay", [P, EH, NB, CPB])
        data["yt"] = data["vt"]
        with ExitStack() as mixing:
            sbm = sb_in(mixing)
            weights = {n: sbm("w_" + n, [P, EH, k]) for n, k in
                       (("w1", 64), ("a1", 64), ("g1", P), ("r", E), ("k", E), ("v", E))}
            weights |= {n: sbm("w_" + n, [k, E]) for n, k in (("w2", 64), ("a2", 64), ("g2", P))}
            carry = sbm("carry", [P, TB])
            head_spread, head_columns = sbm("head_spread", [P, 2 * EH, P]), sbm("head_columns", [P, 32])
            xt = sbm("xt_mix", [P, EH, NB, TB + 1])
            count = start_loads(nc, mix_loaded, [
                (w[:, :, :], halves(d["mix_" + n])) if len(w.shape) == 3 else (w[:, :], d["mix_" + n])
                for n, w in weights.items()] + [(carry[:, :], d["carry"]), (head_spread[:, :, :], d["head_spread"]),
                                           (head_columns[:, :], d["head_columns"]), (w_out[:, :, :], halves(d["w_out"]))])
            layernorm_stats(nc, "ln3_", x, mean, rstd, eps)
            normalise_and_turn(nc, "nt3_", x, mean, rstd, ident, xt)
            finish_loads(nc, mix_loaded, count)
            time_mix_phase(nc, xt, vec, weights, head_spread, head_columns, head_ones, carry, data)
        with ExitStack() as recurrence:
            sbr = sb_in(recurrence)
            chunk_masks, level_masks, level1_t = (
                sbr("chunk_masks", [P, 2 * P]), sbr("level_masks", [P, len(LEVELS), P]), sbr("level1_t", [P, P]))
            count = start_loads(nc, rec_loaded, [(chunk_masks[:, :], d["chunk_masks"]),
                                                 (level_masks[:, :, :], d["level_masks"]), (level1_t[:, :], d["level1_t"])])
            finish_loads(nc, rec_loaded, count)
            recurrence_phase(nc, data, ident, chunk_masks, level_masks, level1_t, head_ones, data["yt"])
        w_switch = sb("w_switch", [P, EH, 2])
        w_in, b_in = sb("w_in", [P, EH, 2 * FFN]), sb("b_in", [P, 2 * FT])
        w_back, b_back = sb("w_back", [P, 2 * FT, E]), sb("b_back", [P, 2, E])
        branch, xt = sb("branch", [P, TILES, 2]), sb("xt_ffn", [P, EH, NB, TB + 1])
        count = start_loads(nc, ffn_loaded, [
            (w_switch[:, :, :], halves(d["w_switch"])), (w_in[:, :, :], halves(d["ffn_in"])), (b_in[:, :], d["ffn_b_in"]),
            (w_back[:, :, :], halves(d["ffn_back"])), (b_back[:, :, :], d["ffn_b_back"])])
        gate_and_project(nc, data, vec, w_out, x)
        layernorm_stats(nc, "ln4_", x, mean, rstd, eps)
        normalise_and_turn(nc, "nt4_", x, mean, rstd, ident, xt)
        finish_loads(nc, ffn_loaded, count)
        switch_phase(nc, xt, w_switch, ident, branch)
        switched_ffn_phase(nc, x, xt, branch, w_in, b_in, w_back, b_back)
        with nc.Block() as block:
            @block.sync
            def _(sp):
                sp.dma_start(out.rearrange("(t p) e -> p t e", p=P), x[:, :, :]).then_inc(stored, 16)
                sp.wait_ge(stored, 16)


def shape_constants():
    p = np.arange(P)
    f = np.float32
    key = np.arange(TPB)[None] * P + p[:, None]
    abias = np.stack([SLOPE * (kt * P + p - (c * QC + QC // 2)) for c in range(NQC) for kt in range(TPB)], 1)
    shift0 = [SLOPE * (QC * (t * P // QC) + QC // 2) for t in range(TPB)]
    line = (SLOPE * key).astype(f)
    high = (line.view(np.uint32) & 0xffff0000).view(f)
    row, col = p[:, None], p[None]
    same = row // L == col // L
    joins = [(row // (2 * m) == col // (2 * m)) & (row % (2 * m) >= m) & (col % (2 * m) < m) for m in LEVELS]
    hidden_slice = np.minimum(np.arange(WIDTH) // HIDDEN, EXPERTS)
    select = np.tile(hidden_slice[None] == np.arange(SLICES)[:, None], (3, 1))
    consts = dict(
        ident=np.eye(P), causal=np.where(col <= row, 0, NEG), anticausal=np.where(row <= col, 0, NEG),
        abias=abias, shift0=np.tile(shift0, (P, 1)), key_alibi=np.stack([high, line - high], -1),
        head_ones=row // RN == col // RN, priority=np.tile(EXPERTS - np.arange(EXPERTS), (P, 1)), select=select,
        head_spread=p[:, None, None] == 32 * np.arange(2 * EH)[:, None] + p // RN, head_columns=p[:, None] // RN == np.arange(32)[None],
        carry=np.tile(np.arange(TB) % L != 0, (P, 1)),
        chunk_masks=np.concatenate([same & (row < col), same & (row <= col)], 1),
        level_masks=np.stack(joins, 1), level1_t=joins[0].T)
    return {n: np.ascontiguousarray(a, dtype=f) for n, a in consts.items()}


def kernel(**inputs):
    import concourse.bacc as bacc
    from concourse.bass_utils import run_bass_kernel_spmd

    def on_every_row(a):
        return np.broadcast_to(a, (P,) + a.shape)

    def side_by_side(a):
        return a.transpose(1, 0, 2).reshape(a.shape[1], -1)

    z = {n: np.asarray(a) for n, a in inputs.items()}
    a0, f0 = (lambda n: z["L0_attn_" + n]), (lambda n: z["L0_ffn_" + n])
    a1, f1 = (lambda n: z["L1_attn_" + n]), (lambda n: z["L1_ffn_" + n])
    arrays = shape_constants()
    arrays |= dict(
        x=a0("hidden_states").reshape(B * S, E), w_qkv=a0("W_attn"), b_qkv=on_every_row(a0("b_attn")),
        w_proj=a0("W_proj"), b_proj=on_every_row(a0("b_proj")), w_router=f0("router_w").T,
        w_gate=np.concatenate([side_by_side(f0("wg")), f0("sg")], 1),
        w_up=np.concatenate([side_by_side(f0("wu")), f0("su")], 1),
        w_down=np.concatenate([f0("wd").reshape(-1, E), f0("sd")], 0),
        vectors=np.stack([a1(n).reshape(EH, P).T for n in VECTORS], -1),
        w_out=a1("W_o"), w_switch=f1("Wg").T,
        ffn_in=np.concatenate([f1("W0a").T, f1("W1a").T], 1), ffn_back=np.concatenate([f1("W0b").T, f1("W1b").T], 0),
        ffn_b_in=np.concatenate([f1("b0a"), f1("b1a")]).reshape(2 * FT, P).T,
        ffn_b_back=on_every_row(np.stack([f1("b0b"), f1("b1b")])))
    arrays |= {"mix_" + n: a1(n) for n in ("w1", "a1", "g1", "w2", "a2", "g2")}
    arrays |= {"mix_" + n: a1("W_" + n) for n in "rkv"}

    nc = bacc.Bacc("TRN2", target_bir_lowering=False, num_devices=1)
    feeds, dram = {}, {}
    for name, a in arrays.items():
        a = np.ascontiguousarray(a)
        feeds[f"in_{name}_dram"] = a
        dram[name] = nc.dram_tensor(f"in_{name}_dram", a.shape, mybir.dt.from_np(a.dtype), kind="ExternalInput").ap()
    out = nc.dram_tensor("out_0_dram", (B * S, E), F32, kind="ExternalOutput").ap()
    two_blocks_program(nc, dram, out)
    result = run_bass_kernel_spmd(nc, [feeds], core_ids=[0])
    return result.results[0]["out_0_dram"].reshape(B, S, E)
```

```python
from contextlib import ExitStack

import numpy as np

import concourse.bass as bass
from concourse import mybir

ALU = mybir.AluOpType
ACT = mybir.ActivationFunctionType
AX = mybir.AxisListType
F32 = mybir.dt.float32
BF16 = mybir.dt.bfloat16
ds = bass.ds

P = 128
B, S, E = 2, 1024, 256
TILES = B * S // P
TPB = S // P
EH = E // P
HEADS, HD = 32, 8
GROUP = 4
UNITS = B * HEADS // GROUP
GPB = HEADS // GROUP
SLOPE = 2.0 ** (-8.0 / HEADS)
NEG = -1e30
EPS = 1e-5
QC = 512
NQC = S // QC


class Chain:

    def __init__(self, eng, sem):
        self.eng, self.sem, self.done, self.round = eng, sem, 0, None

    def loop(self, i, each):
        self.round, self.each, self.start = i, each, self.done

    def end(self, rounds):
        assert self.done - self.start == self.each, self.done - self.start
        self.round, self.done = None, self.start + self.each * rounds

    def mark(self, ins):
        ins.then_inc(self.sem, 1)
        self.done += 1
        return self.done

    def wait(self, mark=None):
        mark = self.done if mark is None else mark
        self.eng.wait_ge(self.sem, mark if self.round is None else self.round * self.each + mark)

    def link(self, ins):
        self.mark(ins)
        self.wait()


def tile_stats(dve, stats, x, tile):
    return dve.bn_stats(stats[:, ds(tile, 1), :], x[:, ds(tile, 1), :])


def layernorm_stats(nc, tag, x, stats, mean, rstd, eps, taken=True):
    with ExitStack() as ctx:
        sb = lambda n, s, d=F32: ctx.enter_context(nc.sbuf_tensor(tag + n, s, d))
        sem = lambda n: ctx.enter_context(nc.semaphore(tag + n))
        half, diff, var, std = (sb(n, [P, TILES]) for n in ("half", "diff", "var", "std"))
        chain_s, var_ready, std_ready = sem("chain"), sem("var_ready"), sem("std_ready")
        with nc.Block() as block:
            @block.vector
            def _(dve):
                c = Chain(dve, chain_s)
                if not taken:
                    with dve.Fori(0, TILES) as i:
                        c.loop(i, 1)
                        c.mark(tile_stats(dve, stats, x, i))
                    c.end(TILES)
                    c.wait()
                c.link(dve.tensor_tensor(half[:, :], stats[:, :, 1], stats[:, :, 4], ALU.add))
                c.link(dve.tensor_tensor(diff[:, :], stats[:, :, 1], stats[:, :, 4], ALU.subtract))
                c.link(dve.tensor_tensor(var[:, :], stats[:, :, 2], stats[:, :, 5], ALU.add))
                c.link(dve.tensor_scalar(mean[:, :], half[:, :], 0.5, None, ALU.mult))
                c.link(dve.scalar_tensor_tensor(diff[:, :], diff[:, :], 0.25, diff[:, :], ALU.mult, ALU.mult))
                dve.scalar_tensor_tensor(var[:, :], var[:, :], 1.0 / E, diff[:, :], ALU.mult,
                                         ALU.add).then_inc(var_ready, 1)
                dve.wait_ge(std_ready, 1)
                dve.reciprocal(rstd[:, :], std[:, :])

            @block.scalar
            def _(act):
                act.wait_ge(var_ready, 1)
                act.activation(std[:, :], var[:, :], ACT.Sqrt, bias=eps[:, 0:1]).then_inc(std_ready, 1)


def qkv_phase(nc, x, mean, rstd, ident, w, bias, qparts, kparts, v):
    with ExitStack() as ctx:
        sb = lambda n, s, d=F32: ctx.enter_context(nc.sbuf_tensor("qkv_" + n, s, d))
        ps = lambda n, s, d=F32: ctx.enter_context(nc.psum_tensor("qkv_" + n, s, d))
        sem = lambda n: ctx.enter_context(nc.semaphore("qkv_" + n))
        xn = [sb(f"xn{b}", [P, E]) for b in range(B)]
        xt = [sb(f"xt{b}", [P, EH, P]) for b in range(B)]
        qk = [sb(f"qk{b}", [P, 2 * E]) for b in range(B)]
        rest = [sb(f"rest{b}", [P, 2 * E]) for b in range(B)]
        pt = [ps(f"pt{b}", [P, 512]) for b in range(B)]
        pq = [ps(f"pq{b}", [P, 1024]) for b in range(B)]
        names = "xn_ready xt_psum xt_ready proj_ready qk_ready high_ready rest_ready mid_ready low_done proj_used"
        s = {n: sem(n) for n in names.split()}
        scale = HD ** -0.5

        def parts_at(t, buf, part, b):
            return buf[:, part, b * GPB:(b + 1) * GPB, ds(t, 1), :].rearrange("p g t c -> p (g t) c")

        def rounds(step):
            def program(eng):
                step(eng, -1, True, False)
                step(eng, 0, True, False)
                with eng.Fori(0, TPB - 2) as r:
                    step(eng, r + 1, True, True)
                step(eng, TPB - 1, False, True)
                step(eng, TPB, False, True)
            return program

        def now(t):
            return not (isinstance(t, int) and t in (-1, TPB))

        def vector_step(dve, t, more, before):
            for b in range(B if more else 0):
                if now(t):
                    dve.wait_ge(s["xt_psum"], t * B + (b + 1))
                tile = t + (b * TPB + 1)
                dve.tensor_scalar(xn[b][:, :], x[:, ds(tile, 1), :].rearrange("p a e -> p (a e)"),
                                  mean[:, ds(tile, 1)], rstd[:, ds(tile, 1)],
                                  ALU.subtract, ALU.mult).then_inc(s["xn_ready"], 1)
            for b in range(B):
                if now(t):
                    dve.wait_ge(s["proj_ready"], t * B + (b + 1))
                    dve.scalar_tensor_tensor(qk[b][:, 0:E], pq[b][:, 0:E], scale, bias[:, 0:E],
                                             ALU.mult, ALU.add).then_inc(s["qk_ready"], 1)
                    dve.tensor_tensor(qk[b][:, E:2 * E], pq[b][:, E:2 * E], bias[:, E:2 * E],
                                      ALU.add).then_inc(s["qk_ready"], 1)
                    dve.tensor_tensor(parts_at(t, v, 0, b),
                                      pq[b][:, 2 * E:3 * E].rearrange("p (g c) -> p g c", g=GPB),
                                      bias[:, 2 * E:3 * E].rearrange("p (g c) -> p g c", g=GPB),
                                      ALU.add).then_inc(s["proj_used"], 1)
                if before:
                    dve.wait_ge(s["mid_ready"], (t - 1) * B + (b + 1))
                    for n, buf in enumerate((qparts, kparts)):
                        dve.tensor_tensor(parts_at(t - 1, buf, 2, b),
                                          rest[b][:, n * E:(n + 1) * E].rearrange("p (g c) -> p g c", g=GPB),
                                          parts_at(t - 1, buf, 1, b), ALU.subtract).then_inc(s["low_done"], 1)
                if now(t):
                    dve.wait_ge(s["high_ready"], (t * B + (b + 1)) * 2)
                    if before:
                        dve.wait_ge(s["low_done"], ((t - 1) * B + (b + 1)) * 2)
                    for n, buf in enumerate((qparts, kparts)):
                        dve.tensor_tensor(rest[b][:, n * E:(n + 1) * E].rearrange("p (g c) -> p g c", g=GPB),
                                          qk[b][:, n * E:(n + 1) * E].rearrange("p (g c) -> p g c", g=GPB),
                                          parts_at(t, buf, 0, b), ALU.subtract).then_inc(s["rest_ready"], 1)

        def scalar_step(act, t, more, before):
            for b in range(B):
                if now(t):
                    act.wait_ge(s["qk_ready"], (t * B + (b + 1)) * 2)
                    for n, buf in enumerate((qparts, kparts)):
                        act.copy(parts_at(t, buf, 0, b),
                                 qk[b][:, n * E:(n + 1) * E].rearrange("p (g c) -> p g c", g=GPB)
                                 ).then_inc(s["high_ready"], 1)
                if more:
                    act.wait_ge(s["xt_psum"], (t + 1) * B + (b + 1))
                    act.copy(xt[b][:, :, :], pt[b][:, 0:E].rearrange("p (h c) -> p h c", h=EH)
                             ).then_inc(s["xt_ready"], 1)

        def pool_step(pool, t, more, before):
            for b in range(B if now(t) else 0):
                pool.wait_ge(s["rest_ready"], (t * B + (b + 1)) * 2)
                for n, buf in enumerate((qparts, kparts)):
                    last = pool.tensor_copy(parts_at(t, buf, 1, b),
                                            rest[b][:, n * E:(n + 1) * E].rearrange("p (g c) -> p g c", g=GPB))
                last.then_inc(s["mid_ready"], 1)

        def tensor_step(pe, t, more, before):
            for b in range(B if now(t) else 0):
                pe.wait_ge(s["xt_ready"], t * B + (b + 1))
                if before:
                    pe.wait_ge(s["proj_used"], (t - 1) * B + (b + 1))
                for lo, hi in ((0, 512), (512, 768)):
                    for h in range(EH):
                        mm = pe.matmul(pq[b][:, lo:hi], xt[b][:, h, :], w[:, h, lo:hi],
                                       start=h == 0, stop=h == EH - 1)
                mm.then_inc(s["proj_ready"], 1)
            for b in range(B if more else 0):
                pe.wait_ge(s["xn_ready"], (t + 1) * B + (b + 1))
                for h in range(EH):
                    mm = pe.transpose(pt[b][:, h * P:(h + 1) * P], xn[b][:, h * P:(h + 1) * P], ident[:, :])
                mm.then_inc(s["xt_psum"], 1)

        with nc.Block() as block:
            @block.vector
            def _(dve):
                rounds(vector_step)(dve)

            @block.scalar
            def _(act):
                rounds(scalar_step)(act)

            @block.gpsimd
            def _(pool):
                rounds(pool_step)(pool)

            @block.tensor
            def _(pe):
                rounds(tensor_step)(pe)


ROWS = 64
PRODUCTS = 6
SHIFT_ROW = PRODUCTS * HD
ALIBI_ROW = SHIFT_ROW + 3
CROWS = 5
KEY_ORDER = [(0, 1, 3, 2), (0, 7, 1, 6, 2, 5, 3, 4)]
STEPS = [(c, kt) for c in range(NQC) for kt in KEY_ORDER[c]]
LAST0 = len(KEY_ORDER[0]) - 1
FILLS = [([(3, 0, 4)], 40, 1, 4), ([(4, 0, 4)], 16, 1, 4), ([(5, 0, 4)], 48, 1, 4), ([(6, 0, 4)], 27, 1, 4),
         ([(7, 0, 4)], 56, 1, 4), ([(7, 4, 4)], 60, 1, 4), ([(0, 0, 1), (2, 0, 3)], 7, 1, 4),
         ([(4, 4, 1), (6, 4, 3)], 23, 1, 4), ([(1, 0, 2), (5, 4, 2)], 32, 20, 2)]
SLOTS = 72
PAIR_FILLS = 2 * len(FILLS)
FILLS_PER_STEP = [4, 4, 3, 3, 3, 3, 4, 3, 3, 3, 3, 0]


def slot_events(kind):
    extra = {0: ["shift_own", "turn 0", "prev", "turn 1"], 1: ["turn 2"], 2: ["turn 3"], 3: ["out_prev"],
             6: ["out_now"], 8: ["shift 0"]}
    ev, fill = [], 0

    def fills(count):
        nonlocal fill
        for _ in range(count):
            ev.append(("fill", fill // PAIR_FILLS, fill % PAIR_FILLS))
            fill += 1
            if fill % PAIR_FILLS == 0:
                ev.append(("max", fill // PAIR_FILLS - 1))

    for k in range(len(STEPS)):
        step = []
        if "s" in kind and k != 1:
            step.append(("scores", k, 0))
        for name in extra.get(k, []):
            what, _, arg = name.partition(" ")
            if what == "turn" and "m" in kind:
                step.append((what, int(arg)))
            if what == "shift" and "m" in kind:
                step.append((what, int(arg), 0))
            if what == "shift_own" and "s" in kind:
                step.append(("shift", 1, 1))
            if what == "prev" and "p" in kind:
                step += [("pv", len(STEPS) - 1, 1), ("take", 1, 1)]
            if what == "out_prev" and "p" in kind:
                step.append(("out", 1, 1))
            if what == "out_now" and "s" in kind:
                step.append(("out", 0, 0))
        if "s" in kind:
            if k == 0:
                step.append(("scores", 1, 0))
            step.append(("scores", k, 1))
            if k >= 1:
                step.append(("pv", k - 1, 0))
            if k == LAST0 + 1:
                step.append(("take", 0, 0))
        left = FILLS_PER_STEP[k] if "m" in kind else 0
        after = [n for n, e in enumerate(step) if e[0] in ("scores", "turn", "pv", "out")
                 and not any(x == ("turn", 1) for x in step[n + 1:])]
        for n, e in enumerate(step):
            ev.append(e)
            if n in after:
                now = -(-left // (len(after) - after.index(n)))
                fills(now)
                left -= now
        fills(left)
    return ev


def score_place(k, pair):
    return {(1, 0): 1, (0, 1): 2}.get((k, pair), 2 * k + pair)


def is_shared(e):
    return e[0] in ("shift", "out") or (e[0] == "turn" and e[1] >= 2)


def shared_uses(kind):
    return sum(is_shared(e) for e in slot_events(kind))


def shared_place(events, n, u):
    before = sum(is_shared(e) for e in events[:n])
    first, second, full = shared_uses("m"), shared_uses("sm"), shared_uses("psm")
    if isinstance(u, int) and u <= 0:
        return before + (first if u == 0 else 0)
    if isinstance(u, int) and u == UNITS:
        return first + second + (UNITS - 2) * full + shared_uses("ps") + before
    return (u - 1) * full + (first + second + before)


def attention_phase(nc, ident, ident16, causal16, anticausal16, abias, shift0, key_alibi, qparts, kparts, v, attn):
    with ExitStack() as ctx:
        sb = lambda n, s, d=F32: ctx.enter_context(nc.sbuf_tensor("at_" + n, s, d))
        ps = lambda n, s, d=F32: ctx.enter_context(nc.psum_tensor("at_" + n, s, d))
        sem = lambda n: ctx.enter_context(nc.semaphore("at_" + n))
        qstack, kstack = (sb(n, [P, TPB, GROUP, ROWS], BF16) for n in ("qstack", "kstack"))
        qt = [sb(f"qt{i}", [P, 2, S], BF16) for i in range(2)]
        kt_ = [sb(f"kt{i}", [P, 2, S], BF16) for i in range(2)]
        vs = [sb(f"vs{i}", [P, TPB, GROUP, 32]) for i in range(2)]
        probs = [sb(f"probs{i}", [P, GROUP, QC]) for i in range(2)]
        block_max = sb("block_max", [P, GROUP, SLOTS])
        row_max = sb("row_max", [P, GROUP, TPB])
        shift = sb("shift", [P, 2, 2, TPB])
        rest = sb("rest", [P, 2, 2, TPB])
        shift16 = sb("shift16", [P, 2, 2, CROWS, TPB], BF16)
        rows16 = [sb(f"rows16{i}", [2 * CROWS * TPB, P], BF16) for i in range(2)]
        ot = sb("ot", [P, QC])
        rden = sb("rden", [P, QC // P, GROUP])
        p_score = [ps(f"p_score{i}", [P, 2, QC]) for i in range(2)]
        p_fill = [ps(f"p_fill{i}", [P, QC]) for i in range(2)]
        p_out = ps("p_out", [P, QC])
        p_shared = ps("p_shared", [P, QC])
        shared16 = p_shared[:, :].bitcast(BF16)
        s = {n: sem(n) for n in ("preset preset_dve first_queries stack_ready v_ready pair_full pair_used shared_full shared_used fill_ready fill_used "
                                 "max_ready shift_ready rows0 rows1 scores_ready exp_done pv_done "
                                 "out_taken pool_chain dve_chain").split()}
        rows_loaded = [s["rows0"], s["rows1"]]
        NS = len(STEPS)
        DIAG = [k for k, (c, kt) in enumerate(STEPS) if kt * P >= c * QC]

        def left(k):
            c, kt = STEPS[k]
            return max(0, kt * P - c * QC)

        def slots(slot):
            def program(eng):
                slot(eng, -1, 1, "m")
                slot(eng, 0, 0, "sm")
                with eng.Fori(0, UNITS // 2 - 2) as r:
                    slot(eng, r * 2 + 1, 1, "psm")
                    slot(eng, r * 2 + 2, 0, "psm")
                slot(eng, UNITS - 3, 1, "psm")
                slot(eng, UNITS - 2, 0, "psm")
                slot(eng, UNITS - 1, 1, "ps")
                slot(eng, UNITS, 0, "p")
            return program

        def turn_bank(n):
            return p_fill[n][:, :].bitcast(BF16) if n < 2 else shared16

        def wait_turned(eng, events, n, u):
            if is_shared(events[n]):
                eng.wait_ge(s["shared_full"], shared_place(events, n, u) + 1)
            else:
                eng.wait_ge(s["pair_full"], (u + 1) * 2 + (events[n][1] + 1))

        def early(u, k=0):
            return isinstance(u, int) and u == 0 and k < 2

        def tensor_slot(pe, u, par, kind):
            ev, nxt = slot_events(kind), 1 - par
            for n, e in enumerate(ev):
                if is_shared(e):
                    before = shared_place(ev, n, u)
                    if not (isinstance(before, int) and before == 0):
                        pe.wait_ge(s["shared_used"], before)
                elif e[0] == "turn" and not (isinstance(u, int) and u < 0):
                    pe.wait_ge(s["fill_used"], (u + 1) * 2 * PAIR_FILLS)
                if e[0] == "turn":
                    if e[1] == 0:
                        pe.wait_ge(s["stack_ready"], u + 2)
                        if isinstance(u, int) and u < 0:
                            pe.wait_ge(s["first_queries"], 1)
                    stack, pair = (qstack, kstack)[e[1] % 2], e[1] // 2
                    for t in range(TPB):
                        mm = pe.transpose(turn_bank(e[1])[:, t * P:(t + 1) * P],
                                          stack[:, t, 2 * pair:2 * pair + 2, :].rearrange("p h r -> p (h r)"),
                                          ident16[:, :])
                    mm.then_inc(s["shared_full" if is_shared(e) else "pair_full"], 1)
                elif e[0] == "fill":
                    pair, f = e[1:]
                    at, h = f // 2, f % 2
                    if pair * PAIR_FILLS + f >= 2:
                        pe.wait_ge(s["fill_used"], (u + 1) * 2 * PAIR_FILLS + pair * PAIR_FILLS + f - 1)
                    if f == 0 and pair == 0:
                        pe.wait_ge(s["pair_used"], (u + 2) * 2)
                    elif f == 0:
                        pe.wait_ge(s["shared_used"], shared_place(ev, ev.index(("turn", 2 * pair + 1)), u) + 1)
                    bank, col = p_fill[f % 2], 0
                    for t, b0, nb in FILLS[at][0]:
                        diag = b0 + nb == t + 1
                        mm = pe.matmul(bank[:, col:col + nb * P], qt[nxt][h * ROWS:(h + 1) * ROWS, pair, t * P:(t + 1) * P],
                                       kt_[nxt][h * ROWS:(h + 1) * ROWS, pair, b0 * P:(b0 + nb) * P],
                                       start=col == 0, stop=not diag, skip_group_check=True)
                        col += nb * P
                        if diag:
                            mm = pe.matmul(bank[:, col - P:col], ident16[:, :], causal16[:, :],
                                           start=False, stop=True, skip_group_check=True)
                    mm.then_inc(s["fill_ready"], 1)
                elif e[0] == "shift":
                    pe.wait_ge(s["shift_ready"], (u + 1) * 2 if e[2] else (u + 1) * 2 + 1)
                    pe.transpose(shared16[0:2 * CROWS * TPB, 0:P],
                                 shift16[:, e[1], :, :, :].rearrange("p h r t -> p (h r t)"),
                                 ident16[:, :]).then_inc(s["shared_full"], 1)
                elif e[0] == "scores":
                    k, pair = e[1:]
                    c, kt = STEPS[k]
                    if k == 0:
                        pe.wait_ge(rows_loaded[pair], (u + 1) * 32)
                    if k or not early(u):
                        pe.wait_ge(s["exp_done"], u * 2 * NS + (score_place(k - 1, pair) + 1))
                    for h in range(2):
                        mm = pe.matmul(p_score[pair][:, h, left(k):QC],
                                       kt_[par][h * ROWS:(h + 1) * ROWS, pair, kt * P:(kt + 1) * P],
                                       qt[par][h * ROWS:(h + 1) * ROWS, pair, c * QC + left(k):(c + 1) * QC],
                                       start=True, stop=k not in DIAG, skip_group_check=True)
                        if k in DIAG:
                            mm = pe.matmul(p_score[pair][:, h, left(k):left(k) + P], ident16[:, :], anticausal16[:, :],
                                           start=False, stop=True, skip_group_check=True)
                    mm.then_inc(s["scores_ready"], 1)
                elif e[0] == "pv":
                    k, unit = e[1], u - e[2]
                    c, kt = STEPS[k]
                    if k == 0:
                        pe.wait_ge(s["v_ready"], u + 1)
                    if kt == KEY_ORDER[c][0] and (c or not early(u)):
                        pe.wait_ge(s["out_taken"], unit * NQC + c)
                    pe.wait_ge(s["exp_done"], unit * 2 * NS + (score_place(k, 1) + 1))
                    for h in range(GROUP):
                        mm = pe.matmul(p_out[32 * h:32 * h + 32, left(k):QC], vs[nxt if e[2] else par][:, kt, h, :],
                                       probs[k % 2][:, h, left(k):QC], start=kt == KEY_ORDER[c][0],
                                       stop=kt == KEY_ORDER[c][-1], skip_group_check=True)
                    mm.then_inc(s["pv_done"], 1)
                elif e[0] == "out":
                    pe.wait_ge(s["out_taken"], (u - e[2]) * NQC + e[1] + 1)
                    for t in range(QC // P):
                        mm = pe.transpose(p_shared[:, t * P:(t + 1) * P], ot[:, t * P:(t + 1) * P], ident[:, :])
                    mm.then_inc(s["shared_full"], 1)

        def scalar_slot(act, u, par, kind):
            ev, nxt = slot_events(kind), 1 - par
            for n, e in enumerate(ev):
                if e[0] == "turn" and e[1] % 2 == 0:
                    wait_turned(act, ev, n, u)
                    act.copy(qt[nxt][:, e[1] // 2, :], turn_bank(e[1])[:, 0:S]
                             ).then_inc(s["shared_used" if is_shared(e) else "pair_used"], 1)
                elif e[0] == "shift":
                    act.wait_ge(s["shared_full"], shared_place(ev, n, u) + 1)
                    act.copy(rows16[e[1]][:, :], shared16[0:2 * CROWS * TPB, 0:P]).then_inc(s["shared_used"], 1)
                elif e[0] == "scores":
                    k, pair = e[1:]
                    c, kt = STEPS[k]
                    act.wait_ge(s["scores_ready"], u * 2 * NS + (score_place(k, pair) + 1))
                    if not early(u, k):
                        act.wait_ge(s["pv_done"], u * NS + (k - 1))
                    act.activation(probs[k % 2][:, 2 * pair:2 * pair + 2, left(k):QC],
                                   p_score[pair][:, :, left(k):QC], ACT.Exp,
                                   bias=abias[:, c * TPB + kt:c * TPB + kt + 1]).then_inc(s["exp_done"], 1)
                elif e[0] == "take":
                    act.wait_ge(s["pv_done"], (u - e[2]) * NS + (NS if e[1] else LAST0 + 1))
                    act.copy(ot[:, :], p_out[:, :]).then_inc(s["out_taken"], 1)

        def vector_slot(dve, u, par, kind):
            ev, nxt = slot_events(kind), 1 - par
            for n, e in enumerate(ev):
                if e[0] == "turn" and e[1] % 2:
                    wait_turned(dve, ev, n, u)
                    dve.tensor_copy(kt_[nxt][:, e[1] // 2, :], turn_bank(e[1])[:, 0:S]
                                    ).then_inc(s["shared_used" if is_shared(e) else "pair_used"], 1)
                elif e[0] == "fill":
                    pair, f = e[1:]
                    (_, first, step, count), h = FILLS[f // 2], 2 * pair + f % 2
                    dve.wait_ge(s["fill_ready"], (u + 1) * 2 * PAIR_FILLS + pair * PAIR_FILLS + f + 1)
                    if step == 1:
                        dst, src = block_max[:, h, first:first + count], p_fill[f % 2][:, :].rearrange("p (a c) -> p a c", c=P)
                    else:
                        dst = block_max[:, h, first:first + 2 * step].rearrange("p (a c) -> p a c", c=step)[:, :, 0:count]
                        src = p_fill[f % 2][:, :].rearrange("p (a b c) -> p a b c", a=2, c=P)
                    dve.tensor_reduce(dst, src, AX.X, ALU.max).then_inc(s["fill_used"], 1)
                elif e[0] == "max":
                    pair = e[1]
                    dve.wait_ge(s["fill_used"], (u + 1) * 2 * PAIR_FILLS + (pair + 1) * PAIR_FILLS)
                    dve.tensor_reduce(row_max[:, 2 * pair:2 * pair + 2, :].rearrange("p h (j e) -> p h e j", e=2),
                                      block_max[:, 2 * pair:2 * pair + 2, 0:64].rearrange(
                                          "p h (e j c) -> p h e j c", e=2, j=TPB // 2),
                                      AX.X, ALU.max).then_inc(s["max_ready"], 1)
                elif e[0] == "out":
                    dve.wait_ge(s["shared_full"], shared_place(ev, n, u) + 1)
                    view = p_shared[:, :].rearrange("p (t h r) -> p t h r", t=QC // P, h=GROUP)
                    dve.reciprocal(rden[:, :, :], view[:, :, :, HD]).then_inc(s["dve_chain"], 1)
                    unit = u - e[2]
                    dve.wait_ge(s["dve_chain"], unit * NQC + e[1] + 1)
                    dve.tensor_tensor(
                        attn[:, ds(unit, 1), 4 * e[1]:4 * e[1] + 4, :].rearrange("p u t (h r) -> p (u t) h r", r=HD),
                        view[:, :, :, 0:HD], rden[:, :, :].unsqueeze(3).to_broadcast([P, QC // P, GROUP, HD]),
                        ALU.mult).then_inc(s["shared_used"], 1)

        def build_stack(eng, u, which=(0, 1)):
            sides = ((qstack, qparts, ((0, 0, 3, 1), (1, 3, 6, 2), (2, 4, 5, 1))),
                     (kstack, kparts, ((0, 2, 5, 1), (1, 1, 6, 4), (2, 0, 1, 1))))
            for stack, parts, places in [sides[i] for i in which]:
                view = stack[:, :, :, 0:PRODUCTS * HD].rearrange("p t g (r c) -> p (t g) r c", c=HD)
                for part, lo, hi, step in places:
                    dst = view[:, :, lo:hi:step, :]
                    src = parts[:, part, ds(u, 1), :, :].rearrange("p u t (g c) -> p (u t g) c", c=HD)
                    last = eng.tensor_copy(dst, src.unsqueeze(2).to_broadcast(list(dst.shape)))
            last.then_inc(s["stack_ready" if 1 in which else "first_queries"], 1)

        def pool_slot(pool, u, par, kind):
            ev, nxt = slot_events(kind), 1 - par
            maxima = "m" in kind
            if maxima:
                if "p" in kind:
                    pool.wait_ge(s["pv_done"], u * NS)
                pool.tensor_copy(vs[nxt][:, :, :, 0:HD],
                                 v[:, 0, ds(u + 1, 1), :, :].rearrange("p u t (g c) -> p (u t) g c", c=HD)
                                 ).then_inc(s["v_ready"], 1)
            more = maxima and not (isinstance(u, int) and u == UNITS - 2)
            for n, e in enumerate(ev):
                if e == ("turn", 3):
                    if more:
                        pool.wait_ge(s["shared_full"], shared_place(ev, ev.index(("turn", 3)), u) + 1)
                        build_stack(pool, u + 2)
                if e[0] == "max":
                    pair = e[1]
                    pool.wait_ge(s["max_ready"], (u + 1) * 2 + pair + 1)
                    base = [(u + 1) * 8 + 4 * pair]

                    def link(ins):
                        ins.then_inc(s["pool_chain"], 1)
                        base[0] = base[0] + 1
                        pool.wait_ge(s["pool_chain"], base[0])
                    cut = shift16[:, pair, :, :, :]
                    own, top = shift0[:, :].unsqueeze(1).to_broadcast([P, 2, TPB]), row_max[:, 2 * pair:2 * pair + 2, :]
                    link(pool.tensor_tensor(shift[:, pair, :, :], own, top, ALU.subtract))
                    link(pool.tensor_tensor(cut[:, :, 0, :], own, top, ALU.subtract))
                    link(pool.tensor_tensor(rest[:, pair, :, :], shift[:, pair, :, :], cut[:, :, 0, :], ALU.subtract))
                    link(pool.tensor_tensor(cut[:, :, 1, :], shift[:, pair, :, :], cut[:, :, 0, :], ALU.subtract))
                    pool.tensor_tensor(cut[:, :, 2, :], rest[:, pair, :, :], cut[:, :, 1, :], ALU.subtract
                                       ).then_inc(s["shift_ready"], 1)

        def sync_slot(sp, u, par, kind):
            ev, nxt = slot_events(kind), 1 - par
            for n, e in enumerate(ev):
                if e[0] == "shift":
                    sp.wait_ge(s["shared_used"], shared_place(ev, n, u) + 1)
                    for h in range(2):
                        at = h * ROWS + SHIFT_ROW
                        sp.dma_start(qt[par if e[2] else nxt][at:at + CROWS, e[1], :],
                                     rows16[e[1]][h * CROWS * TPB:(h + 1) * CROWS * TPB, :]
                                     ).then_inc(rows_loaded[e[1]], 16)

        with nc.Block() as block:
            @block.vector
            def _(dve):
                done = 0
                for rows, stack, value in ((slice(SHIFT_ROW, ROWS), qstack, 0.0),
                                           (slice(ALIBI_ROW, ALIBI_ROW + 2), qstack, 1.0)):
                    dve.memset(stack[:, :, :, rows], value).then_inc(s["preset_dve"], 1)
                    done += 1
                    dve.wait_ge(s["preset_dve"], done)
                dve.memset(block_max[:, :, :], NEG)
                for i in range(2):
                    dve.memset(vs[i][:, :, :, HD + 1:32], 0.0)
                    dve.memset(vs[i][:, :, :, HD:HD + 1], 1.0)

            @block.gpsimd
            def _(pool):
                done = 0
                for ins in (lambda: pool.memset(kstack[:, :, :, SHIFT_ROW:ROWS], 0.0),
                            lambda: pool.memset(kstack[:, :, :, SHIFT_ROW:SHIFT_ROW + 3], 1.0),
                            lambda: pool.memset(shift16[:, :, :, :, :], 0.0),
                            lambda: pool.tensor_copy(kstack[:, :, :, ALIBI_ROW:ALIBI_ROW + 2],
                                                     key_alibi[:, :, :].unsqueeze(2).to_broadcast([P, TPB, GROUP, 2]))):
                    ins().then_inc(s["preset"], 1)
                    done += 1
                    pool.wait_ge(s["preset"], done)
        with nc.Block() as block:
            @block.tensor
            def _(pe):
                slots(tensor_slot)(pe)

            @block.scalar
            def _(act):
                slots(scalar_slot)(act)

            @block.vector
            def _(dve):
                build_stack(dve, 0, which=(0,))
                slots(vector_slot)(dve)

            @block.gpsimd
            def _(pool):
                build_stack(pool, 0, which=(1,))
                slots(pool_slot)(pool)

            @block.sync
            def _(sp):
                slots(sync_slot)(sp)


def project_attention(nc, attn, x, bias, ident, w, stats):
    with ExitStack() as ctx:
        sb = lambda n, s, d=F32: ctx.enter_context(nc.sbuf_tensor("pa_" + n, s, d))
        ps = lambda n, s, d=F32: ctx.enter_context(nc.psum_tensor("pa_" + n, s, d))
        sem = lambda n: ctx.enter_context(nc.semaphore("pa_" + n))
        tile = [sb(f"tile{b}", [P, E]) for b in range(B)]
        turned = [sb(f"turned{b}", [P, EH, P]) for b in range(B)]
        p_turn = [ps(f"p_turn{b}", [P, 512]) for b in range(B)]
        p_proj = [ps(f"p_proj{b}", [P, 512]) for b in range(B)]
        tile_ready, turn_psum, turn_ready, proj_ready, proj_used, biased = (
            sem(n) for n in ("tile_ready", "turn_psum", "turn_ready", "proj_ready", "proj_used", "biased"))

        def x_tile(t, b):
            return x[:, ds(t + b * TPB, 1), :].rearrange("p a e -> p (a e)")

        with nc.Block() as block:
            @block.gpsimd
            def _(pool):
                pool.sem_inc(turn_psum, B)
                pool.sem_inc(proj_used, B)
                with pool.Fori(0, TPB) as t:
                    for b in range(B):
                        pool.wait_ge(turn_psum, t * B + b + 1)
                        pool.tensor_copy(tile[b][:, :].rearrange("p (g c) -> p g c", g=GPB),
                                         attn[:, b * GPB:(b + 1) * GPB, ds(t, 1), :].rearrange("p g t c -> p (g t) c")
                                         ).then_inc(tile_ready, 1)
                        pool.tensor_tensor(x_tile(t, b), x_tile(t, b), bias[:, :], ALU.add).then_inc(biased, 1)

            @block.tensor
            def _(pe):
                with pe.Fori(0, TPB) as t:
                    for b in range(B):
                        pe.wait_ge(tile_ready, t * B + b + 1)
                        for h in range(EH):
                            mm = pe.transpose(p_turn[b][:, h * P:(h + 1) * P], tile[b][:, h * P:(h + 1) * P], ident[:, :])
                        mm.then_inc(turn_psum, 1)
                    for b in range(B):
                        pe.wait_ge(turn_ready, t * B + b + 1)
                        pe.wait_ge(proj_used, t * B + b + 1)
                        for h in range(EH):
                            mm = pe.matmul(p_proj[b][:, 0:E], turned[b][:, h, :], w[:, h, :],
                                           start=h == 0, stop=h == EH - 1)
                        mm.then_inc(proj_ready, 1)

            @block.scalar
            def _(act):
                with act.Fori(0, TPB) as t:
                    for b in range(B):
                        act.wait_ge(turn_psum, t * B + b + 1 + B)
                        act.copy(turned[b][:, :, :], p_turn[b][:, 0:E].rearrange("p (h c) -> p h c", h=EH)
                                 ).then_inc(turn_ready, 1)

            @block.vector
            def _(dve):
                with dve.Fori(0, TPB) as t:
                    for b in range(B):
                        dve.wait_ge(proj_ready, t * B + b + 1)
                        dve.wait_ge(biased, t * B + b + 1)
                        dve.tensor_tensor(x_tile(t, b), p_proj[b][:, 0:E], x_tile(t, b), ALU.add
                                          ).then_inc(proj_used, 1)
                    for b in range(B):
                        dve.wait_ge(proj_used, t * B + (B + b + 1))
                        tile_stats(dve, stats, x, t + b * TPB)


def normalise_and_turn(nc, tag, x, mean, rstd, ident, xt):
    with ExitStack() as ctx:
        sb = lambda n, s, d=F32: ctx.enter_context(nc.sbuf_tensor(tag + n, s, d))
        ps = lambda n, s, d=F32: ctx.enter_context(nc.psum_tensor(tag + n, s, d))
        sem = lambda n: ctx.enter_context(nc.semaphore(tag + n))
        xn = [sb(f"xn{i}", [P, E]) for i in range(8)]
        p_turn = [ps(f"p_turn{i}", [P, 512]) for i in range(4)]
        xn_ready, turned, taken = sem("xn_ready"), sem("turned"), sem("taken")
        with nc.Block() as block:
            @block.vector
            def _(dve):
                dve.sem_inc(turned, 4)
                dve.sem_inc(taken, 4)
                with dve.Fori(0, TILES // 8) as r:
                    for i in range(8):
                        if i % 2 == 0:
                            dve.wait_ge(turned, r * 4 + i // 2 + 1)
                        dve.tensor_scalar(xn[i][:, :], x[:, ds(r * 8 + i, 1), :].rearrange("p a e -> p (a e)"),
                                          mean[:, ds(r * 8 + i, 1)], rstd[:, ds(r * 8 + i, 1)],
                                          ALU.subtract, ALU.mult).then_inc(xn_ready, 1)

            @block.tensor
            def _(pe):
                with pe.Fori(0, TILES // 8) as r:
                    for j in range(4):
                        pe.wait_ge(xn_ready, r * 8 + 2 * j + 2)
                        pe.wait_ge(taken, r * 4 + j + 1)
                        for i in range(2):
                            for h in range(EH):
                                mm = pe.transpose(p_turn[j][:, (h * 2 + i) * P:(h * 2 + i + 1) * P],
                                                  xn[2 * j + i][:, h * P:(h + 1) * P], ident[:, :])
                        mm.then_inc(turned, 1)

            @block.scalar
            def _(act):
                with act.Fori(0, TILES // 8) as r:
                    for j in range(4):
                        act.wait_ge(turned, r * 4 + j + 5)
                        first = 1 + 2 * (j % 2) * P
                        act.copy(xt[:, :, ds(r * 2 + j // 2, 1), first:first + 2 * P].rearrange("p h r c -> p (h r) c"),
                                 p_turn[j][:, :].rearrange("p (h c) -> p h c", h=EH)).then_inc(taken, 1)


EXPERTS, TOPK, HIDDEN, SHARED_HIDDEN = 8, 2, 176, 352
WIDTH = EXPERTS * HIDDEN + SHARED_HIDDEN
MT = -(-WIDTH // P)
TB = 512
NB = B * S // TB
SLICES = EXPERTS + 1


def router_phase(nc, xt, wr, ident, ident16, priority, gates_t):
    with ExitStack() as ctx:
        sb = lambda n, s, d=F32: ctx.enter_context(nc.sbuf_tensor("ro_" + n, s, d))
        ps = lambda n, s, d=F32: ctx.enter_context(nc.psum_tensor("ro_" + n, s, d))
        sem = lambda n: ctx.enter_context(nc.semaphore("ro_" + n))
        logits_t = sb("logits_t", [EXPERTS, NB, TB])
        T3 = [P, TILES, EXPERTS]
        work = {n: sb(n, T3) for n in "gate shifted pick1 pick2 left order kept rest".split()}
        row = {n: sb(n, [P, TILES]) for n in "top sum first top2 first2 total inv".split()}
        parts = sb("parts", [P, TILES, 3, SLICES], BF16)
        p_logits = ps("p_logits", [P, NB, TB])
        p_tok = ps("p_tok", [P, 512])
        p_gates = ps("p_gates", [P, 1024])
        chain_s, logits_ready, logits_in, tok_ready, shifted_ready, exp_ready, parts_ready, gates_ready = (
            sem(n) for n in "chain logits_ready logits_in tok_ready shifted_ready exp_ready parts_ready gates_ready".split())

        def rows(name):
            return row[name][:, :].unsqueeze(2).to_broadcast(T3)

        with nc.Block() as block:
            @block.tensor
            def _(pe):
                for n in range(NB):
                    for h in range(EH):
                        mm = pe.matmul(p_logits[0:EXPERTS, n, :], wr[:, h, :], xt[:, h, n, 1:],
                                       start=h == 0, stop=h == EH - 1)
                mm.then_inc(logits_ready, 1)
                pe.wait_ge(logits_in, 1)
                for t in range(TILES):
                    mm = pe.transpose(p_tok[:, t * EXPERTS:(t + 1) * EXPERTS],
                                      logits_t[:, t // 4, (t % 4) * P:(t % 4 + 1) * P], ident[0:EXPERTS, 0:EXPERTS])
                mm.then_inc(tok_ready, 1)
                pe.wait_ge(parts_ready, 1)
                for t in range(TILES):
                    mm = pe.transpose(p_gates[:, :].bitcast(BF16)[0:3 * SLICES, t * P:(t + 1) * P],
                                      parts[:, t, :, :].rearrange("p a b -> p (a b)"), ident16[:, :])
                mm.then_inc(gates_ready, 1)

            @block.scalar
            def _(act):
                act.wait_ge(logits_ready, 1)
                act.copy(logits_t[:, :, :], p_logits[0:EXPERTS, :, :]).then_inc(logits_in, 1)
                act.wait_ge(shifted_ready, 1)
                act.activation(work["gate"][:, :, :], work["shifted"][:, :, :], ACT.Exp).then_inc(exp_ready, 1)
                act.wait_ge(gates_ready, 1)
                act.copy(gates_t[:, :], p_gates[:, :].bitcast(BF16)[0:3 * SLICES, :])

            @block.vector
            def _(dve):
                c = Chain(dve, chain_s)
                w = {n: t[:, :, :] for n, t in work.items()}
                tok = p_tok[:, 0:TILES * EXPERTS].rearrange("p (t e) -> p t e", e=EXPERTS)
                order = priority[:, :].unsqueeze(1).to_broadcast(T3)

                def pick(values, top, first, out):
                    c.link(dve.tensor_reduce(row[top][:, :], values, AX.X, ALU.max))
                    c.link(dve.tensor_tensor(out, values, rows(top), ALU.is_equal))
                    c.link(dve.tensor_tensor(w["order"], out, order, ALU.mult))
                    c.link(dve.tensor_reduce(row[first][:, :], w["order"], AX.X, ALU.max))
                    c.link(dve.tensor_tensor(out, w["order"], rows(first), ALU.is_equal))

                c.link(dve.memset(parts[:, :, :, :], 0.0))
                c.link(dve.memset(parts[:, :, 0, EXPERTS:SLICES], 1.0))
                dve.wait_ge(tok_ready, 1)
                c.link(dve.tensor_reduce(row["top"][:, :], tok, AX.X, ALU.max))
                dve.tensor_tensor(w["shifted"], tok, rows("top"), ALU.subtract).then_inc(shifted_ready, 1)
                dve.wait_ge(exp_ready, 1)
                c.link(dve.tensor_reduce(row["sum"][:, :], w["gate"], AX.X, ALU.add))
                c.link(dve.reciprocal(row["inv"][:, :], row["sum"][:, :]))
                c.link(dve.tensor_tensor(w["gate"], w["gate"], rows("inv"), ALU.mult))
                pick(w["gate"], "top", "first", w["pick1"])
                c.link(dve.scalar_tensor_tensor(w["left"], w["pick1"], -2.0, w["gate"], ALU.mult, ALU.add))
                pick(w["left"], "top2", "first2", w["pick2"])
                c.link(dve.tensor_tensor(w["pick1"], w["pick1"], w["pick2"], ALU.add))
                c.link(dve.tensor_tensor(w["kept"], w["gate"], w["pick1"], ALU.mult))
                c.link(dve.tensor_reduce(row["total"][:, :], w["kept"], AX.X, ALU.add))
                c.link(dve.tensor_scalar(row["total"][:, :], row["total"][:, :], 1e-20, None, ALU.add))
                c.link(dve.reciprocal(row["inv"][:, :], row["total"][:, :]))
                c.link(dve.tensor_tensor(w["kept"], w["kept"], rows("inv"), ALU.mult))
                c.link(dve.tensor_copy(parts[:, :, 0, 0:EXPERTS], w["kept"]))
                c.link(dve.tensor_tensor(w["rest"], w["kept"], parts[:, :, 0, 0:EXPERTS], ALU.subtract))
                c.link(dve.tensor_copy(parts[:, :, 1, 0:EXPERTS], w["rest"]))
                dve.tensor_tensor(parts[:, :, 2, 0:EXPERTS], w["rest"], parts[:, :, 1, 0:EXPERTS],
                                  ALU.subtract).then_inc(parts_ready, 1)


def moe_phase(nc, x, xt, gates_t, select, w_gate, w_up, w_down, stats):
    with ExitStack() as ctx:
        sb = lambda n, s, d=F32: ctx.enter_context(nc.sbuf_tensor("moe_" + n, s, d))
        ps = lambda n, s, d=F32: ctx.enter_context(nc.psum_tensor("moe_" + n, s, d))
        sem = lambda n: ctx.enter_context(nc.semaphore("moe_" + n))
        act_out = [sb(f"act{i}", [P, TB]) for i in range(2)]
        prod = [sb(f"prod{i}", [P, TB]) for i in range(2)]
        hidden = [sb(f"hidden{i}", [P, TB]) for i in range(2)]
        p_gate, p_up, p_sel = ([ps(f"{n}{i}", [P, TB]) for i in range(2)] for n in ("p_gate", "p_up", "p_sel"))
        p_down = ps("p_down", [P, TB // P, E])
        gate_ready, up_ready, sel_ready, act_ready, prod_ready, hidden_ready, down_ready, down_used = (
            sem(n) for n in "gate_ready up_ready sel_ready act_ready prod_ready hidden_ready down_ready down_used".split())

        def rows(m):
            return min(P, WIDTH - m * P)

        with nc.Block() as block:
            @block.tensor
            def _(pe):
                with pe.Fori(0, NB) as n:
                    def down(m):
                        pe.wait_ge(hidden_ready, n * MT + m + 1)
                        if m == 0:
                            pe.wait_ge(down_used, n + 1)
                        for t in range(TB // P):
                            mm = pe.matmul(p_down[:, t, :], hidden[m % 2][0:rows(m), t * P:(t + 1) * P],
                                           w_down[0:rows(m), m, :], start=m == 0 and t % 2 == 0,
                                           stop=m == MT - 1, skip_group_check=True)
                        mm.then_inc(down_ready, 1)

                    for m in range(MT):
                        k, i = rows(m), m % 2
                        cols = slice(m * P, m * P + k)
                        if m >= 2:
                            pe.wait_ge(hidden_ready, n * MT + m - 1)
                        for bank, w, ready in ((p_gate, w_gate, gate_ready), (p_up, w_up, up_ready)):
                            for h in range(EH):
                                mm = pe.matmul(bank[i][0:k, :], w[:, h, cols],
                                               xt[:, h, ds(n, 1), 1:].rearrange("p n c -> p (n c)"),
                                               start=h == 0, stop=h == EH - 1)
                            mm.then_inc(ready, 1)
                        pe.matmul(p_sel[i][0:k, :], select[:, cols], gates_t[:, ds(n * TB, TB)],
                                  start=True, stop=True).then_inc(sel_ready, 1)
                        if m >= 1:
                            down(m - 1)
                    down(MT - 1)

            @block.scalar
            def _(act):
                with act.Fori(0, NB) as n:
                    for m in range(MT):
                        k, i = rows(m), m % 2
                        act.wait_ge(gate_ready, n * MT + m + 1)
                        if m >= 2:
                            act.wait_ge(prod_ready, n * MT + m - 1)
                        act.activation(act_out[i][0:k, :], p_gate[i][0:k, :], ACT.Silu).then_inc(act_ready, 1)

            @block.vector
            def _(dve):
                dve.sem_inc(down_used, 1)
                with dve.Fori(0, NB) as n:
                    for m in range(MT):
                        k, i = rows(m), m % 2
                        dve.wait_ge(up_ready, n * MT + m + 1)
                        dve.wait_ge(act_ready, n * MT + m + 1)
                        dve.tensor_tensor(prod[i][0:k, :], p_up[i][0:k, :], act_out[i][0:k, :],
                                          ALU.mult).then_inc(prod_ready, 1)
                        dve.wait_ge(prod_ready, n * MT + m + 1)
                        dve.wait_ge(sel_ready, n * MT + m + 1)
                        if m >= 2:
                            dve.wait_ge(down_ready, n * MT + m - 1)
                        dve.tensor_tensor(hidden[i][0:k, :], p_sel[i][0:k, :], prod[i][0:k, :],
                                          ALU.mult).then_inc(hidden_ready, 1)
                    dve.wait_ge(down_ready, n * MT + MT)
                    tiles = x[:, ds(n * 4, 4), :]
                    dve.tensor_tensor(tiles, p_down[:, :, :], tiles, ALU.add).then_inc(down_used, 1)
                    for t in range(TB // P):
                        dve.wait_ge(down_used, n + 2)
                        tile_stats(dve, stats, x, n * (TB // P) + t)


RH, RN = 4, 64
L = 64
KAPPA = float(np.exp(-0.5))
CPB = TB // L
VECTORS = "x_w x_a x_g x_r x_v x_k w0 a0 k_k k_a r_k gn_scale gn_offset".split()
VEC = {n: i for i, n in enumerate(VECTORS + ["keep_a"])}
MIXES = "w a g r v k".split()


def time_mix_phase(nc, xt, vec, weights, head_spread, head_columns, head_ones, chunk_carry, out):
    with ExitStack() as ctx:
        sb = lambda n, s, d=F32: ctx.enter_context(nc.sbuf_tensor("tm_" + n, s, d))
        ps = lambda n, s, d=F32: ctx.enter_context(nc.psum_tensor("tm_" + n, s, d))
        sem = lambda n: ctx.enter_context(nc.semaphore("tm_" + n))
        HT = [P, EH, TB]
        QT = TB // 2
        xx = sb("xx", HT)
        xm = [sb(f"xm{i}", HT) for i in range(2)]
        low_w, low_a, low_g = sb("low_w", [64, TB]), sb("low_a", [64, TB]), sb("low_g", [P, TB])
        cum, kn, sq, up, coef = (sb(n, HT) for n in ("cum", "kn", "sq", "up", "coef"))
        norm = sb("norm", [P, QT])
        down = sb("down", [P, EH, CPB, L + 1])
        p_low = [ps(f"p_low{i}", [P, TB]) for i in range(2)]
        p_full = [ps(f"p_full{i}", HT) for i in range(2)]
        p_sum = ps("p_sum", HT)
        s = {n: sem(n) for n in ("chain mix_ready mix_used low_ready full_ready full_used cum_ready sq_ready "
                                 "small_ready clamp_ready root_ready inv_ready spread_ready spread_used rk_ready "
                                 "bonus_ready bonus_used exp_ready bt_ready at_done scaled").split()}
        full = lambda t: t[:, :, :]
        blk = lambda name, n: out[name][:, :, ds(n, 1), :].rearrange("p h n c -> p (h n) c")
        chunks = lambda t: t.rearrange("p h (c l) -> p h c l", l=L)

        def v_(name, h):
            return vec[:, h, VEC[name]:VEC[name] + 1]

        def half_of(name, h, n):
            return out[name][:, h, ds(n, 1), :].rearrange("p n c -> p (n c)")

        def rounds(step):
            def program(eng):
                step(eng, 0, None)
                with eng.Fori(0, NB - 1) as n:
                    step(eng, n + 1, n)
                step(eng, None, NB - 1)
            return program

        with nc.Block() as block:
            @block.vector
            def _(dve):
                c = Chain(dve, s["chain"])
                for name, count in (("mix_used", 2), ("full_used", 2), ("bonus_used", 1), ("bonus_ready", 1),
                                    ("exp_ready", 2), ("at_done", 1), ("scaled", 1)):
                    dve.sem_inc(s[name], count)
                c.link(dve.memset(down[:, :, :, 0:1], 1.0))
                c.link(dve.memset(xt[:, :, :, 0:1], 0.0))
                c.link(dve.tensor_copy(xt[:, :, 1::2, 0], xt[:, :, 0::2, TB]))
                c.link(dve.tensor_scalar(vec[:, :, VEC["keep_a"]:VEC["keep_a"] + 1], vec[:, :, VEC["k_a"]:VEC["k_a"] + 1],
                                         -1.0, 1.0, ALU.mult, ALU.add))

                def step(front, back):
                    m, n = front, back

                    def mix(i):
                        if m is None:
                            return
                        dve.wait_ge(s["mix_used"], m * 6 + i + 1)
                        for h in range(EH):
                            ins = dve.scalar_tensor_tensor(
                                xm[i % 2][:, h, :], xx[:, h, :], v_("x_" + MIXES[i], h),
                                xt[:, h, ds(m, 1), 1:].rearrange("p n c -> p (n c)"), ALU.mult, ALU.add)
                            if h == 0:
                                c.mark(ins)
                        ins.then_inc(s["mix_ready"], 1)

                    if m is not None:
                        if n is not None:
                            dve.wait_ge(s["mix_ready"], m * 6)
                        c.wait()
                        difference = c.mark(dve.tensor_tensor(
                            full(xx), xt[:, :, ds(m, 1), 0:TB].rearrange("p h n c -> p (h n) c"),
                            xt[:, :, ds(m, 1), 1:].rearrange("p h n c -> p (h n) c"), ALU.subtract))
                    if n is not None:
                        dve.wait_ge(s["exp_ready"], n * 2 + 2)
                        dve.wait_ge(s["full_used"], n * 6 + 3)
                        for h in range(EH):
                            ins = dve.tensor_tensor_scan(cum[:, h, :], chunk_carry[:, :], half_of("bonus", h, n), 0.0,
                                                         ALU.mult, ALU.add)
                            if h == 0:
                                c.mark(ins)
                        ins.then_inc(s["cum_ready"], 1)
                    if m is not None:
                        c.wait(difference)
                    mix(0)
                    mix(1)
                    if n is not None:
                        dve.wait_ge(s["bonus_ready"], n + 1)
                        dve.wait_ge(s["full_used"], n * 6 + 4)
                        for h in range(EH):
                            c.mark(dve.tensor_scalar(coef[:, h, :], half_of("bt", h, n), v_("k_a", h), v_("keep_a", h),
                                                     ALU.mult, ALU.add))
                        dve.wait_ge(s["full_used"], n * 6 + 8)
                        for h in range(EH):
                            c.mark(dve.tensor_scalar(kn[:, h, :], half_of("kt", h, n), v_("k_k", h), None, ALU.mult))
                        c.wait()
                        dve.tensor_tensor(full(sq), full(kn), full(kn), ALU.mult).then_inc(s["sq_ready"], 1)
                        c.mark(dve.tensor_tensor(blk("kt", n), full(coef), blk("kt", n), ALU.mult))
                    mix(2)
                    if n is not None:
                        c.wait()
                        for h in range(EH):
                            ins = dve.scalar_tensor_tensor(coef[:, h, :], half_of("rt", h, n), v_("r_k", h),
                                                           half_of("kt", h, n), ALU.mult, ALU.mult)
                            if h == 0:
                                c.mark(ins)
                        ins.then_inc(s["rk_ready"], 1)
                    mix(3)
                    if n is not None:
                        dve.wait_ge(s["small_ready"], n + 1)
                        dve.tensor_scalar(norm[:, :], p_sum[:, 0, 0:QT], 1e-24, None, ALU.max).then_inc(s["clamp_ready"], 1)
                    mix(4)
                    if n is not None:
                        dve.wait_ge(s["root_ready"], n + 1)
                        dve.reciprocal(norm[:, :], norm[:, :]).then_inc(s["inv_ready"], 1)
                    mix(5)
                    if n is not None:
                        dve.wait_ge(s["spread_ready"], n + 1)
                        dve.tensor_tensor(full(kn), full(kn), full(p_sum), ALU.mult).then_inc(s["spread_used"], 1)
                        dve.wait_ge(s["spread_used"], n + 1)
                        dve.tensor_tensor(blk("bt", n), full(kn), blk("bt", n), ALU.mult).then_inc(s["bt_ready"], 1)
                        dve.wait_ge(s["exp_ready"], n * 2 + 4)
                        for h in range(EH):
                            c.mark(dve.scalar_tensor_tensor(
                                out["at"][:, h, ds(n, 1), :].rearrange("p n (c l) -> p (n c) l", l=L),
                                kn[:, h, :].rearrange("p (c l) -> p c l", l=L), -1.0, down[:, h, :, 0:L],
                                ALU.mult, ALU.mult))
                        c.mark(dve.tensor_copy(out["chunk_decay"][:, :, ds(n, 1), :].rearrange("p h n c -> p (h n) c"),
                                               down[:, :, :, L]))
                        c.wait()
                        dve.sem_inc(s["at_done"], 1)
                        dve.wait_ge(s["bonus_ready"], n + 2)
                        dve.tensor_tensor(blk("bonus", n), full(p_sum), blk("vt", n), ALU.mult).then_inc(s["bonus_used"], 1)

                step(0, None)
                with dve.Fori(0, NB - 1) as n:
                    c.loop(n, 7 + 10)
                    step(n + 1, n)
                c.end(NB - 1)
                step(None, NB - 1)

            @block.gpsimd
            def _(pool):
                with pool.Fori(0, NB) as n:
                    pool.wait_ge(s["exp_ready"], n * 2 + 4)
                    pool.wait_ge(s["rk_ready"], n + 1)
                    pool.tensor_tensor(chunks(blk("rt", n)), chunks(blk("rt", n)), down[:, :, :, 1:], ALU.mult)
                    pool.tensor_tensor(blk("kt", n), blk("kt", n), full(up), ALU.mult)
                    pool.wait_ge(s["bt_ready"], n + 1)
                    pool.tensor_tensor(blk("bt", n), blk("bt", n), full(up), ALU.mult).then_inc(s["scaled"], 1)

            def tensor_step(pe, m, n):
                def first(i):
                    if m is None:
                        return
                    name = MIXES[i]
                    pe.wait_ge(s["mix_ready"], m * 6 + i + 1)
                    if i < 3:
                        rows = {"w": 64, "a": 64, "g": P}[name]
                        for h in range(EH):
                            mm = pe.matmul(p_low[i % 2][0:rows, :], weights[name + "1"][:, h, :], xm[i % 2][:, h, :],
                                           start=h == 0, stop=h == EH - 1)
                    else:
                        pe.wait_ge(s["full_used"], m * 6 + i + 1)
                        for o in range(EH):
                            for h in range(EH):
                                mm = pe.matmul(p_full[i % 2][:, o, :], weights[name][:, h, o * P:(o + 1) * P],
                                               xm[i % 2][:, h, :], start=h == 0, stop=h == EH - 1)
                    mm.then_inc(s["mix_used"], 1)

                def second(i):
                    if m is None:
                        return
                    pe.wait_ge(s["low_ready"], m * 3 + i + 1)
                    pe.wait_ge(s["full_used"], m * 6 + i + 1)
                    low, w = ((low_w, weights["w2"]), (low_a, weights["a2"]), (low_g, weights["g2"]))[i]
                    for o in range(EH):
                        mm = pe.matmul(p_full[i % 2][:, o, :], w[:, o * P:(o + 1) * P], low[:, :], start=True, stop=True)
                    mm.then_inc(s["full_ready"], 1)

                first(0)
                first(1)
                if n is not None:
                    pe.wait_ge(s["sq_ready"], n + 1)
                    pe.wait_ge(s["bonus_used"], n + 1)
                    for h in range(EH):
                        for j in range(2):
                            g = 32 * (2 * h + j)
                            mm = pe.matmul(p_sum[g:g + 32, 0, 0:QT], head_columns[:, :], sq[:, h, j * QT:(j + 1) * QT],
                                           start=True, stop=True, skip_group_check=True)
                    mm.then_inc(s["small_ready"], 1)
                second(0)
                first(2)
                second(1)
                second(2)
                if n is not None:
                    pe.wait_ge(s["inv_ready"], n + 1)
                    for h in range(EH):
                        for j in range(2):
                            mm = pe.matmul(p_sum[:, h, j * QT:(j + 1) * QT], head_spread[:, 2 * h + j, :], norm[:, :],
                                           start=True, stop=True, skip_group_check=True)
                    mm.then_inc(s["spread_ready"], 1)
                first(3)
                if n is not None:
                    pe.wait_ge(s["spread_used"], n + 1)
                    pe.wait_ge(s["rk_ready"], n + 1)
                    for o in range(EH):
                        mm = pe.matmul(p_sum[:, o, :], head_ones[:, :], coef[:, o, :], start=True, stop=True)
                    mm.then_inc(s["bonus_ready"], 1)
                first(4)
                first(5)

            @block.tensor
            def _(pe):
                rounds(tensor_step)(pe)

            def scalar_step(act, m, n):
                def low(i, dst, func):
                    act.wait_ge(s["mix_used"], m * 6 + i + 3)
                    src = p_low[i % 2][0:dst.shape[0], :]
                    ins = act.copy(dst[:, :], src) if func is None else act.activation(dst[:, :], src, func)
                    ins.then_inc(s["low_ready"], 1)

                def take(i, dst, bias=None):
                    if i < 3:
                        act.wait_ge(s["full_ready"], m * 3 + i + 1)
                    else:
                        act.wait_ge(s["mix_used"], m * 6 + i + 3)
                    if bias is None:
                        act.copy(blk(dst, m), p_full[i % 2][:, :, :]).then_inc(s["full_used"], 1)
                    else:
                        act.activation(half_of(dst, 0, m), p_full[i % 2][:, 0, :], ACT.Sigmoid, bias=v_(bias, 0))
                        act.activation(half_of(dst, 1, m), p_full[i % 2][:, 1, :], ACT.Sigmoid, bias=v_(bias, 1)
                                       ).then_inc(s["full_used"], 1)

                if n is not None:
                    act.wait_ge(s["cum_ready"], n + 1)
                    act.wait_ge(s["at_done"], n + 1)
                    act.wait_ge(s["scaled"], n + 1)
                    for h in range(EH):
                        ins = act.activation(down[:, h, :, 1:], cum[:, h, :].rearrange("p (c l) -> p c l", l=L),
                                             ACT.Exp, scale=-KAPPA)
                    ins.then_inc(s["exp_ready"], 1)
                    act.activation(full(up), full(cum), ACT.Exp, scale=KAPPA).then_inc(s["exp_ready"], 1)
                if m is not None:
                    low(0, low_w, ACT.Tanh)
                    low(1, low_a, None)
                    take(0, "bonus", "w0")
                    low(2, low_g, ACT.Sigmoid)
                    take(1, "bt", "a0")
                if n is not None:
                    act.wait_ge(s["clamp_ready"], n + 1)
                    act.activation(norm[:, :], norm[:, :], ACT.Sqrt).then_inc(s["root_ready"], 1)
                if m is not None:
                    take(2, "gt")
                    take(3, "rt")
                    take(4, "vt")
                    take(5, "kt")

            @block.scalar
            def _(act):
                rounds(scalar_step)(act)


LEVELS = [1 << i for i in range(L.bit_length() - 1)]
HALF_CHUNKS = P // L


def marks_of(*names):
    return {n: i + 1 for i, n in enumerate(names)} | {"each": len(names)}


INNER = [m for m in LEVELS if m > 1]
PE_MARKS = marks_of("turn", "a1", "a2", "a3", "w0", *[f"{k}{m}" for m in INNER for k in ("z", "xz", "zy")
                                                      if not (k == "xz" and m == INNER[-1])],
                    "ta", "r", "yv", "gh0", "gh1")
DVE_MARKS = marks_of("a1e", "a1o", "a2e", "a2o", "x1e", "x1o", "x1",
                     *[f"{k}{m}" for m in INNER for k in ("z", "x", "y") if not (k == "x" and m == INNER[-1])],
                     "r", "gh0", "d0a", "d0", "g0", "gh1", "d1a", "d1", "g1")
ACT_MARKS = marks_of("tok", "w0", "ta", "yp")
HOP_MADE = marks_of("ys0", "hop0", "ys1", "hop1")
HOP_DONE = marks_of("s0a", "s0", "s1a", "s1")


def recurrence_phase(nc, data, ident, masks, level_masks, level1_t, head_ones, yt):
    with ExitStack() as ctx:
        sb = lambda n, s, d=F32: [ctx.enter_context(nc.sbuf_tensor(f"rc_{n}{b}", s, d)) for b in range(B)]
        sem = lambda n: [ctx.enter_context(nc.semaphore(f"rc_{n}{b}")) for b in range(B)]
        bank = [[ctx.enter_context(nc.psum_tensor(f"rc_bank{b}_{i}", [P, 512], F32)) for i in range(4)] for b in range(B)]
        bt, kt, vt = sb("bt", [P, EH, P]), sb("kt", [P, EH, P]), sb("vt", [P, EH, P])
        ar = sb("ar", [P, EH, 2 * P])
        tok_b, tok_k, tok_v = sb("tok_b", [P, E]), sb("tok_k", [P, E]), sb("tok_v", [P, E])
        aw = sb("aw", [P, RH, 2 * RN])
        ab = sb("ab", [P, 2, EH, 2, P])
        ak = sb("ak", [P, 2, EH, 2, P])
        X, Y, Z = sb("X", [P, RH, P]), sb("Y", [P, RH, P]), sb("Z", [P, RH, P])
        ta = sb("ta", [P, EH, 2, P])
        rh, y_own = sb("rh", [P, EH, P]), sb("y_own", [P, EH, P])
        gh = [sb(f"gh{c}_", [P, EH, 2, P]) for c in range(2)]
        state = [sb(f"state{c}_", [P, EH, P]) for c in range(2)]
        made, dve_did, act_did, staged = sem("made"), sem("dve_did"), sem("act_did"), sem("staged")
        y1_made, tok_seen = sem("y1_made"), sem("tok_seen")
        hop_made, hop_done, y_out = sem("hop_made"), sem("hop_done"), sem("y_out")

        def flat(t):
            return t[:, :, :, :].rearrange("p h n c -> p h (n c)")

        def src(name, t, b):
            return flat(data[name])[:, :, ds(t * P + b * S, P)]

        def pe_wait(pe, t, b, dve=None, act=None):
            if dve:
                pe.wait_ge(dve_did[b], t * DVE_MARKS["each"] + DVE_MARKS[dve])
            if act:
                pe.wait_ge(act_did[b], t * ACT_MARKS["each"] + ACT_MARKS[act])

        def hop_wait(eng, sem_, marks, t, b, name):
            eng.wait_ge(sem_[b], (t - 1) * marks["each"] + marks[name] + (sem_ is hop_done))

        def last(t):
            return isinstance(t, int) and t == TPB

        def decay_at(t, b, c):
            return ds(t * HALF_CHUNKS + (b * S // L + c), 1)

        def rounds(stages, carried):
            def program(eng):
                def run(t, skip, only):
                    for stage in stages:
                        if not (skip and stage in carried) and not (only and stage not in carried):
                            for b in range(B):
                                stage(t, b)
                run(0, True, False)
                with eng.Fori(0, TPB - 1) as r:
                    run(r + 1, False, False)
                run(TPB, False, True)
            return program

        def heads():
            return [(h, h // 2, h % 2) for h in range(RH)]

        def head_rows(par):
            return slice(par * RN, par * RN + RN)

        with nc.Block() as block:
            @block.tensor
            def _(pe):
                def turn(t, b):
                    pe.wait_ge(staged[b], t + 1)
                    if not isinstance(t, int):
                        pe.wait_ge(dve_did[b], t * DVE_MARKS["each"])
                        pe.wait_ge(act_did[b], t * ACT_MARKS["each"])
                    for n, (a, c) in enumerate(((bt, kt), (ar, vt))):
                        for h in range(EH):
                            pe.transpose(bank[b][n][:, h * P:(h + 1) * P], a[b][:, h, 0:P], ident[:, :])
                            mm = pe.transpose(bank[b][n][:, (2 + h) * P:(3 + h) * P], c[b][:, h, :], ident[:, :])
                    mm.then_inc(made[b], 1)

                def against(rows_of, banks, width, rhs):
                    def stage(t, b):
                        for h, half, par in heads():
                            r = head_rows(par)
                            mm = pe.matmul(bank[b][banks[par]][:, half * width:(half + 1) * width],
                                           rows_of[b][r, half, 0:P], rhs[b][r, half, 0:width],
                                           start=True, stop=True, skip_group_check=True)
                        mm.then_inc(made[b], 1)
                    return stage

                def against_own(rows_of, banks):
                    def stage(t, b):
                        for half in range(EH):
                            for par, c in ((0, 0), (1, 1), (1, 0), (0, 1)):
                                r, cols = head_rows(par), slice(c * L, (c + 1) * L)
                                mm = pe.matmul(bank[b][banks[par]][cols, half * 2 * L:(half + 1) * 2 * L],
                                               rows_of[b][r, half, cols],
                                               ar[b][r, half, :].rearrange("p (k c) -> p k c", k=2)[:, :, cols],
                                               start=True, stop=True, skip_group_check=True)
                        mm.then_inc(made[b], 1)
                    return stage

                def a1(t, b):
                    against_own(bt, (2, 3))(t, b)

                def a2(t, b):
                    pe_wait(pe, t, b, act="tok")
                    pe.sem_inc(tok_seen[b], 1)
                    against_own(kt, (0, 1))(t, b)

                def a3(t, b):
                    pe_wait(pe, t, b, dve="a1o")
                    against(ar, (2, 3), P, bt)(t, b)

                def per_head(n, lhs, rhs, width=P):
                    def stage(t, b):
                        for h, half, par in heads():
                            mm = pe.matmul(bank[b][n][:, h * width:(h + 1) * width], lhs(b, h, half, par),
                                           rhs(b, h, half, par), start=True, stop=True)
                        mm.then_inc(made[b], 1)
                    return stage

                def w0(t, b):
                    pe_wait(pe, t, b, dve="a2o")
                    per_head(0, lambda b, h, half, par: ak[b][:, par, half, 0, :],
                             lambda b, h, half, par: tok_v[b][:, h * RN:(h + 1) * RN], RN)(t, b)

                def z(m):
                    def stage(t, b):
                        pe_wait(pe, t, b, dve="x1" if m == 2 else f"x{m // 2}")
                        per_head(1, lambda b, h, half, par: ab[b][:, par, half, 0, :],
                                 lambda b, h, half, par: X[b][:, h, :])(t, b)
                    return stage

                def xz(m):
                    def stage(t, b):
                        if m == INNER[0]:
                            pe.wait_ge(y1_made[b], 2 * t + 2)
                        pe_wait(pe, t, b, dve=f"z{m}")
                        per_head(2, lambda b, h, half, par: Y[b][:, h, :], lambda b, h, half, par: Z[b][:, h, :])(t, b)
                    return stage

                def zy(m):
                    def stage(t, b):
                        pe_wait(pe, t, b, dve=f"z{m}")
                        per_head(3, lambda b, h, half, par: Z[b][:, h, :], lambda b, h, half, par: Y[b][:, h, :])(t, b)
                    return stage

                def ta_(t, b):
                    pe_wait(pe, t, b, dve=f"y{INNER[-1]}", act="w0")
                    if not isinstance(t, int):
                        pe.wait_ge(y_out[b], t)
                    per_head(0, lambda b, h, half, par: Y[b][:, h, :], lambda b, h, half, par: aw[b][:, h, :])(t, b)

                def r_(t, b):
                    pe_wait(pe, t, b, act="ta")
                    for h, half, par in heads():
                        mm = pe.matmul(bank[b][1][head_rows(par), half * P:(half + 1) * P],
                                       ta[b][:, half, 0, head_rows(par)], ab[b][:, par, half, 1, :],
                                       start=half == 0, stop=True, skip_group_check=True)
                    mm.then_inc(made[b], 1)

                def yv(t, b):
                    for h, half, par in heads():
                        out = bank[b][2][head_rows(par), half * P:(half + 1) * P]
                        pe.matmul(out, ta[b][:, half, 1, head_rows(par)], ab[b][:, par, half, 1, :],
                                  start=half == 0, stop=False, skip_group_check=True)
                        mm = pe.matmul(out, tok_v[b][:, h * RN:(h + 1) * RN], ak[b][:, par, half, 1, :],
                                       start=False, stop=True, skip_group_check=True)
                    mm.then_inc(made[b], 1)

                def gh_(c):
                    def stage(t, b):
                        dst, rows = bank[b][(3, 0)[c]], slice(c * L, (c + 1) * L)
                        for half in range(EH):
                            cols = slice(half * P, (half + 1) * P)
                            at = half * 2 * P
                            pe.matmul(dst[:, at:at + P], ta[b][rows, half, 0, :], tok_b[b][rows, cols],
                                      start=True, stop=True)
                            pe.matmul(dst[:, at + P:at + 2 * P], tok_b[b][rows, cols], ta[b][rows, half, 1, :],
                                      start=True, stop=False)
                            mm = pe.matmul(dst[:, at + P:at + 2 * P], tok_k[b][rows, cols], tok_v[b][rows, cols],
                                           start=False, stop=True)
                        mm.then_inc(made[b], 1)
                    return stage

                def ys(c):
                    def stage(t, b):
                        if c == 0:
                            if last(t):
                                pe.wait_ge(dve_did[b], t * DVE_MARKS["each"])
                            else:
                                pe_wait(pe, t, b, act="w0")
                            pe.wait_ge(hop_done[b], (t - 1) * HOP_DONE["each"] + 1)
                        else:
                            hop_wait(pe, hop_done, HOP_DONE, t, b, "s0")
                        for half in range(EH):
                            mm = pe.matmul(bank[b][0][:, half * P + c * L:half * P + (c + 1) * L],
                                           state[c][b][:, half, :], rh[b][:, half, c * L:(c + 1) * L],
                                           start=True, stop=True, skip_group_check=True)
                        mm.then_inc(hop_made[b], 1)
                    return stage

                def hop(c):
                    def stage(t, b):
                        for half in range(EH):
                            mm = pe.matmul(bank[b][0][:, (EH + half) * P:(EH + half + 1) * P], gh[c][b][:, half, 0, :],
                                           state[c][b][:, half, :], start=True, stop=True, skip_group_check=True)
                        mm.then_inc(hop_made[b], 1)
                    return stage

                ys0, hop0, ys1, hop1 = ys(0), hop(0), ys(1), hop(1)
                stages = [turn, a1, a2, a3, w0]
                for m in INNER:
                    stages += [z(m), zy(m)] if m == INNER[-1] else [z(m), xz(m), zy(m)]
                    stages += {INNER[0]: [ys0, hop0], INNER[2]: [ys1, hop1]}.get(m, [])

                stages += [ta_, r_, yv, gh_(0), gh_(1)]
                rounds(stages, (ys0, hop0, ys1, hop1))(pe)

            @block.vector
            def _(dve):
                def did(b, ins):
                    ins.then_inc(dve_did[b], 1)

                def own(t, b, name):
                    dve.wait_ge(dve_did[b], t * DVE_MARKS["each"] + DVE_MARKS[name])

                def need(t, b, name):
                    dve.wait_ge(made[b], t * PE_MARKS["each"] + PE_MARKS[name])

                def masked(stage_name, dst, banks):
                    def stage(t, b):
                        need(t, b, stage_name)
                        spread = [P, 2, HALF_CHUNKS, L]
                        for par in range(2):
                            for half in range(EH):
                                ins = dve.tensor_tensor(
                                    dst[b][:, par, half, :, :].rearrange("p k (c l) -> p k c l", l=L),
                                    bank[b][banks[par]][:, half * 2 * L:(half + 1) * 2 * L].rearrange(
                                        "p (k l) -> p k l", k=2).unsqueeze(2).to_broadcast(spread),
                                    masks[:, :].rearrange("p (k c l) -> p k c l", k=2, l=L), ALU.mult)
                                if half == EH - 1:
                                    did(b, ins)
                    return stage

                eye = ident[:, :].unsqueeze(1).to_broadcast([P, RH, P])

                def x1(t, b):
                    need(t, b, "a3")
                    for par in range(2):
                        did(b, dve.tensor_tensor(
                            X[b][:, par::2, :], bank[b][2 + par][:, 0:2 * P].rearrange("p (h c) -> p h c", h=EH),
                            level_masks[:, 0, :].unsqueeze(1).to_broadcast([P, EH, P]), ALU.mult))
                    own(t, b, "x1o")
                    did(b, dve.tensor_tensor(X[b][:, :, :], X[b][:, :, :], eye, ALU.add))

                def z(m):
                    def stage(t, b):
                        need(t, b, f"z{m}")
                        did(b, dve.tensor_tensor(
                            Z[b][:, :, :], bank[b][1][:, :].rearrange("p (h c) -> p h c", h=RH),
                            level_masks[:, LEVELS.index(m), :].unsqueeze(1).to_broadcast([P, RH, P]), ALU.mult))
                    return stage

                def grow(kind, buf, n, m):
                    def stage(t, b):
                        need(t, b, {"x": "xz", "y": "zy"}[kind] + str(m))
                        did(b, dve.tensor_tensor(buf[b][:, :, :], bank[b][n][:, :].rearrange("p (h c) -> p h c", h=RH),
                                                 buf[b][:, :, :], ALU.add))
                    return stage

                def r_(t, b):
                    need(t, b, "r")
                    did(b, dve.tensor_tensor(rh[b][:, :, :], bank[b][1][:, 0:2 * P].rearrange("p (h c) -> p h c", h=EH),
                                             src("rt", t, b), ALU.add))

                def gh_(c):
                    def stage(t, b):
                        need(t, b, f"gh{c}")
                        made_here = bank[b][(3, 0)[c]][:, :].rearrange("p (h k c) -> p h k c", h=EH, k=2)
                        did(b, dve.tensor_tensor(gh[c][b][:, :, 0, :], made_here[:, :, 0, :],
                                                 head_ones[:, :].unsqueeze(1).to_broadcast([P, EH, P]), ALU.mult))
                        for half in range(EH):
                            did(b, dve.scalar_tensor_tensor(
                                gh[c][b][:, half, 1, :], made_here[:, half, 1, :],
                                flat(data["chunk_decay"])[:, half, decay_at(t, b, c)], head_ones[:, :],
                                ALU.mult, ALU.mult))
                        own(t, b, f"gh{c}")
                        did(b, dve.tensor_tensor(gh[c][b][:, :, 0, :], gh[c][b][:, :, 0, :],
                                                 ident[:, :].unsqueeze(1).to_broadcast([P, EH, P]), ALU.add))
                    return stage

                def advance(c):
                    def stage(t, b):
                        hop_wait(dve, hop_made, HOP_MADE, t, b, f"hop{c}")
                        for half in range(EH):
                            dve.scalar_tensor_tensor(
                                state[1 - c][b][:, half, :], bank[b][0][:, (EH + half) * P:(EH + half + 1) * P],
                                flat(data["chunk_decay"])[:, half, decay_at(t - 1, b, c)], gh[c][b][:, half, 1, :],
                                ALU.mult, ALU.add).then_inc(hop_done[b], 1)
                        if c == 1:
                            dve.wait_ge(act_did[b], t * ACT_MARKS["each"])
                            dve.tensor_tensor(flat(yt)[:, :, ds((t - 1) * P + b * S, P)],
                                              bank[b][0][:, 0:2 * P].rearrange("p (h c) -> p h c", h=EH),
                                              y_own[b][:, :, :], ALU.add).then_inc(y_out[b], 1)
                    return stage

                adv0, adv1 = advance(0), advance(1)
                stages = [masked("a1", ab, (2, 3)), masked("a2", ak, (0, 1)), x1]
                for m in INNER:
                    stages.append(z(m))
                    if m != INNER[-1]:
                        stages.append(grow("x", X, 2, m))
                    stages.append(grow("y", Y, 3, m))
                    stages += {INNER[0]: [adv0], INNER[2]: [adv1]}.get(m, [])
                stages += [r_, gh_(0), gh_(1)]
                rounds(stages, (adv0, adv1))(dve)

            @block.scalar
            def _(act):
                def need(t, b, name):
                    act.wait_ge(made[b], t * PE_MARKS["each"] + PE_MARKS[name])

                def tok(t, b):
                    need(t, b, "turn")
                    act.copy(tok_b[b][:, :], bank[b][0][:, 0:E])
                    act.copy(tok_k[b][:, :], bank[b][0][:, E:2 * E])
                    act.copy(aw[b][:, :, 0:RN], bank[b][1][:, 0:E].rearrange("p (h c) -> p h c", h=RH))
                    act.copy(tok_v[b][:, :], bank[b][1][:, E:2 * E]).then_inc(act_did[b], 1)

                def w0(t, b):
                    need(t, b, "w0")
                    act.copy(aw[b][:, :, RN:2 * RN], bank[b][0][:, 0:E].rearrange("p (h c) -> p h c", h=RH)
                             ).then_inc(act_did[b], 1)

                def ta_(t, b):
                    need(t, b, "ta")
                    for half in range(EH):
                        ins = act.copy(ta[b][:, half, :, :].rearrange("p k (q c) -> p q k c", q=2),
                                       bank[b][0][:, half * 2 * P:(half + 1) * 2 * P].rearrange(
                                           "p (q k c) -> p q k c", q=2, k=2))
                    ins.then_inc(act_did[b], 1)

                def y_(t, b):
                    need(t, b, "yv")
                    act.copy(y_own[b][:, :, :], bank[b][2][:, 0:2 * P].rearrange("p (h c) -> p h c", h=EH)
                             ).then_inc(act_did[b], 1)

                with act.Fori(0, TPB) as t:
                    for stage in (tok, w0, ta_, y_):
                        for b in range(B):
                            stage(t, b)

            @block.gpsimd
            def _(pool):
                def stage(t, b):
                    pool.tensor_copy(ar[b][:, :, 0:P], src("at", t, b))
                    pool.tensor_copy(ar[b][:, :, P:2 * P], src("rt", t, b))
                    pool.tensor_copy(vt[b][:, :, :], src("vt", t, b))
                    pool.tensor_copy(kt[b][:, :, :], src("kt", t, b))
                    pool.tensor_copy(bt[b][:, :, :], src("bt", t, b)).then_inc(staged[b], 1)

                for b in range(B):
                    pool.memset(state[0][b][:, :, :], 0.0).then_inc(hop_done[b], 1)
                    stage(0, b)

                def y1(t, b):
                    pool.wait_ge(dve_did[b], t * DVE_MARKS["each"] + DVE_MARKS["a1o"])
                    if not isinstance(t, int):
                        pool.wait_ge(made[b], (t - 1) * PE_MARKS["each"] + PE_MARKS["ta"])
                    pool.tensor_tensor(
                        Y[b][:, :, :].rearrange("p (h q) c -> p q h c", q=2), ab[b][:, :, :, 0, :],
                        level1_t[:, :].unsqueeze(1).unsqueeze(1).to_broadcast([P, 2, EH, P]), ALU.mult
                        ).then_inc(y1_made[b], 1)
                    pool.wait_ge(y1_made[b], 2 * t + 1)
                    pool.tensor_tensor(Y[b][:, :, :], Y[b][:, :, :],
                                       ident[:, :].unsqueeze(1).to_broadcast([P, RH, P]), ALU.add
                                       ).then_inc(y1_made[b], 1)

                for b in range(B):
                    y1(0, b)
                with pool.Fori(0, TPB - 1) as t:
                    for b in range(B):
                        pool.wait_ge(made[b], t * PE_MARKS["each"] + PE_MARKS["a3"])
                        stage(t + 1, b)
                    for b in range(B):
                        y1(t + 1, b)


def gate_and_project(nc, data, vec, w, x, stats):
    with ExitStack() as ctx:
        sb = lambda n, s, d=F32: ctx.enter_context(nc.sbuf_tensor("gp_" + n, s, d))
        ps = lambda n, s, d=F32: ctx.enter_context(nc.psum_tensor("gp_" + n, s, d))
        sem = lambda n: ctx.enter_context(nc.semaphore("gp_" + n))
        gated = [sb(f"gated{i}", [P, EH, TB]) for i in range(2)]
        p_proj = [ps(f"p_proj{i}", [P, TB // P, E]) for i in range(2)]
        scaled_ready, gated_ready, proj_ready, proj_used = (
            sem(n) for n in "scaled_ready gated_ready proj_ready proj_used".split())

        def rows(name, h, n):
            return data[name][:, h, ds(n, 1), :].rearrange("p n c -> p (n c)")

        def v_(name, h):
            return vec[:, h, VEC[name]:VEC[name] + 1]

        with nc.Block() as block:
            @block.vector
            def _(dve):
                dve.sem_inc(proj_ready, 2)
                with dve.Fori(0, NB // 2) as r:
                    for i in range(2):
                        n = r * 2 + i
                        dve.wait_ge(proj_ready, r * 2 + i + 1)
                        for h in range(EH):
                            dve.scalar_tensor_tensor(gated[i][:, h, :], rows("yt", h, n), v_("gn_scale", h),
                                                     rows("bonus", h, n), ALU.mult, ALU.add).then_inc(scaled_ready, 1)
                        for h in range(EH):
                            dve.wait_ge(scaled_ready, (r * 2 + i) * EH + h + 1)
                            dve.scalar_tensor_tensor(gated[i][:, h, :], gated[i][:, h, :], v_("gn_offset", h),
                                                     rows("gt", h, n), ALU.add, ALU.mult).then_inc(gated_ready, 1)
                    for i in range(2):
                        dve.wait_ge(proj_ready, r * 2 + i + 3)
                        tiles = x[:, ds((r * 2 + i) * (TB // P), TB // P), :]
                        dve.tensor_tensor(tiles, p_proj[i][:, :, :], tiles, ALU.add).then_inc(proj_used, 1)
                        for t in range(TB // P):
                            dve.wait_ge(proj_used, r * 2 + i + 3)
                            tile_stats(dve, stats, x, (r * 2 + i) * (TB // P) + t)

            @block.tensor
            def _(pe):
                pe.sem_inc(proj_used, 2)
                with pe.Fori(0, NB // 2) as r:
                    for i in range(2):
                        pe.wait_ge(gated_ready, (r * 2 + i + 1) * EH)
                        pe.wait_ge(proj_used, r * 2 + i + 1)
                        for t in range(TB // P):
                            for h in range(EH):
                                mm = pe.matmul(p_proj[i][:, t, :], gated[i][:, h, t * P:(t + 1) * P], w[:, h, :],
                                               start=h == 0 and t % 2 == 0, stop=h == EH - 1, skip_group_check=True)
                        mm.then_inc(proj_ready, 1)


FFN = 2 * E
FT = FFN // P
TIE = 2.0 ** -25


def switch_phase(nc, xt, w_switch, ident, masks):
    with ExitStack() as ctx:
        sb = lambda n, s, d=F32: ctx.enter_context(nc.sbuf_tensor("sw_" + n, s, d))
        ps = lambda n, s, d=F32: ctx.enter_context(nc.psum_tensor("sw_" + n, s, d))
        sem = lambda n: ctx.enter_context(nc.semaphore("sw_" + n))
        logits_t = sb("logits_t", [2, NB, TB])
        tok = sb("tok", [P, TILES, 2])
        lead = sb("lead", [P, TILES])
        p_logits = ps("p_logits", [P, NB, TB])
        p_tok = ps("p_tok", [P, 512])
        logits_ready, logits_in, tok_ready, chain_s = (sem(n) for n in "logits_ready logits_in tok_ready chain".split())
        with nc.Block() as block:
            @block.tensor
            def _(pe):
                for n in range(NB):
                    for h in range(EH):
                        mm = pe.matmul(p_logits[0:2, n, :], w_switch[:, h, :], xt[:, h, n, 1:],
                                       start=h == 0, stop=h == EH - 1)
                mm.then_inc(logits_ready, 1)
                pe.wait_ge(logits_in, 1)
                for t in range(TILES):
                    mm = pe.transpose(p_tok[:, t * 2:(t + 1) * 2],
                                      logits_t[:, t // 4, (t % 4) * P:(t % 4 + 1) * P], ident[0:2, 0:2])
                mm.then_inc(tok_ready, 1)

            @block.scalar
            def _(act):
                act.wait_ge(logits_ready, 1)
                act.copy(logits_t[:, :, :], p_logits[0:2, :, :]).then_inc(logits_in, 1)

            @block.vector
            def _(dve):
                c = Chain(dve, chain_s)
                dve.wait_ge(tok_ready, 1)
                c.link(dve.tensor_copy(tok[:, :, :].rearrange("p t e -> p (t e)"), p_tok[:, 0:2 * TILES]))
                c.link(dve.tensor_tensor(lead[:, :], tok[:, :, 1], tok[:, :, 0], ALU.subtract))
                dve.tensor_scalar(masks[:, :, 1], lead[:, :], TIE, None, ALU.is_gt)
                dve.tensor_scalar(masks[:, :, 0], lead[:, :], TIE, None, ALU.is_le)


def switched_ffn_phase(nc, x, xt, masks, w_in, b_in, w_out, b_out, out):
    with ExitStack() as ctx:
        sb = lambda n, s, d=F32: ctx.enter_context(nc.sbuf_tensor("ff_" + n, s, d))
        ps = lambda n, s, d=F32: ctx.enter_context(nc.psum_tensor("ff_" + n, s, d))
        sem = lambda n: ctx.enter_context(nc.semaphore("ff_" + n))
        hidden = [sb(f"hidden{i}", [P, TB]) for i in range(2)]
        p_in = [ps(f"p_in{i}", [P, TB]) for i in range(2)]
        p_out = [ps(f"p_out{e}", [P, TB // P, E]) for e in range(2)]
        in_ready, hidden_ready, out_ready, out_used, chain_s, stored = (
            sem(n) for n in "in_ready hidden_ready out_ready out_used chain stored".split())
        HT = 2 * FT
        TPN = TB // P

        with nc.Block() as block:
            @block.sync
            def _(sp):
                with sp.Fori(0, NB) as n:
                    sp.wait_ge(out_used, n * 2 + 4)
                    sp.dma_start(out.rearrange("(t p) e -> p t e", p=P)[:, ds(n * TPN, TPN), :],
                                 x[:, ds(n * TPN, TPN), :]).then_inc(stored, 16)
                sp.wait_ge(stored, NB * 16)

            @block.tensor
            def _(pe):
                pe.sem_inc(out_used, 2)
                with pe.Fori(0, NB) as n:
                    def out(m):
                        e = m // FT
                        pe.wait_ge(hidden_ready, n * HT + m + 1)
                        if m % FT == 0:
                            pe.wait_ge(out_used, n * 2 + e + 1)
                        for t in range(TPN):
                            mm = pe.matmul(p_out[e][:, t, :], hidden[m % 2][:, t * P:(t + 1) * P], w_out[:, m, :],
                                           start=m % FT == 0 and t % 2 == 0, stop=m % FT == FT - 1,
                                           skip_group_check=True)
                        mm.then_inc(out_ready, 1)

                    for m in range(HT):
                        if m >= 2:
                            pe.wait_ge(hidden_ready, n * HT + m - 1)
                        for h in range(EH):
                            mm = pe.matmul(p_in[m % 2][:, :], w_in[:, h, m * P:(m + 1) * P],
                                           xt[:, h, ds(n, 1), 1:].rearrange("p n c -> p (n c)"),
                                           start=h == 0, stop=h == EH - 1)
                        mm.then_inc(in_ready, 1)
                        if m >= 1:
                            out(m - 1)
                    out(HT - 1)

            @block.scalar
            def _(act):
                act.sem_inc(out_ready, 2)
                with act.Fori(0, NB) as n:
                    for m in range(HT):
                        act.wait_ge(in_ready, n * HT + m + 1)
                        act.wait_ge(out_ready, n * HT + m + 1)
                        act.activation(hidden[m % 2][:, :], p_in[m % 2][:, :], ACT.Gelu if m < FT else ACT.Relu,
                                       bias=b_in[:, m:m + 1]).then_inc(hidden_ready, 1)

            @block.vector
            def _(dve):
                c = Chain(dve, chain_s)
                with dve.Fori(0, NB) as n:
                    c.loop(n, 4 * TPN)
                    at = lambda t: x[:, ds(n * TPN + t, 1), :].rearrange("p a e -> p (a e)")
                    mask = lambda t, e: masks[:, ds(n * TPN + t, 1), e]
                    for e in range(2):
                        for t in range(TPN):
                            if e:
                                c.wait(t + 1)
                            c.mark(dve.scalar_tensor_tensor(at(t), b_out[:, e, :], mask(t, e), at(t), ALU.mult, ALU.add))
                    for e in range(2):
                        dve.wait_ge(out_ready, n * HT + (e + 1) * FT + 2)
                        for t in range(TPN):
                            c.wait((1 + e) * TPN + t + 1)
                            c.mark(dve.scalar_tensor_tensor(at(t), p_out[e][:, t, :], mask(t, e), at(t), ALU.mult, ALU.add))
                        c.wait()
                        dve.sem_inc(out_used, 1)


def start_loads(nc, done, pairs):
    with nc.Block() as block:
        @block.sync
        def _(sp):
            for dst, src in pairs:
                sp.dma_start(dst, src).then_inc(done, 16)
    return len(pairs)


def finish_loads(nc, done, count):
    with nc.Block() as block:
        @block.sync
        def _(sp):
            sp.wait_ge(done, count * 16)


def halves(dram):
    return dram.rearrange("(h p) n -> p h n", p=P)


def two_blocks_program(nc, d, out):
    with ExitStack() as ctx:
        def sb_in(scope):
            return lambda n, s, dt=F32: scope.enter_context(nc.sbuf_tensor(n, s, dt))
        sb, sem = sb_in(ctx), lambda n: ctx.enter_context(nc.semaphore(n))
        x_loaded, start_loaded, moe_loaded, mix_loaded, rec_loaded, ffn_loaded = (
            sem(n) for n in "x_loaded start_loaded moe_loaded mix_loaded rec_loaded ffn_loaded".split())
        x = sb("x", [P, TILES, E])
        ident, ident16 = sb("ident", [P, P]), sb("ident16", [P, P], BF16)
        stats = sb("stats", [P, TILES, 6])
        mean, rstd, eps = sb("mean", [P, TILES]), sb("rstd", [P, TILES]), sb("eps", [P, 1])
        head_ones = sb("head_ones", [P, P])
        vec = sb("vec", [P, EH, len(VECTORS) + 1])
        vec_in = vec[:, :, 0:len(VECTORS)]

        with ExitStack() as block0:
            sb0 = sb_in(block0)
            attn = sb0("attn", [P, UNITS, TPB, GROUP * HD])
            w_proj, b_proj = sb0("w_proj", [P, EH, E]), sb0("b_proj", [P, E])
            w_router, priority = sb0("w_router", [P, EH, EXPERTS]), sb0("priority", [P, EXPERTS])
            with ExitStack() as attention:
                sba = sb_in(attention)
                qparts, kparts = (sba(n, [P, 3, UNITS, TPB, GROUP * HD], BF16) for n in ("qparts", "kparts"))
                v = sba("v", [P, 1, UNITS, TPB, GROUP * HD])
                causal, anticausal = sba("causal", [P, P]), sba("anticausal", [P, P])
                causal16, anticausal16 = sba("causal16", [P, P], BF16), sba("anticausal16", [P, P], BF16)
                abias, shift0 = sba("abias", [P, NQC * TPB]), sba("shift0", [P, TPB])
                key_alibi = sba("key_alibi", [P, TPB, 2])
                with ExitStack() as projection:
                    sbp = sb_in(projection)
                    w_qkv, b_qkv = sbp("w_qkv", [P, EH, 3 * E]), sbp("b_qkv", [P, 3 * E])
                    start_loads(nc, x_loaded, [(x[:, :, :], d["x"].rearrange("(t p) e -> p t e", p=P))])
                    count = start_loads(nc, start_loaded, [
                        (ident[:, :], d["ident"]),
                        (w_qkv[:, :, :], halves(d["w_qkv"])), (b_qkv[:, :], d["b_qkv"]),
                        (causal[:, :], d["causal"]), (anticausal[:, :], d["anticausal"]),
                        (abias[:, :], d["abias"]), (shift0[:, :], d["shift0"]),
                        (key_alibi[:, :, :], d["key_alibi"]),
                        (w_proj[:, :, :], halves(d["w_proj"])), (b_proj[:, :], d["b_proj"]),
                        (w_router[:, :, :], halves(d["w_router"])), (priority[:, :], d["priority"]),
                        (head_ones[:, :], d["head_ones"]), (vec_in, d["vectors"])])
                    with nc.Block() as block:
                        @block.vector
                        def _(dve):
                            dve.memset(eps[:, :], EPS)
                            dve.wait_ge(x_loaded, 16)
                    layernorm_stats(nc, "ln1_", x, stats, mean, rstd, eps, taken=False)
                    with nc.Block() as block:
                        @block.vector
                        def _(dve):
                            dve.wait_ge(start_loaded, count * 16)
                            dve.tensor_copy(ident16[:, :], ident[:, :])
                            dve.tensor_copy(causal16[:, :], causal[:, :])
                            dve.tensor_copy(anticausal16[:, :], anticausal[:, :])
                            dve.tensor_scalar(b_qkv[:, 0:E], b_qkv[:, 0:E], HD ** -0.5, None, ALU.mult)
                    qkv_phase(nc, x, mean, rstd, ident, w_qkv, b_qkv, qparts, kparts, v)
                attention_phase(nc, ident, ident16, causal16, anticausal16, abias, shift0, key_alibi,
                                qparts, kparts, v, attn)
            select32, select = sb0("select32", [3 * SLICES, WIDTH]), sb0("select", [3 * SLICES, WIDTH], BF16)
            w_gate, w_up = sb0("w_gate", [P, EH, WIDTH]), sb0("w_up", [P, EH, WIDTH])
            w_down = sb0("w_down", [P, MT, E])
            whole = WIDTH // P
            count = start_loads(nc, moe_loaded, [
                (select32[:, :], d["select"]), (w_gate[:, :, :], halves(d["w_gate"])),
                (w_up[:, :, :], halves(d["w_up"])),
                (w_down[:, 0:whole, :], d["w_down"][0:whole * P, :].rearrange("(m p) e -> p m e", p=P)),
                (w_down[0:WIDTH - whole * P, whole, :], d["w_down"][whole * P:WIDTH, :])])
            project_attention(nc, attn, x, b_proj, ident, w_proj, stats)
            layernorm_stats(nc, "ln2_", x, stats, mean, rstd, eps)
            xt = sb0("xt_moe", [P, EH, NB, TB + 1])
            gates_t = sb0("gates_t", [3 * SLICES, B * S], BF16)
            normalise_and_turn(nc, "nt2_", x, mean, rstd, ident, xt)
            router_phase(nc, xt, w_router, ident, ident16, priority, gates_t)
            with nc.Block() as block:
                @block.vector
                def _(dve):
                    dve.wait_ge(moe_loaded, count * 16)
                    dve.tensor_copy(select[:, :], select32[:, :])
            moe_phase(nc, x, xt, gates_t, select, w_gate, w_up, w_down, stats)

        w_out = sb("w_out", [P, EH, E])
        data = {n: sb(n, [P, EH, NB, TB]) for n in "rt at bt kt vt gt bonus".split()}
        data["chunk_decay"] = sb("chunk_decay", [P, EH, NB, CPB])
        data["yt"] = data["vt"]
        with ExitStack() as mixing:
            sbm = sb_in(mixing)
            weights = {n: sbm("w_" + n, [P, EH, k]) for n, k in
                       (("w1", 64), ("a1", 64), ("g1", P), ("r", E), ("k", E), ("v", E))}
            weights |= {n: sbm("w_" + n, [k, E]) for n, k in (("w2", 64), ("a2", 64), ("g2", P))}
            carry = sbm("carry", [P, TB])
            head_spread, head_columns = sbm("head_spread", [P, 2 * EH, P]), sbm("head_columns", [P, 32])
            xt = sbm("xt_mix", [P, EH, NB, TB + 1])
            count = start_loads(nc, mix_loaded, [
                (w[:, :, :], halves(d["mix_" + n])) if len(w.shape) == 3 else (w[:, :], d["mix_" + n])
                for n, w in weights.items()] + [(carry[:, :], d["carry"]), (head_spread[:, :, :], d["head_spread"]),
                                           (head_columns[:, :], d["head_columns"]), (w_out[:, :, :], halves(d["w_out"]))])
            layernorm_stats(nc, "ln3_", x, stats, mean, rstd, eps)
            normalise_and_turn(nc, "nt3_", x, mean, rstd, ident, xt)
            finish_loads(nc, mix_loaded, count)
            time_mix_phase(nc, xt, vec, weights, head_spread, head_columns, head_ones, carry, data)
        with ExitStack() as recurrence:
            sbr = sb_in(recurrence)
            chunk_masks, level_masks, level1_t = (
                sbr("chunk_masks", [P, 2 * P]), sbr("level_masks", [P, len(LEVELS), P]), sbr("level1_t", [P, P]))
            count = start_loads(nc, rec_loaded, [(chunk_masks[:, :], d["chunk_masks"]),
                                                 (level_masks[:, :, :], d["level_masks"]), (level1_t[:, :], d["level1_t"])])
            finish_loads(nc, rec_loaded, count)
            recurrence_phase(nc, data, ident, chunk_masks, level_masks, level1_t, head_ones, data["yt"])
        w_switch = sb("w_switch", [P, EH, 2])
        w_in, b_in = sb("w_in", [P, EH, 2 * FFN]), sb("b_in", [P, 2 * FT])
        w_back, b_back = sb("w_back", [P, 2 * FT, E]), sb("b_back", [P, 2, E])
        branch, xt = sb("branch", [P, TILES, 2]), sb("xt_ffn", [P, EH, NB, TB + 1])
        count = start_loads(nc, ffn_loaded, [
            (w_switch[:, :, :], halves(d["w_switch"])), (w_in[:, :, :], halves(d["ffn_in"])), (b_in[:, :], d["ffn_b_in"]),
            (w_back[:, :, :], halves(d["ffn_back"])), (b_back[:, :, :], d["ffn_b_back"])])
        gate_and_project(nc, data, vec, w_out, x, stats)
        layernorm_stats(nc, "ln4_", x, stats, mean, rstd, eps)
        normalise_and_turn(nc, "nt4_", x, mean, rstd, ident, xt)
        finish_loads(nc, ffn_loaded, count)
        switch_phase(nc, xt, w_switch, ident, branch)
        switched_ffn_phase(nc, x, xt, branch, w_in, b_in, w_back, b_back, out)


def shape_constants():
    p = np.arange(P)
    f = np.float32
    key = np.arange(TPB)[None] * P + p[:, None]
    abias = np.stack([SLOPE * (kt * P + p - (c * QC + QC // 2)) for c in range(NQC) for kt in range(TPB)], 1)
    shift0 = [SLOPE * (QC * (t * P // QC) + QC // 2) for t in range(TPB)]
    line = (SLOPE * key).astype(f)
    high = (line.view(np.uint32) & 0xffff0000).view(f)
    row, col = p[:, None], p[None]
    same = row // L == col // L
    joins = [(row // (2 * m) == col // (2 * m)) & (row % (2 * m) >= m) & (col % (2 * m) < m) for m in LEVELS]
    hidden_slice = np.minimum(np.arange(WIDTH) // HIDDEN, EXPERTS)
    select = np.tile(hidden_slice[None] == np.arange(SLICES)[:, None], (3, 1))
    consts = dict(
        ident=np.eye(P), causal=np.where(col <= row, 0, NEG), anticausal=np.where(row <= col, 0, NEG),
        abias=abias, shift0=np.tile(shift0, (P, 1)), key_alibi=np.stack([high, line - high], -1),
        head_ones=row // RN == col // RN, priority=np.tile(EXPERTS - np.arange(EXPERTS), (P, 1)), select=select,
        head_spread=p[:, None, None] == 32 * np.arange(2 * EH)[:, None] + p // RN, head_columns=p[:, None] // RN == np.arange(32)[None],
        carry=np.tile(np.arange(TB) % L != 0, (P, 1)),
        chunk_masks=np.concatenate([same & (row < col), same & (row <= col)], 1),
        level_masks=np.stack(joins, 1), level1_t=joins[0].T)
    return {n: np.ascontiguousarray(a, dtype=f) for n, a in consts.items()}


def kernel(**inputs):
    import concourse.bacc as bacc
    from concourse.bass_utils import run_bass_kernel_spmd

    def on_every_row(a):
        return np.broadcast_to(a, (P,) + a.shape)

    def side_by_side(a):
        return a.transpose(1, 0, 2).reshape(a.shape[1], -1)

    z = {n: np.asarray(a) for n, a in inputs.items()}
    a0, f0 = (lambda n: z["L0_attn_" + n]), (lambda n: z["L0_ffn_" + n])
    a1, f1 = (lambda n: z["L1_attn_" + n]), (lambda n: z["L1_ffn_" + n])
    arrays = shape_constants()
    arrays |= dict(
        x=a0("hidden_states").reshape(B * S, E), w_qkv=a0("W_attn"), b_qkv=on_every_row(a0("b_attn")),
        w_proj=a0("W_proj"), b_proj=on_every_row(a0("b_proj")), w_router=f0("router_w").T,
        w_gate=np.concatenate([side_by_side(f0("wg")), f0("sg")], 1),
        w_up=np.concatenate([side_by_side(f0("wu")), f0("su")], 1),
        w_down=np.concatenate([f0("wd").reshape(-1, E), f0("sd")], 0),
        vectors=np.stack([a1(n).reshape(EH, P).T for n in VECTORS], -1),
        w_out=a1("W_o"), w_switch=f1("Wg").T,
        ffn_in=np.concatenate([f1("W0a").T, f1("W1a").T], 1), ffn_back=np.concatenate([f1("W0b").T, f1("W1b").T], 0),
        ffn_b_in=np.concatenate([f1("b0a"), f1("b1a")]).reshape(2 * FT, P).T,
        ffn_b_back=on_every_row(np.stack([f1("b0b"), f1("b1b")])))
    arrays |= {"mix_" + n: a1(n) for n in ("w1", "a1", "g1", "w2", "a2", "g2")}
    arrays |= {"mix_" + n: a1("W_" + n) for n in "rkv"}

    nc = bacc.Bacc("TRN2", target_bir_lowering=False, num_devices=1)
    feeds, dram = {}, {}
    for name, a in arrays.items():
        a = np.ascontiguousarray(a)
        feeds[f"in_{name}_dram"] = a
        dram[name] = nc.dram_tensor(f"in_{name}_dram", a.shape, mybir.dt.from_np(a.dtype), kind="ExternalInput").ap()
    out = nc.dram_tensor("out_0_dram", (B * S, E), F32, kind="ExternalOutput").ap()
    two_blocks_program(nc, dram, out)
    result = run_bass_kernel_spmd(nc, [feeds], core_ids=[0])
    return result.results[0]["out_0_dram"].reshape(B, S, E)
```
